# Optimizing a Trainium2 kernel written in Bass

```python
import numpy as np
import jax
import jax.numpy as jnp

def _softmax(x, axis=-1):
    return jax.nn.softmax(x, axis=axis)

def _gelu(x):
    return jax.nn.gelu(x, approximate=True)

def _silu(x):
    return jax.nn.silu(x)

def _sigmoid(x):
    return jax.nn.sigmoid(x)

def _layernorm(x, axis=-1, eps=1e-05):
    m = jnp.mean(x, axis=axis, keepdims=True)
    v = jnp.var(x, axis=axis, keepdims=True)
    return (x - m) / jnp.sqrt(v + eps)

def _scatter_add(tgt, idx, src, axis=0):
    return tgt.at[idx].add(src)

def _segment_sum(src, seg, n):
    return jax.ops.segment_sum(src, seg, n)
kernel_name = 'mk_gps_d1_gnn_r8_54295d'

def setup_inputs(seed: int=0):
    np.random.seed(seed)
    _w = jnp.asarray

    def _rec_inputs():
        import jax
        import jax.numpy as jnp
        _gk = jax.random.key(seed)
        x = -8.776e-05 + 1 * jax.random.normal(jax.random.fold_in(_gk, 1), (6250, 256), jnp.float32)
        src = jax.random.randint(jax.random.fold_in(_gk, 2), (100000,), 0, 6250, jnp.int32)
        dst = jax.random.randint(jax.random.fold_in(_gk, 3), (100000,), 0, 6250, jnp.int32)
        _o = jnp.argsort(dst, stable=True)
        src = src[_o]
        dst = dst[_o]
        return (x, src, dst)
    x, src, dst = _rec_inputs()

    def _L0_gnn_setup():
        import math
        import jax, jax.numpy as jnp
        import numpy as np
        N = 2500
        E = 40000
        D_IN = 256
        D_OUT = 256
        H = 8
        DK = D_OUT // H
        key = jax.random.key(seed)
        ks = jax.random.split(key, 16)
        h = jax.random.normal(ks[0], (N, D_IN), dtype=jnp.float32)
        src = jax.random.randint(ks[1], (E,), 0, N, dtype=jnp.int32)
        dst = jax.random.randint(ks[2], (E,), 0, N, dtype=jnp.int32)
        s = 1.0 / math.sqrt(D_IN)
        Wk = jax.random.uniform(ks[3], (D_OUT, D_IN), jnp.float32, -s, s)
        bk = jnp.zeros((D_OUT,), jnp.float32)
        Wq = jax.random.uniform(ks[4], (D_OUT, D_IN), jnp.float32, -s, s)
        bq = jnp.zeros((D_OUT,), jnp.float32)
        Wv = jax.random.uniform(ks[5], (D_OUT, D_IN), jnp.float32, -s, s)
        bv = jnp.zeros((D_OUT,), jnp.float32)
        so = 1.0 / math.sqrt(D_OUT)
        Wa = jax.random.uniform(ks[6], (D_OUT, D_OUT), jnp.float32, -so, so)
        ba = jnp.zeros((D_OUT,), jnp.float32)
        bound = math.sqrt(6.0 / (DK + DK))
        rel_att = jax.random.uniform(ks[7], (H, DK, DK), jnp.float32, -bound, bound)
        rel_msg = jax.random.uniform(ks[8], (H, DK, DK), jnp.float32, -bound, bound)
        rel_pri = jnp.ones((H,), jnp.float32)
        skip = jnp.ones((), jnp.float32)
        return {'h': h, 'src': src, 'dst': dst, 'Wk': Wk, 'bk': bk, 'Wq': Wq, 'bq': bq, 'Wv': Wv, 'bv': bv, 'Wa': Wa, 'ba': ba, 'rel_att': rel_att, 'rel_msg': rel_msg, 'rel_pri': rel_pri, 'skip': skip}
    _L0_gnn_all = _L0_gnn_setup()
    _L0_gnn_in = {k: v for k, v in _L0_gnn_all.items() if k in ('Wk', 'bk', 'Wq', 'bq', 'Wv', 'bv', 'Wa', 'ba', 'rel_att', 'rel_msg', 'rel_pri', 'skip')}
    del _L0_gnn_all

    def _L0_mix_setup():
        import jax, jax.numpy as jnp
        import numpy as np
        HEADS = 8
        DIM_HEAD = 64
        EPS = 1e-05

        def _inst_norm_lastdim(t):
            mu = jnp.mean(t, axis=-1, keepdims=True)
            var = jnp.mean(jnp.square(t - mu), axis=-1, keepdims=True)
            return (t - mu) * jax.lax.rsqrt(var + EPS)
        key = jax.random.key(seed)
        k1, k2, k3, k4 = jax.random.split(key, 4)
        b, n, dim = (4, 1024, 256)
        inner = HEADS * DIM_HEAD
        x = jax.random.normal(k1, (b, n, dim), dtype=jnp.float32)
        Wqkv = jax.random.normal(k2, (3 * inner, dim), dtype=jnp.float32) * (1.0 / np.sqrt(dim))
        Wout = jax.random.normal(k3, (dim, inner), dtype=jnp.float32) * (1.0 / np.sqrt(inner))
        bout = jax.random.normal(k4, (dim,), dtype=jnp.float32) * 0.01
        return {'x': x, 'Wqkv': Wqkv, 'Wout': Wout, 'bout': bout}
    _L0_mix_all = _L0_mix_setup()
    _L0_mix_in = {k: v for k, v in _L0_mix_all.items() if k in ('Wqkv', 'Wout', 'bout')}
    del _L0_mix_all

    def _L0_ffn_setup():
        import jax, jax.numpy as jnp
        import numpy as np
        B, N, D = (16, 512, 256)
        NUM_EXPERTS, TOP_K, HEADS = (4, 2, 4)
        N_EDGES = 131072
        LN_EPS = 1e-05

        def _layernorm(x, g, b):
            mu = x.mean(-1, keepdims=True)
            var = ((x - mu) ** 2).mean(-1, keepdims=True)
            return (x - mu) * jax.lax.rsqrt(var + LN_EPS) * g + b

        def _forward(x, edge_index, W_gat, att_src, att_dst, b_gat, ln_gamma, ln_beta, W1, b1, W2, b2):
            Bc, Nc, Dc = x.shape
            M = Bc * Nc
            x_flat = x.reshape(M, Dc)
            h = (x_flat @ W_gat).reshape(M, HEADS, NUM_EXPERTS)
            loops = jnp.arange(M, dtype=edge_index.dtype)
            src = jnp.concatenate([edge_index[0], loops])
            dst = jnp.concatenate([edge_index[1], loops])
            a_src = (h * att_src).sum(-1)
            a_dst = (h * att_dst).sum(-1)
            e = jax.nn.leaky_relu(a_src[src] + a_dst[dst], negative_slope=0.2)
            e_max = jax.ops.segment_max(e, dst, num_segments=M)
            ee = jnp.exp(e - e_max[dst])
            denom = jax.ops.segment_sum(ee, dst, num_segments=M)
            alpha = ee / (denom[dst] + 1e-16)
            msg = h[src] * alpha[:, :, None]
            agg = jax.ops.segment_sum(msg, dst, num_segments=M).reshape(M, HEADS * NUM_EXPERTS) + b_gat
            scores = _layernorm(agg, ln_gamma, ln_beta).reshape(M, HEADS, NUM_EXPERTS).mean(1)
            scores = scores.reshape(Bc, Nc, NUM_EXPERTS)
            topk_s, topk_i = jax.lax.top_k(scores, TOP_K)
            w = jax.nn.softmax(topk_s, axis=-1)
            out = jnp.zeros_like(x)
            for ei in range(NUM_EXPERTS):
                g = jnp.where(topk_i == ei, w, 0.0).sum(-1)
                hh = jax.nn.gelu(x @ W1[ei] + b1[ei], approximate=False)
                out = out + g[..., None] * (hh @ W2[ei] + b2[ei])
            return out
        key = jax.random.key(seed)
        ks = jax.random.split(key, 8)
        s = 0.05
        return {'x': jax.random.normal(ks[0], (B, N, D), jnp.float32), 'W_gat': jax.random.normal(ks[1], (D, HEADS * NUM_EXPERTS), jnp.float32) * s, 'att_src': jax.random.normal(ks[2], (HEADS, NUM_EXPERTS), jnp.float32) * s, 'att_dst': jax.random.normal(ks[3], (HEADS, NUM_EXPERTS), jnp.float32) * s, 'b_gat': jnp.zeros((HEADS * NUM_EXPERTS,), jnp.float32), 'ln_gamma': jnp.ones((HEADS * NUM_EXPERTS,), jnp.float32), 'ln_beta': jnp.zeros((HEADS * NUM_EXPERTS,), jnp.float32), 'W1': jax.random.normal(ks[4], (NUM_EXPERTS, D, 2 * D), jnp.float32) * s, 'b1': jnp.zeros((NUM_EXPERTS, 2 * D), jnp.float32), 'W2': jax.random.normal(ks[5], (NUM_EXPERTS, 2 * D, D), jnp.float32) * s, 'b2': jnp.zeros((NUM_EXPERTS, D), jnp.float32), 'edge_index': jax.random.randint(ks[6], (2, N_EDGES), 0, B * N, jnp.int32)}
    _L0_ffn_all = _L0_ffn_setup()
    _L0_ffn_in = {k: v for k, v in _L0_ffn_all.items() if k in ('W_gat', 'att_src', 'att_dst', 'b_gat', 'ln_gamma', 'ln_beta', 'W1', 'b1', 'W2', 'b2', 'edge_index')}
    del _L0_ffn_all
    return {'x': x, 'src': src, 'dst': dst, 'L0_gnn_Wk': _L0_gnn_in['Wk'], 'L0_gnn_bk': _L0_gnn_in['bk'], 'L0_gnn_Wq': _L0_gnn_in['Wq'], 'L0_gnn_bq': _L0_gnn_in['bq'], 'L0_gnn_Wv': _L0_gnn_in['Wv'], 'L0_gnn_bv': _L0_gnn_in['bv'], 'L0_gnn_Wa': _L0_gnn_in['Wa'], 'L0_gnn_ba': _L0_gnn_in['ba'], 'L0_gnn_rel_att': _L0_gnn_in['rel_att'], 'L0_gnn_rel_msg': _L0_gnn_in['rel_msg'], 'L0_gnn_rel_pri': _L0_gnn_in['rel_pri'], 'L0_gnn_skip': _L0_gnn_in['skip'], 'L0_mix_Wqkv': _L0_mix_in['Wqkv'], 'L0_mix_Wout': _L0_mix_in['Wout'], 'L0_mix_bout': _L0_mix_in['bout'], 'L0_ffn_W_gat': _L0_ffn_in['W_gat'], 'L0_ffn_att_src': _L0_ffn_in['att_src'], 'L0_ffn_att_dst': _L0_ffn_in['att_dst'], 'L0_ffn_b_gat': _L0_ffn_in['b_gat'], 'L0_ffn_ln_gamma': _L0_ffn_in['ln_gamma'], 'L0_ffn_ln_beta': _L0_ffn_in['ln_beta'], 'L0_ffn_W1': _L0_ffn_in['W1'], 'L0_ffn_b1': _L0_ffn_in['b1'], 'L0_ffn_W2': _L0_ffn_in['W2'], 'L0_ffn_b2': _L0_ffn_in['b2'], 'L0_ffn_edge_index': _L0_ffn_in['edge_index']}

def reference(x, src, dst, L0_gnn_Wk, L0_gnn_bk, L0_gnn_Wq, L0_gnn_bq, L0_gnn_Wv, L0_gnn_bv, L0_gnn_Wa, L0_gnn_ba, L0_gnn_rel_att, L0_gnn_rel_msg, L0_gnn_rel_pri, L0_gnn_skip, L0_mix_Wqkv, L0_mix_Wout, L0_mix_bout, L0_ffn_W_gat, L0_ffn_att_src, L0_ffn_att_dst, L0_ffn_b_gat, L0_ffn_ln_gamma, L0_ffn_ln_beta, L0_ffn_W1, L0_ffn_b1, L0_ffn_W2, L0_ffn_b2, L0_ffn_edge_index):
    import jax
    import jax.numpy as jnp

    def _L0_gnn_ref(h, src, dst, Wk, bk, Wq, bq, Wv, bv, Wa, ba, rel_att, rel_msg, rel_pri, skip):
        import math
        import jax, jax.numpy as jnp
        import numpy as np
        N = 2500
        E = 40000
        D_IN = 256
        D_OUT = 256
        H = 8
        DK = D_OUT // H
        n = h.shape[0]
        sqrt_dk = math.sqrt(DK)
        k = (h @ Wk.T + bk).reshape(n, H, DK)
        q = (h @ Wq.T + bq).reshape(n, H, DK)
        v = (h @ Wv.T + bv).reshape(n, H, DK)
        k = jnp.einsum('nhd,hde->nhe', k, rel_att)
        v = jnp.einsum('nhd,hde->nhe', v, rel_msg)
        score = jnp.einsum('ehd,ehd->eh', q[dst], k[src]) * rel_pri / sqrt_dk
        m = jax.ops.segment_max(score, dst, num_segments=n)
        ex = jnp.exp(score - m[dst])
        z = jax.ops.segment_sum(ex, dst, num_segments=n)
        attn = ex / z[dst]
        agg = jax.ops.segment_sum(v[src] * attn[:, :, None], dst, num_segments=n)
        t = agg.reshape(n, D_OUT)
        trans = t @ Wa.T + ba
        alpha = jax.nn.sigmoid(skip)
        return trans * alpha + h * (1.0 - alpha)

    def _L0_mix_ref(x, Wqkv, Wout, bout):
        import jax, jax.numpy as jnp
        import numpy as np
        HEADS = 8
        DIM_HEAD = 64
        EPS = 1e-05

        def _inst_norm_lastdim(t):
            mu = jnp.mean(t, axis=-1, keepdims=True)
            var = jnp.mean(jnp.square(t - mu), axis=-1, keepdims=True)
            return (t - mu) * jax.lax.rsqrt(var + EPS)
        b, n, dim = x.shape
        qkv = jnp.einsum('bnc,fc->bnf', x, Wqkv)
        q, k, v = jnp.split(qkv, 3, axis=-1)

        def to_heads(t):
            return t.reshape(b, n, HEADS, DIM_HEAD).transpose(0, 2, 1, 3)
        q, k, v = (to_heads(q), to_heads(k), to_heads(v))
        k = _inst_norm_lastdim(k)
        v = _inst_norm_lastdim(v)
        dots = jnp.einsum('bhnd,bhne->bhde', k, v)
        out = jnp.einsum('bhnd,bhde->bhne', q, dots) / n
        out = out.transpose(0, 2, 1, 3).reshape(b, n, HEADS * DIM_HEAD)
        return jnp.einsum('bnf,cf->bnc', out, Wout) + bout

    def _L0_ffn_ref(x, W_gat, att_src, att_dst, b_gat, ln_gamma, ln_beta, W1, b1, W2, b2, edge_index):
        import jax, jax.numpy as jnp
        import numpy as np
        B, N, D = (16, 512, 256)
        NUM_EXPERTS, TOP_K, HEADS = (4, 2, 4)
        N_EDGES = 131072
        LN_EPS = 1e-05

        def _layernorm(x, g, b):
            mu = x.mean(-1, keepdims=True)
            var = ((x - mu) ** 2).mean(-1, keepdims=True)
            return (x - mu) * jax.lax.rsqrt(var + LN_EPS) * g + b

        def _forward(x, edge_index, W_gat, att_src, att_dst, b_gat, ln_gamma, ln_beta, W1, b1, W2, b2):
            Bc, Nc, Dc = x.shape
            M = Bc * Nc
            x_flat = x.reshape(M, Dc)
            h = (x_flat @ W_gat).reshape(M, HEADS, NUM_EXPERTS)
            loops = jnp.arange(M, dtype=edge_index.dtype)
            src = jnp.concatenate([edge_index[0], loops])
            dst = jnp.concatenate([edge_index[1], loops])
            a_src = (h * att_src).sum(-1)
            a_dst = (h * att_dst).sum(-1)
            e = jax.nn.leaky_relu(a_src[src] + a_dst[dst], negative_slope=0.2)
            e_max = jax.ops.segment_max(e, dst, num_segments=M)
            ee = jnp.exp(e - e_max[dst])
            denom = jax.ops.segment_sum(ee, dst, num_segments=M)
            alpha = ee / (denom[dst] + 1e-16)
            msg = h[src] * alpha[:, :, None]
            agg = jax.ops.segment_sum(msg, dst, num_segments=M).reshape(M, HEADS * NUM_EXPERTS) + b_gat
            scores = _layernorm(agg, ln_gamma, ln_beta).reshape(M, HEADS, NUM_EXPERTS).mean(1)
            scores = scores.reshape(Bc, Nc, NUM_EXPERTS)
            topk_s, topk_i = jax.lax.top_k(scores, TOP_K)
            w = jax.nn.softmax(topk_s, axis=-1)
            out = jnp.zeros_like(x)
            for ei in range(NUM_EXPERTS):
                g = jnp.where(topk_i == ei, w, 0.0).sum(-1)
                hh = jax.nn.gelu(x @ W1[ei] + b1[ei], approximate=False)
                out = out + g[..., None] * (hh @ W2[ei] + b2[ei])
            return out
        return _forward(x, edge_index, W_gat, att_src, att_dst, b_gat, ln_gamma, ln_beta, W1, b1, W2, b2)
    xn = _layernorm(x, axis=-1)
    x = x + _L0_gnn_ref(xn, src, dst, L0_gnn_Wk, L0_gnn_bk, L0_gnn_Wq, L0_gnn_bq, L0_gnn_Wv, L0_gnn_bv, L0_gnn_Wa, L0_gnn_ba, L0_gnn_rel_att, L0_gnn_rel_msg, L0_gnn_rel_pri, L0_gnn_skip) + _L0_mix_ref(xn[None], L0_mix_Wqkv, L0_mix_Wout, L0_mix_bout)[0]
    x = x + _L0_ffn_ref(_layernorm(x, axis=-1)[None], L0_ffn_W_gat, L0_ffn_att_src, L0_ffn_att_dst, L0_ffn_b_gat, L0_ffn_ln_gamma, L0_ffn_ln_beta, L0_ffn_W1, L0_ffn_b1, L0_ffn_W2, L0_ffn_b2, L0_ffn_edge_index)[0]
    return x

_drawn_inputs = setup_inputs


def setup_inputs(seed=0):
    import zlib

    import numpy as np

    out = dict(_drawn_inputs(seed))
    spreads = {'L0_gnn_bk': (0.0, 0.8),
     'L0_gnn_bq': (0.0, 0.8),
     'L0_gnn_bv': (0.0, 0.1),
     'L0_gnn_ba': (0.0, 0.1),
     'L0_gnn_rel_pri': (1.0, 0.6),
     'L0_ffn_b_gat': (0.0, 0.1),
     'L0_ffn_ln_gamma': (1.0, 0.2),
     'L0_ffn_ln_beta': (0.0, 0.1),
     'L0_ffn_b1': (0.0, 0.1),
     'L0_ffn_b2': (0.0, 0.1)}
    factors = {}
    for name, (base, spread) in spreads.items():
        noise = np.random.default_rng([zlib.crc32(name.encode()), seed]).standard_normal(out[name].shape)
        drawn = base * np.exp(spread * noise) if base else spread * noise
        out[name] = jnp.asarray(drawn.astype(out[name].dtype))
    for name, factor in factors.items():
        out[name] = (out[name] * factor).astype(out[name].dtype)
    return out
```

```python
from contextlib import ExitStack

import concourse.bass as bass
from concourse import mybir

ALU = mybir.AluOpType
ACT = mybir.ActivationFunctionType
AX = mybir.AxisListType
F32 = mybir.dt.float32
BF16 = mybir.dt.bfloat16
I32 = mybir.dt.int32
BANK = 512


class Consts:

    def __init__(self, nc, ctx):
        sb = lambda n, s, d: ctx.enter_context(nc.sbuf_tensor(n, s, d))
        self.ident = sb("ident", [P, P], F32)
        self.ident_b = sb("ident_b", [P, P], BF16)
        self.upto = sb("upto", [P, P], F32)
        self.ones = sb("ones", [P, P], F32)
        self.after = sb("after", [P, P], F32)
        self.lane_b = sb("lane_b", [P, P], BF16)
        self.lane_c = sb("lane_c", [P, 1], F32)
        lane_i = sb("lane_i", [P, P], I32)
        lane_ci = sb("lane_ci", [P, 1], I32)
        with ExitStack() as own:
            s_base = nc.alloc_semaphore("consts_base")
            s_made = nc.alloc_semaphore("consts_made")
            block = own.enter_context(nc.Block())

            @block.gpsimd
            def _(pool):
                pool.iota(lane_i[:, :], pattern=[[1, P]], base=0, channel_multiplier=0).then_inc(s_base, 1)
                pool.iota(lane_ci[:, :], pattern=[[0, 1]], base=0, channel_multiplier=1).then_inc(s_base, 1)
                pool.memset(self.ident[:, :], 0.0).then_inc(s_base, 1)
                pool.memset(self.upto[:, :], 1.0).then_inc(s_base, 1)
                pool.memset(self.after[:, :], 1.0).then_inc(s_base, 1)
                pool.wait_ge(s_base, 5)
                pool.affine_select(out=self.ident[:, :], in_=self.ident[:, :], compare_op=ALU.not_equal, fill=1.0,
                                   base=0, pattern=[[-1, P]], channel_multiplier=1).then_inc(s_made, 1)
                pool.affine_select(out=self.upto[:, :], in_=self.upto[:, :], compare_op=ALU.is_ge, fill=0.0,
                                   base=0, pattern=[[1, P]], channel_multiplier=-1).then_inc(s_made, 1)
                pool.affine_select(out=self.after[:, :], in_=self.after[:, :], compare_op=ALU.is_gt, fill=0.0,
                                   base=0, pattern=[[-1, P]], channel_multiplier=1).then_inc(s_made, 1)

            @block.vector
            def _(dve):
                nc.vector.memset(self.ones[:, :], 1.0)
                dve.wait_ge(s_made, 3)
                nc.vector.tensor_copy(self.ident_b[:, :], self.ident[:, :])
                nc.vector.tensor_copy(self.lane_b[:, :], lane_i[:, :])
                nc.vector.tensor_copy(self.lane_c[:, :], lane_ci[:, :])


P = 128
GRP = 8
HIS = 64
HOLE = P * HIS - 1


class Steps:

    def __init__(self, eng, sem):
        self.eng, self.sem, self.n, self.base = eng, sem, 0, 0

    def link(self, ins):
        ins.then_inc(self.sem, 1)
        self.n += 1
        self.eng.wait_ge(self.sem, self.base + self.n)

    def loop(self, i, start, per):
        self.base, self.n, self.kept = (i - start) * per + self.n, 0, self.n
        self.per = per

    def loop_end(self, passes):
        assert self.n == self.per, (self.n, self.per)
        self.base, self.n = 0, self.kept + passes * self.per


def spans(total, size):
    return [(a, min(size, total - a)) for a in range(0, total, size)]


def sort_edges(nc, name, consts, src, dst, batches, nodes, pairs_out, dst_rows, counts, ends, often_sorted=False):
    edges = dst.shape[0]
    tiles = spans(batches, P)
    groups = batches // GRP
    assert groups % 2 == 0
    with ExitStack() as ctx:
        sb = lambda n, s, d: ctx.enter_context(nc.sbuf_tensor(f"{name}_{n}", s, d))
        ps = lambda n, s, d: ctx.enter_context(nc.psum_tensor(f"{name}_{n}", s, d))
        sem = lambda n: nc.alloc_semaphore(f"{name}_{n}")
        nt = len(tiles)
        raw = sb("raw", [P, 2, nt, P], I32)
        rawf = sb("rawf", [P, 2, nt, P], F32)
        pairs = sb("pairs", [P, batches, 2], I32)
        dst_c = sb("dst_c", [P, batches], F32)
        part_i = sb("part_i", [P, 2, batches], I32)
        lo_c = sb("lo_c", [P, batches], BF16)
        hi_c = sb("hi_c", [P, batches], BF16)
        one_lo = sb("one_lo", [P, 2, GRP, P], BF16)
        one_hi = sb("one_hi", [P, 2, GRP, HIS], BF16)
        lo_t = sb("lo_t", [P, GRP * P], F32)
        rows = sb("rows", [P, 2, GRP * P], F32)
        scrap = sb("scrap", [P, GRP, P], F32)
        rank = sb("rank", [P, 2, GRP], F32)
        table = sb("table", [P, 2, (GRP + 1) * HIS], F32)
        looked = sb("looked", [P, GRP, HIS], F32)
        found = sb("found", [P, GRP], F32)
        slot = sb("slot", [P, 2, GRP], I32)
        total = sb("total", [P, HIS], F32)
        zero = sb("zero", [P, HIS], F32)
        pair_ring = sb("pair_ring", [P, 2, GRP, 2], I32)
        ps_rows = [ps(f"ps_rows{b}", [P, BANK], F32) for b in range(2)]
        ps_cnt = [ps(f"ps_cnt{b}", [P, BANK], F32)[:, 0:HIS] for b in range(2)]
        ps_t = ps("ps_t", [P, GRP * P], BF16)
        ps_pre = ps("ps_pre", [P, GRP * HIS], F32)
        ps_look = ps("ps_look", [P, GRP * HIS], F32)
        ps_off = ps("ps_off", [P, BANK], F32)

        s_pad, s_in, s_float, s_rows = sem("padded"), sem("lists_in"), sem("as_float"), sem("rows_out")
        s_turned, s_taken = sem("turned"), sem("taken")
        s_own = sem("vector_steps")
        s_onehot, s_counted = sem("onehot"), sem("counted")
        s_tot, s_off = sem("totals"), sem("offsets")
        s_row = [sem(f"row_in{b}") for b in range(2)]
        s_rank, s_trans, s_olt, s_pre, s_tab, s_look, s_mul = (sem("ranked"), sem("onehot_turned"),
            sem("onehot_t"), sem("prefix"), sem("table"), sem("looked_up"), sem("look_read"))
        s_slot, s_ring = sem("slots"), sem("pairs_in_ring")
        s_scat = [sem(f"scattered{b}") for b in range(2)]
        s_pad_flat = sem("flat_padded")
        s_flat, s_cmp, s_bad, s_flag, s_copy, s_same = (sem("flat_in"), sem("compared"), sem("disorder"), sem("flag"),
                                                        sem("pair_rows"), sem("copied"))
        n_turns = 2 * nt
        if often_sorted:
            lines = max(k for k in range(1, P + 1) if edges % k == 0)
            per = edges // lines
            flat = sb("flat", [lines, per + 1], I32)
            less = sb("less", [lines, per], F32)
            falls = sb("falls", [lines, 1], F32)
            unsorted = sb("unsorted", [P, 1], I32)
            pair_rows = sb("pair_rows", [P, nt, P, 2], I32)

        def either(eng, place, copy=None):
            if not often_sorted:
                place()
                return
            eng.wait_ge(s_flag, 1)
            flag = eng.value_load(unsorted[0:1, 0:1])
            with eng.If(flag):
                place()
            if copy is not None:
                with eng.Else():
                    copy()

        full, rest = edges // P, edges % P
        nfull = full // P
        loads = []
        for a, arr in enumerate((src, dst)):
            if nfull:
                loads.append((raw[:, a, 0:nfull, :], arr[0:nfull * P * P].rearrange("(i p e) -> p i e", p=P, e=P)))
            if full > nfull * P:
                k = full - nfull * P
                loads.append((raw[0:k, a, nfull, :], arr[nfull * P * P:full * P].rearrange("(p e) -> p e", e=P)))
            if rest:
                loads.append((raw[full - nfull * P:full - nfull * P + 1, a, nfull, 0:rest],
                              arr[full * P:edges].rearrange("(p e) -> p e", p=1)))
        block = ctx.enter_context(nc.Block())

        @block.sync
        def _(sp):
            if nfull < nt:
                sp.wait_ge(s_pad, 1)
            for on_chip, in_dram in loads:
                sp.dma_start(on_chip, in_dram).then_inc(s_in, 16)
            if often_sorted:
                sp.wait_ge(s_pad_flat, 1)
                sp.dma_start(flat[:, 0:per], dst.rearrange("(q e) -> q e", e=per)).then_inc(s_flat, 16)
                sp.dma_start(flat[0:lines - 1, per:per + 1], dst.rearrange("(q e) -> q e", e=per)[1:lines, 0:1],
                             allow_slow_non_contiguous=True).then_inc(s_flat, 16)
            sp.wait_ge(s_float, 1)
            for i, (t0, k) in enumerate(tiles):
                sp.dma_start(dst_rows[t0:t0 + k, :], rawf[0:k, 1, i, :]).then_inc(s_rows, 16)
            sp.wait_ge(s_rows, 16 * nt)

            def rows_in(i, b, first):
                if not first:
                    sp.wait_ge(s_rank, 2 * i + b - 1)
                sp.dma_start(rows[:, b, :], dst_rows[bass.ds((2 * i + b) * GRP, GRP), :]
                             .rearrange("(o t) e -> o (t e)", o=1).broadcast_to([P, GRP * P])).then_inc(s_row[b], 16)

            def place():
                for b in range(2):
                    rows_in(0, b, True)
                with sp.Fori(1, groups // 2) as i:
                    for b in range(2):
                        rows_in(i, b, False)

            def copy():
                sp.wait_ge(s_copy, 1)
                for i, (t0, k) in enumerate(tiles):
                    sp.dma_start(pairs_out[t0 * P:(t0 + k) * P, :].rearrange("(p e) c -> p e c", e=P), pair_rows[0:k, i, :, :])\
                        .then_inc(s_same, 16)
                sp.wait_ge(s_same, 16 * nt)

            either(sp, place, copy)

        @block.tensor
        def _(pe):
            pe.wait_ge(s_float, 1)
            n = 0
            for a in range(2):
                for i, (t0, k) in enumerate(tiles):
                    if n >= 2:
                        pe.wait_ge(s_taken, n - 1)
                    pe.transpose(ps_rows[n % 2][:, 0:k], rawf[0:k, a, i, :], consts.ident[0:k, 0:k]).then_inc(s_turned, 1)
                    n += 1

            def count(i, b, first):
                g = 2 * i + b
                pe.wait_ge(s_onehot, g + 1)
                if not first:
                    pe.wait_ge(s_tot, g - 1)
                for j in range(GRP):
                    mm = pe.matmul(ps_cnt[b], one_lo[:, b, j, :], one_hi[:, b, j, :], start=(j == 0), stop=(j == GRP - 1))
                mm.then_inc(s_counted, 1)

            for b in range(2):
                count(0, b, True)
            with pe.Fori(1, groups // 2) as i:
                for b in range(2):
                    count(i, b, False)
            pe.wait_ge(s_tot, groups)
            pe.matmul(ps_off[:, 0:HIS], consts.upto[:, :], total[:, :], start=True, stop=True)
            pe.matmul(ps_off[:, HIS:2 * HIS], consts.ones[:, :], total[:, :], start=True, stop=True).then_inc(s_off, 1)
            if often_sorted:
                pe.wait_ge(s_cmp, 1)
                pe.matmul(ps_pre[:, 0:1], consts.ones[0:lines, :], falls[:, :], start=True, stop=True).then_inc(s_bad, 1)

            def place(i, b, first):
                g = 2 * i + b
                pe.wait_ge(s_onehot, groups + g + 1)
                if not (first and b == 0):
                    pe.wait_ge(s_tab, g)
                for j in range(GRP):
                    pe.transpose(ps_t[:, j * P:(j + 1) * P], one_lo[:, b, j, :], consts.ident_b[:, :])
                for j in range(GRP):
                    pe_ = pe.matmul(ps_pre[:, j * HIS:], one_lo[:, b, j, :],
                                    one_hi[:, b, j:j + 1, :].broadcast_to([P, GRP - j, HIS]),
                                    start=(j == 0), stop=(j == GRP - 1), skip_group_check=True)
                pe_.then_inc(s_pre, 1)
                pe.wait_ge(s_olt, g + 1)
                pe.wait_ge(s_tab, g + 1)
                if not (first and b == 0):
                    pe.wait_ge(s_mul, g)
                for j in range(GRP):
                    mm = pe.matmul(ps_look[:, j * HIS:(j + 1) * HIS], lo_t[:, j * P:(j + 1) * P],
                                   table[:, b, j * HIS:(j + 1) * HIS], start=True, stop=True)
                mm.then_inc(s_look, 1)

            def all_places():
                for b in range(2):
                    place(0, b, True)
                with pe.Fori(1, groups // 2) as i:
                    for b in range(2):
                        place(i, b, False)

            either(pe, all_places)

        @block.scalar
        def _(act):
            def turn(i, b, first):
                act.wait_ge(s_pre, 2 * i + b + 1)
                nc.scalar.copy(lo_t[:, :], ps_t[:, :]).then_inc(s_olt, 1)

            def all_turns():
                for b in range(2):
                    turn(0, b, True)
                with act.Fori(1, groups // 2) as i:
                    for b in range(2):
                        turn(i, b, False)

            either(act, all_turns)

        @block.vector
        def _(dve):
            own = Steps(dve, s_own)
            if nfull < nt:
                own.link(nc.vector.memset(raw[:, 0, nt - 1, :], 0))
                nc.vector.memset(raw[:, 1, nt - 1, :], HOLE).then_inc(s_pad, 1)
            if often_sorted:
                nc.vector.memset(flat[:, per:per + 1], HOLE).then_inc(s_pad_flat, 1)
            nc.vector.memset(total[:, :], 0.0)
            own.link(nc.vector.memset(zero[:, :], 0.0))
            dve.wait_ge(s_in, 16 * len(loads))
            k_last = tiles[-1][1]
            if k_last < P and nt > 1:
                nc.vector.tensor_copy(rawf[:, :, 0:nt - 1, :], raw[:, :, 0:nt - 1, :])
                nc.vector.tensor_copy(rawf[0:k_last, :, nt - 1, :], raw[0:k_last, :, nt - 1, :]).then_inc(s_float, 1)
            else:
                nc.vector.tensor_copy(rawf[:, :, :, :], raw[:, :, :, :]).then_inc(s_float, 1)
            if often_sorted:
                dve.wait_ge(s_float, 1)
                for i, (t0, k) in enumerate(tiles):
                    nc.vector.tensor_copy(pair_rows[0:k, i, :, 1], raw[0:k, 1, i, :])
                    last = nc.vector.tensor_scalar(pair_rows[0:k, i, :, 0], rawf[0:k, 0, i, :], float(nodes - 1), None, ALU.min)
                last.then_inc(s_copy, 1)
                dve.wait_ge(s_flat, 32)
                own.link(nc.vector.tensor_tensor(less[:, :], flat[:, 1:per + 1], flat[:, 0:per], ALU.is_lt))
                nc.vector.tensor_reduce(falls[:, :], less[:, :], AX.X, ALU.add).then_inc(s_cmp, 1)
            n = 0
            for a in range(2):
                for i, (t0, k) in enumerate(tiles):
                    dve.wait_ge(s_turned, n + 1)
                    if a == 0:
                        nc.vector.tensor_scalar(pairs[:, t0:t0 + k, 0], ps_rows[n % 2][:, 0:k], float(nodes - 1), None,
                                                ALU.min).then_inc(s_taken, 1)
                    else:
                        nc.vector.tensor_copy(dst_c[:, t0:t0 + k], ps_rows[n % 2][:, 0:k])
                        nc.vector.tensor_copy(pairs[:, t0:t0 + k, 1], ps_rows[n % 2][:, 0:k]).then_inc(s_taken, 1)
                    n += 1
            dve.wait_ge(s_taken, n_turns)
            nc.vector.tensor_scalar(part_i[:, 0, :], pairs[:, :, 1], P - 1, None, ALU.bitwise_and)
            own.link(nc.vector.tensor_scalar(part_i[:, 1, :], pairs[:, :, 1], 7, None, ALU.logical_shift_right))
            nc.vector.tensor_copy(lo_c[:, :], part_i[:, 0, :])
            own.link(nc.vector.tensor_copy(hi_c[:, :], part_i[:, 1, :]))

            def onehots(g, b):
                t0 = g * GRP
                nc.vector.tensor_tensor(one_lo[:, b, :, :], consts.lane_b[:, 0:P].unsqueeze(1).broadcast_to([P, GRP, P]),
                                        lo_c[:, bass.ds(t0, GRP)].unsqueeze(2).broadcast_to([P, GRP, P]), ALU.is_equal)
                nc.vector.tensor_tensor(one_hi[:, b, :, :], consts.lane_b[:, 0:HIS].unsqueeze(1).broadcast_to([P, GRP, HIS]),
                                        hi_c[:, bass.ds(t0, GRP)].unsqueeze(2).broadcast_to([P, GRP, HIS]), ALU.is_equal)\
                    .then_inc(s_onehot, 1)

            def add_up(g, b):
                dve.wait_ge(s_counted, g + 1)
                if not (isinstance(g, int) and g == 0):
                    dve.wait_ge(s_tot, g)
                nc.vector.tensor_tensor(total[:, :], total[:, :], ps_cnt[b], ALU.add).then_inc(s_tot, 1)

            onehots(0, 0)
            onehots(1, 1)
            with dve.Fori(1, groups // 2) as i:
                for b in range(2):
                    add_up(2 * i + b - 2, b)
                    onehots(2 * i + b, b)
            for b in range(2):
                add_up(groups - 2 + b, b)
            dve.wait_ge(s_tot, groups)
            nc.vector.tensor_copy(counts[:, :], total[:, :])
            dve.wait_ge(s_off, 1)
            own.link(nc.vector.tensor_copy(looked[:, 0, :], ps_off[:, HIS:2 * HIS]))
            own.link(nc.vector.tensor_tensor_scan(looked[:, 1, :], looked[:, 0, :], zero[:, :], 0.0, ALU.add, ALU.add))
            own.link(nc.vector.tensor_tensor(looked[:, 2, :], looked[:, 1, :], looked[:, 0, :], ALU.subtract))
            own.link(nc.vector.tensor_tensor(ends[:, :], ps_off[:, 0:HIS], looked[:, 2, :], ALU.add))
            own.link(nc.vector.tensor_tensor(table[:, 0, 0:HIS], ends[:, :], counts[:, :], ALU.subtract))

            def place(i, b, first):
                g = 2 * i + b
                if not first:
                    dve.wait_ge(s_look, g - 1)
                onehots(g, b)
                dve.wait_ge(s_row[b], 16 * i + 16)
                for j in range(GRP):
                    rk = nc.vector.scalar_tensor_tensor(scrap[:, j, :], rows[:, b, j * P:(j + 1) * P],
                                                        dst_c[:, bass.ds(g * GRP + j, 1)], consts.after[:, :],
                                                        ALU.is_equal, ALU.mult, accum_out=rank[:, b, j:j + 1])
                rk.then_inc(s_rank, 1)
                dve.wait_ge(s_pre, g + 1)
                own.link(nc.vector.tensor_tensor(table[:, b, HIS:], ps_pre[:, :].rearrange("p (j h) -> p j h", h=HIS),
                                                 table[:, b, 0:HIS].unsqueeze(1).broadcast_to([P, GRP, HIS]), ALU.add))
                nc.vector.tensor_copy(table[:, 1 - b, 0:HIS], table[:, b, GRP * HIS:]).then_inc(s_tab, 1)
                dve.wait_ge(s_tab, g + 1)
                dve.wait_ge(s_look, g + 1)
                nc.vector.tensor_tensor(looked[:, :, :], ps_look[:, :].rearrange("p (j h) -> p j h", h=HIS),
                                        one_hi[:, b, :, :], ALU.mult).then_inc(s_mul, 1)
                dve.wait_ge(s_mul, g + 1)
                own.link(nc.vector.tensor_reduce(found[:, :], looked[:, :, :], AX.X, ALU.add))
                if not first:
                    dve.wait_ge(s_scat[b], 16 * GRP * i)
                nc.vector.tensor_tensor(slot[:, b, :], found[:, :], rank[:, b, :], ALU.add).then_inc(s_slot, 1)

            def all_places():
                for b in range(2):
                    place(0, b, True)
                with dve.Fori(1, groups // 2) as i:
                    own.loop(i, 1, 4)
                    for b in range(2):
                        place(i, b, False)
                    own.loop_end(groups // 2 - 1)

            if often_sorted:
                dve.wait_ge(s_bad, 1)
                nc.vector.tensor_copy(unsorted[:, :], ps_pre[:, 0:1]).then_inc(s_flag, 1)
            either(dve, all_places)

        @block.gpsimd
        def _(pool):
            def scatter(i, b, first):
                g = 2 * i + b
                if not first:
                    pool.wait_ge(s_scat[b], 16 * GRP * i)
                pool.wait_ge(s_slot, g + 1)
                pool.tensor_copy(pair_ring[:, b, :, :], pairs[:, bass.ds(g * GRP, GRP), :]).then_inc(s_ring, 1)
                pool.wait_ge(s_ring, g + 1)
                pool.nop(nofuse=True)
                for j in range(GRP):
                    pool.indirect_dma_start(pairs_out[:, :], bass.IndirectOffsetOnAxis(ap=slot[:, b, j:j + 1], axis=0),
                                            pair_ring[:, b, j, :], None).then_inc(s_scat[b], 16)

            def all_scatters():
                for b in range(2):
                    scatter(0, b, True)
                with pool.Fori(1, groups // 2) as i:
                    for b in range(2):
                        scatter(i, b, False)
                for b in range(2):
                    pool.wait_ge(s_scat[b], 16 * GRP * (groups // 2))

            either(pool, all_scatters)
FAR = 1.0e30


def group_loop(eng, count, body, steps=None, per=0):
    for b in range(2):
        body(0, b, True)
    with eng.Fori(1, count // 2) as i:
        if steps:
            steps.loop(i, 1, per)
        for b in range(2):
            body(i, b, False)
        if steps:
            steps.loop_end(count // 2 - 1)
    if count % 2:
        body(count // 2, 0, False)


class EdgeLists:

    def __init__(self, nc, ctx, name, batches, heads, last):
        self.batches, self.heads = batches, heads
        self.src_c = ctx.enter_context(nc.sbuf_tensor(f"{name}_src_c", [P, batches], I32))
        self.dst_c = ctx.enter_context(nc.sbuf_tensor(f"{name}_dst_c", [P, batches], F32))
        self.node_c = ctx.enter_context(nc.sbuf_tensor(f"{name}_node_c", [P, batches], I32))
        self.last = last
        self.rows = nc.dram_tensor(f"{name}_sorted_rows", [batches, P], F32, kind="Internal").ap()
        self.cuts = nc.dram_tensor(f"{name}_cuts", [batches, heads, 2 * P], F32, kind="Internal").ap()


def read_sorted(nc, name, consts, lists, pairs, nodes):
    batches, heads = lists.batches, lists.heads
    tiles = spans(batches, P)
    nt = len(tiles)
    with ExitStack() as ctx:
        sb = lambda n, s, d: ctx.enter_context(nc.sbuf_tensor(f"{name}_{n}", s, d))
        sem = lambda n: nc.alloc_semaphore(f"{name}_{n}")
        raw = sb("sorted", [P, nt, P, 2], I32)
        val = sb("sorted_f", [P, 2, nt, P], F32)
        cut = sb("cut", [P, nt, 2, P], F32)
        bank = [ctx.enter_context(nc.psum_tensor(f"{name}_turn{b}", [P, BANK], F32)) for b in range(2)]
        s_in, s_val, s_cut, s_out = sem("sorted_in"), sem("sorted_float"), sem("cuts"), sem("rows_out")
        s_turned, s_taken, s_own = sem("turned"), sem("taken"), sem("vector_steps")
        block = ctx.enter_context(nc.Block())

        @block.sync
        def _(sp):
            for i, (t0, k) in enumerate(tiles):
                sp.dma_start(raw[0:k, i, :, :], pairs[t0 * P:(t0 + k) * P, :].rearrange("(p e) c -> p e c", e=P)).then_inc(s_in, 16)
            sp.wait_ge(s_val, nt)
            for i, (t0, k) in enumerate(tiles):
                sp.dma_start(lists.rows[t0:t0 + k, :], val[0:k, 1, i, :]).then_inc(s_out, 16)
            sp.wait_ge(s_cut, nt)
            for i, (t0, k) in enumerate(tiles):
                sp.dma_start(lists.cuts[t0:t0 + k, :, :],
                             cut[0:k, i, :, :].rearrange("p a e -> p (a e)").unsqueeze(1).broadcast_to([k, heads, 2 * P]))\
                    .then_inc(s_out, 16)
            sp.wait_ge(s_out, 16 * 2 * nt)

        @block.tensor
        def _(pe):
            pe.wait_ge(s_val, nt)
            n = 0
            for a in range(2):
                for i, (t0, k) in enumerate(tiles):
                    if n >= 2:
                        pe.wait_ge(s_taken, n - 1)
                    pe.transpose(bank[n % 2][:, 0:k], val[0:k, a, i, :], consts.ident[0:k, 0:k]).then_inc(s_turned, 1)
                    n += 1

        @block.vector
        def _(dve):
            own = Steps(dve, s_own)
            nc.vector.memset(lists.last[:, :], -1.0)
            own.link(nc.vector.memset(cut[:, :, :, :], -FAR))
            dve.wait_ge(s_in, 16 * nt)
            for i, (t0, k) in enumerate(tiles):
                nc.vector.tensor_copy(val[0:k, 0, i, :], raw[0:k, i, :, 0])
                nc.vector.tensor_copy(val[0:k, 1, i, :], raw[0:k, i, :, 1]).then_inc(s_val, 1)
            dve.wait_ge(s_val, nt)
            for i, (t0, k) in enumerate(tiles):
                d = val[0:k, 1, i, :]
                nc.vector.tensor_copy(lists.last[0:k, i:i + 1], d[:, P - 1:P])
                nc.vector.tensor_tensor(cut[0:k, i, 0, 1:P], d[:, 1:P], d[:, 0:P - 1], ALU.not_equal)
                own.link(nc.vector.tensor_tensor(cut[0:k, i, 1, 0:P - 1], d[:, 1:P], d[:, 0:P - 1], ALU.not_equal))
                nc.vector.tensor_scalar(cut[0:k, i, 0, 1:P], cut[0:k, i, 0, 1:P], -FAR, None, ALU.mult)
                nc.vector.tensor_scalar(cut[0:k, i, 1, 0:P - 1], cut[0:k, i, 1, 0:P - 1], -FAR, None, ALU.mult).then_inc(s_cut, 1)
            n = 0
            for a in range(2):
                for i, (t0, k) in enumerate(tiles):
                    dve.wait_ge(s_turned, n + 1)
                    if a == 0:
                        nc.vector.tensor_copy(lists.src_c[:, t0:t0 + k], bank[n % 2][:, 0:k]).then_inc(s_taken, 1)
                    else:
                        nc.vector.tensor_scalar(lists.node_c[:, t0:t0 + k], bank[n % 2][:, 0:k], float(nodes - 1), None, ALU.min)
                        nc.vector.tensor_copy(lists.dst_c[:, t0:t0 + k], bank[n % 2][:, 0:k]).then_inc(s_taken, 1)
                    n += 1


def edge_pass(nc, name, consts, lists, src_table, dst_table, width, partial, spread=None):
    batches, heads = lists.batches, lists.heads
    groups = batches // GRP
    s_cols = src_table.shape[1]
    vals = heads * width
    dot = spread is None
    per_batch = 2 if dot else 1
    val0 = s_cols - vals if dot else 0
    sums = heads * (width + 1)
    cols = sums + heads
    gh = GRP * heads
    per_bank = 1 if sums * 2 > BANK else GRP
    n_banks = 2 if per_bank == 1 else 1
    with ExitStack() as ctx:
        sb = lambda n, s, d: ctx.enter_context(nc.sbuf_tensor(f"{name}_{n}", s, d))
        ps = lambda n: ctx.enter_context(nc.psum_tensor(f"{name}_{n}", [P, BANK], F32))
        sem = lambda n: nc.alloc_semaphore(f"{name}_{n}")
        ring = sb("index_ring", [P, 2, 2, GRP], I32)
        s_row = sb("src_rows", [P, 2, GRP, s_cols], F32)
        d_row = sb("dst_rows", [P, 2, GRP, vals], F32) if dot else None
        rows = sb("rows", [P, 2, GRP, P], F32)
        cuts = sb("cuts", [gh, 2, 2, P], F32)
        prod = sb("prod", [P, GRP, vals], F32)
        score = sb("score", [P, 2, gh], F32)
        up = sb("up", [gh, P], F32)
        top = sb("top", [gh, 2, P], F32)
        rel = sb("rel", [gh, P], F32)
        ex = sb("ex", [gh, P], F32)
        same = sb("same", [P, 2, GRP, P], F32)
        msg = sb("msg", [P, 2, GRP, heads, width + 1], F32)
        out = sb("out", [P, 2, GRP, cols], F32)
        p_turn = ps("p_turn")
        p_back = ps("p_back")
        p_max = ps("p_max")
        p_sum = [ps(f"p_sum{k}") for k in range(n_banks)]
        s_ring = sem("ring")
        s_got = [sem(f"gathered{b}") for b in range(2)]
        s_list = [sem(f"rows_in{b}") for b in range(2)]
        s_own = sem("vector_steps")
        s_used, s_score, s_turn, s_top, s_rel, s_ex, s_back, s_msg, s_same = (
            sem("rows_used"), sem("scores"), sem("scores_turned"), sem("maxima"), sem("scores_less_max"),
            sem("exps"), sem("turned_back"), sem("messages"), sem("same_run"))
        s_sum, s_kept, s_max = sem("sums"), sem("sums_kept"), sem("maxima_kept")
        s_out = [sem(f"stored{b}") for b in range(2)]
        half = groups // 2
        sums_per_group = GRP // per_bank
        part_v = partial[0:P * batches, :].rearrange("(p t) c -> p t c", t=batches)

        def p_sum_of(b, j):
            return p_sum[j % 2]

        block = ctx.enter_context(nc.Block())

        @block.gpsimd
        def _(pool):
            def gather(i, b, first):
                g = 2 * i + b
                if not first:
                    pool.wait_ge(s_got[b], 16 * per_batch * GRP * i)
                pool.tensor_copy(ring[:, b, 0, :], lists.src_c[:, bass.ds(g * GRP, GRP)])
                pool.tensor_copy(ring[:, b, 1, :], lists.node_c[:, bass.ds(g * GRP, GRP)]).then_inc(s_ring, 1)
                pool.wait_ge(s_ring, g + 1)
                pool.nop(nofuse=True)
                if not first:
                    pool.wait_ge(s_msg, g - 1)
                    pool.nop(nofuse=True)
                for j in range(GRP):
                    if dot:
                        pool.indirect_dma_start(d_row[:, b, j, :], None, dst_table[:, :],
                                                bass.IndirectOffsetOnAxis(ap=ring[:, b, 1, j:j + 1], axis=0)).then_inc(s_got[b], 16)
                    pool.indirect_dma_start(s_row[:, b, j, :], None, src_table[:, :],
                                            bass.IndirectOffsetOnAxis(ap=ring[:, b, 0, j:j + 1], axis=0)).then_inc(s_got[b], 16)

            group_loop(pool, groups, gather)

        @block.sync
        def _(sp):
            def load(i, b, first):
                g = 2 * i + b
                if not first:
                    sp.wait_ge(s_msg, g - 1)
                sp.dma_start(rows[:, b, :, :].rearrange("p t e -> p (t e)"),
                             lists.rows[bass.ds(g * GRP, GRP), :].rearrange("(o t) e -> o (t e)", o=1)
                             .broadcast_to([P, GRP * P])).then_inc(s_list[b], 16)
                sp.dma_start(cuts[:, b, :, :].rearrange("p a e -> p (a e)"),
                             lists.cuts[bass.ds(g * GRP, GRP), :, :].rearrange("t h e -> (t h) e")).then_inc(s_list[b], 16)

            def store(i, b):
                g = 2 * i + b
                sp.wait_ge(s_kept, (g + 1) * sums_per_group)
                sp.wait_ge(s_max, g + 1)
                sp.dma_start(part_v[:, bass.ds(g * GRP, GRP), :], out[:, b, :, :]).then_inc(s_out[b], 16)

            for b in range(2):
                load(0, b, True)
            with sp.Fori(1, half) as i:
                for b in range(2):
                    store(i - 1, b)
                    load(i, b, False)
            for b in range(2):
                store(half - 1, b)
            for b in range(2):
                sp.wait_ge(s_out[b], 16 * half)

        @block.vector
        def _(dve):
            own = Steps(dve, s_own)

            def group(i, b, first):
                g = 2 * i + b
                dve.wait_ge(s_got[b], 16 * per_batch * GRP * (i + 1))
                if dot:
                    own.link(nc.vector.tensor_tensor(prod[:, :, :], s_row[:, b, :, 0:vals], d_row[:, b, :, :], ALU.mult))
                    nc.vector.tensor_reduce(score[:, b, :], prod[:, :, :].rearrange("p t (h w) -> p (t h) w", w=width),
                                            AX.X, ALU.add).then_inc(s_score, 1)
                else:
                    raw = prod[:, :, 0:heads]
                    own.link(nc.vector.tensor_tensor(raw, s_row[:, b, :, vals:s_cols], spread[:, bass.ds(g * GRP, GRP), :], ALU.add))
                    nc.vector.scalar_tensor_tensor(score[:, b, :].rearrange("p (t h) -> p t h", h=heads), raw, 0.2, raw,
                                                   ALU.mult, ALU.max).then_inc(s_score, 1)
                dve.wait_ge(s_list[b], 32 * (i + 1))
                if not first:
                    dve.wait_ge(s_sum, (g - 1) * sums_per_group)
                nc.vector.tensor_tensor(same[:, b, :, :], rows[:, b, :, :],
                                        lists.dst_c[:, bass.ds(g * GRP, GRP)].unsqueeze(2).broadcast_to([P, GRP, P]),
                                        ALU.is_equal).then_inc(s_same, 1)
                dve.wait_ge(s_turn, g + 1)
                own.link(nc.vector.tensor_tensor_scan(up[:, :], cuts[:, b, 0, :], p_turn[0:gh, 0:P], 0.0, ALU.add, ALU.max))
                own.link(nc.vector.tensor_tensor_scan(top[:, b, ::-1], cuts[:, b, 1, ::-1], up[:, ::-1], 0.0, ALU.add, ALU.max))
                nc.vector.tensor_tensor(rel[:, :], p_turn[0:gh, 0:P], top[:, b, :], ALU.subtract).then_inc(s_rel, 1)
                dve.wait_ge(s_back, g + 1)
                e = p_back[:, 0:gh].rearrange("p (t h) -> p t h", h=heads)
                nc.vector.tensor_copy(msg[:, b, :, :, width], e)
                nc.vector.tensor_tensor(msg[:, b, :, :, 0:width],
                                        s_row[:, b, :, val0:val0 + vals].rearrange("p t (h w) -> p t h w", w=width),
                                        e.unsqueeze(3).broadcast_to([P, GRP, heads, width]), ALU.mult).then_inc(s_msg, 1)

            group_loop(dve, groups, group, own, 6)

        @block.scalar
        def _(act):
            def group(i, b, first):
                g = 2 * i + b
                act.wait_ge(s_rel, g + 1)
                if not (first and b == 0):
                    act.wait_ge(s_back, g)
                nc.scalar.activation(ex[:, :], rel[:, :], ACT.Exp).then_inc(s_ex, 1)
                act.wait_ge(s_back, g + 1)
                if not first:
                    act.wait_ge(s_out[b], 16 * i)
                nc.scalar.copy(out[:, b, :, sums:cols], p_max[:, 0:gh].rearrange("p (t h) -> p t h", h=heads)).then_inc(s_max, 1)
                for j in range(sums_per_group):
                    act.wait_ge(s_sum, g * sums_per_group + j + 1)
                    if per_bank == 1:
                        nc.scalar.copy(out[:, b, j, 0:sums], p_sum_of(b, j)[:, 0:sums]).then_inc(s_kept, 1)
                    else:
                        nc.scalar.copy(out[:, b, :, 0:sums], p_sum[0][:, 0:GRP * sums].rearrange("p (t c) -> p t c", c=sums))\
                            .then_inc(s_kept, 1)

            group_loop(act, groups, group)

        @block.tensor
        def _(pe):
            def group(i, b, first):
                g = 2 * i + b
                pe.wait_ge(s_score, g + 1)
                if not (first and b == 0):
                    pe.wait_ge(s_rel, g)
                pe.nop(nofuse=True)
                pe.transpose(p_turn[0:gh, 0:P], score[:, b, :], consts.ident[:, :]).then_inc(s_turn, 1)
                pe.wait_ge(s_ex, g + 1)
                if not (first and b == 0):
                    pe.wait_ge(s_msg, g)
                    pe.wait_ge(s_max, g)
                pe.nop(nofuse=True)
                pe.transpose(p_back[:, 0:gh], ex[:, :], consts.ident[0:gh, 0:gh])
                pe.transpose(p_max[:, 0:gh], top[:, b, :], consts.ident[0:gh, 0:gh]).then_inc(s_back, 1)
                pe.wait_ge(s_same, g + 1)
                pe.wait_ge(s_msg, g + 1)
                if per_bank == 1:
                    for j in range(GRP):
                        if not (first and b == 0 and j < 2):
                            pe.wait_ge(s_kept, g * GRP + j - 1)
                        pe.matmul(p_sum_of(b, j)[:, 0:sums], same[:, b, j, :],
                                  msg[:, b, j, :, :].rearrange("p h w -> p (h w)"), start=True, stop=True).then_inc(s_sum, 1)
                else:
                    if not (first and b == 0):
                        pe.wait_ge(s_kept, g)
                    for j in range(GRP):
                        mm = pe.matmul(p_sum[0][:, j * sums:(j + 1) * sums], same[:, b, j, :],
                                       msg[:, b, j, :, :].rearrange("p h w -> p (h w)"), start=True, stop=True)
                    mm.then_inc(s_sum, 1)

            group_loop(pe, groups, group)
def spread_over_runs(nc, name, consts, nodes, lists, counts, ends, values, table, spread):
    H = values.shape[2]
    T = lists.batches
    C = P // H
    L = T // C
    tiles = nodes.tiles
    starts = nc.dram_tensor(f"{name}_starts", [P * T + P, H], F32, kind="Internal").ap()
    with ExitStack() as ctx:
        sb = lambda n, s, d=F32: ctx.enter_context(nc.sbuf_tensor(f"{name}_{n}", s, d))
        sem = lambda n: nc.alloc_semaphore(f"{name}_{n}")
        run = sb("run", [P, L * P])
        hold = sb("hold", [P, L * P])
        first_at = sb("first_at", [P, L * P])
        edge = sb("edge", [P, 4, tiles])
        edge_i = sb("edge_i", [P, 3, tiles], I32)
        by_chunk = sb("by_chunk", [P, 2, BANK])
        ring = sb("ring", [P, 2, 1], I32)
        val_ring = sb("val_ring", [P, 2, H])
        head = sb("head", [C, 1])
        head_i = sb("head_i", [C, 1], I32)
        head_v = sb("head_v", [C, H])
        begin = sb("begin", [P, 1])
        bank = [ctx.enter_context(nc.psum_tensor(f"{name}_bank{b}", [P, BANK], F32)) for b in range(2)]
        (s_run, s_head, s_zero, s_cleared, s_idx, s_ring, s_hi, s_hv, s_begin, s_in, s_own, s_perm, s_t, s_k, s_fill, s_t2, s_k2) = (
            sem(n) for n in ("run_in", "head_in", "zero", "cleared", "indices", "ring", "head_index", "head_value", "begin",
                             "starts_in", "steps", "by_chunk", "turned", "taken", "filled", "turned_back", "taken_back"))
        s_sc = [sem(f"scattered{b}") for b in range(2)]
        quads = BANK // P
        passes = L // quads
        block = ctx.enter_context(nc.Block())

        @block.sync
        def _(sp):
            for h in range(H):
                sp.dma_start(run[h * C:(h + 1) * C, :], lists.rows.rearrange("(c l) e -> c (l e)", c=C)).then_inc(s_run, 16)
            sp.dma_start(head[:, :], lists.rows.rearrange("(c l) e -> c (l e)", c=C)[:, 0:1],
                         allow_slow_non_contiguous=True).then_inc(s_head, 16)
            sp.wait_ge(s_zero, 1)
            sp.dma_start(starts[0:P * T, :].rearrange("(p t) h -> p (t h)", p=P), hold[:, :]).then_inc(s_cleared, 16)
            sp.wait_ge(s_hv, 16)
            for h in range(H):
                sp.dma_start(begin[h * C:(h + 1) * C, :], head_v[:, h:h + 1]).then_inc(s_begin, 16)
            for b in range(2):
                sp.wait_ge(s_sc[b], 16 * ((tiles + 1 - b) // 2))
            sp.dma_start(spread[:, :, :], starts[0:P * T, :].rearrange("(p t) h -> p t h", p=P)).then_inc(s_in, 16)

        @block.gpsimd
        def _(pool):
            pool.wait_ge(s_hi, 1)
            pool.indirect_dma_start(head_v[:, :], None, table[:, :], bass.IndirectOffsetOnAxis(ap=head_i[:, :], axis=0)).then_inc(s_hv, 16)
            pool.wait_ge(s_idx, 1)
            pool.wait_ge(s_cleared, 16)

            def scatter(i, b, first):
                n = 2 * i + b
                if not first:
                    pool.wait_ge(s_sc[b], 16 * i)
                pool.tensor_copy(val_ring[:, b, :], values[:, bass.ds(n, 1), :].rearrange("p o h -> p (o h)"))
                pool.tensor_copy(ring[:, b, :], edge_i[:, 0, bass.ds(n, 1)]).then_inc(s_ring, 1)
                pool.wait_ge(s_ring, n + 1)
                pool.nop(nofuse=True)
                pool.indirect_dma_start(starts[:, :], bass.IndirectOffsetOnAxis(ap=ring[:, b, :], axis=0), val_ring[:, b, :], None)\
                    .then_inc(s_sc[b], 16)

            group_loop(pool, tiles, scatter)

        @block.tensor
        def _(pe):
            for q in range(passes):
                pe.wait_ge(s_perm, q + 1)
                if q >= 2:
                    pe.wait_ge(s_k, q - 1)
                for j in range(quads):
                    mm = pe.transpose(bank[q % 2][:, j * P:(j + 1) * P], by_chunk[:, q % 2, j * P:(j + 1) * P], consts.ident[:, :])
                mm.then_inc(s_t, 1)
            pe.wait_ge(s_fill, 1)
            for q in range(passes):
                if q >= 2:
                    pe.wait_ge(s_k2, q - 1)
                for j in range(quads):
                    l = q * quads + j
                    mm = pe.transpose(bank[q % 2][:, j * P:(j + 1) * P], run[:, l * P:(l + 1) * P], consts.ident[:, :])
                mm.then_inc(s_t2, 1)

        @block.vector
        def _(dve):
            own = Steps(dve, s_own)
            V = nc.vector
            V.memset(hold[:, :], 0.0).then_inc(s_zero, 1)
            dve.wait_ge(s_head, 16)
            own.link(V.tensor_scalar(head[:, :], head[:, :], float(nodes.count - 1), None, ALU.min))
            V.tensor_copy(head_i[:, :], head[:, :]).then_inc(s_hi, 1)
            own.link(V.tensor_tensor(edge[:, 0, :], ends[:, 0:tiles], counts[:, 0:tiles], ALU.subtract))
            own.link(V.tensor_copy(edge_i[:, 0, :], edge[:, 0, :]))
            V.tensor_scalar(edge_i[:, 1, :], edge_i[:, 0, :], P - 1, None, ALU.bitwise_and)
            own.link(V.tensor_scalar(edge_i[:, 2, :], edge_i[:, 0, :], 7, None, ALU.logical_shift_right))
            V.tensor_copy(edge[:, 0, :], edge_i[:, 1, :])
            V.tensor_copy(edge[:, 1, :], edge_i[:, 2, :])
            own.link(V.tensor_scalar(edge[:, 2, :], counts[:, 0:tiles], 0.0, None, ALU.is_equal))
            own.link(V.scalar_tensor_tensor(edge[:, 1, :], edge[:, 0, :], float(T), edge[:, 1, :], ALU.mult, ALU.add))
            own.link(V.tensor_scalar(edge[:, 3, :], edge[:, 1, :], -1.0, float(P * T), ALU.mult, ALU.add))
            own.link(V.tensor_scalar(edge[:, 3, :], edge[:, 3, :], consts.lane_c[:, :], None, ALU.add))
            own.link(V.tensor_tensor(edge[:, 3, :], edge[:, 3, :], edge[:, 2, :], ALU.mult))
            V.tensor_tensor(edge_i[:, 0, :], edge[:, 1, :], edge[:, 3, :], ALU.add).then_inc(s_idx, 1)
            dve.wait_ge(s_run, 16 * H)
            dve.wait_ge(s_cleared, 16)
            V.memset(hold[:, 0:1], 1.0)
            own.link(V.tensor_tensor(hold[:, 1:], run[:, 1:], run[:, 0:L * P - 1], ALU.is_equal))
            back = spread[:, :, :].rearrange("p (c l) h -> p l h c", c=C)
            dve.wait_ge(s_in, 16)
            for q in range(passes + 1):
                if q < passes:
                    if q >= 2:
                        dve.wait_ge(s_t, q - 1)
                    V.tensor_copy(by_chunk[:, q % 2, :].rearrange("p (l h c) -> p l h c", l=quads, h=H),
                                  back[:, q * quads:(q + 1) * quads]).then_inc(s_perm, 1)
                if q == 0:
                    continue
                q -= 1
                dve.wait_ge(s_t, q + 1)
                V.tensor_copy(first_at[:, q * BANK:(q + 1) * BANK], bank[q % 2][:, :]).then_inc(s_k, 1)
            dve.wait_ge(s_k, passes)
            own.link(V.memset(first_at[:, 0:1], 0.0))
            dve.wait_ge(s_begin, 16 * H)
            V.tensor_tensor_scan(run[:, :], hold[:, :], first_at[:, :], begin[:, :], ALU.mult, ALU.add).then_inc(s_fill, 1)
            for q in range(passes):
                dve.wait_ge(s_t2, q + 1)
                V.tensor_copy(back[:, q * quads:(q + 1) * quads], bank[q % 2][:, :].rearrange("p (l h c) -> p l h c", l=quads, h=H))\
                    .then_inc(s_k2, 1)


def turn_all(nc, name, ctx, jobs, ident, ready, taken):
    bank = [ctx.enter_context(nc.psum_tensor(f"{name}_turn{b}", [P, BANK], F32)) for b in range(2)]

    def tensor_part(pe, start=0):
        for n, (_, in_) in enumerate(jobs):
            if n >= 2:
                pe.wait_ge(taken, n - 1)
            k = in_.shape[0]
            pe.transpose(bank[n % 2][0:in_.shape[1], 0:k], in_, ident[0:k, 0:k]).then_inc(ready, 1)

    def vector_part(dve):
        for n, (out, in_) in enumerate(jobs):
            dve.wait_ge(ready, n + 1)
            nc.vector.tensor_copy(out, bank[n % 2][0:in_.shape[1], 0:in_.shape[0]]).then_inc(taken, 1)
        dve.wait_ge(taken, len(jobs))

    return tensor_part, vector_part


class Nodes:

    def __init__(self, nc, ctx, nodes, dim):
        self.count, self.dim, self.tiles = nodes, dim, -(-nodes // P)
        sb = lambda n, s: ctx.enter_context(nc.sbuf_tensor(n, s, F32))
        self.x = sb("x", [P, self.tiles, dim])
        self.mean_var = sb("mean_var", [P, self.tiles, 2])
        self.rstd = sb("rstd", [P, self.tiles])
        self.gx = sb("gx", [P, dim // P, dim])
        self.wa_t = sb("wa_t", [P, dim // P, dim])
        self.bias = sb("bias", [P, dim])
        self.eps = sb("eps", [P, 1])


def on_all(row, n):
    return row.rearrange("(o n) -> o n", o=1).broadcast_to([P, n])


def layer_norm_stats(nc, name, nodes, LN_EPS=1e-5):
    with ExitStack() as ctx:
        parts = ctx.enter_context(nc.sbuf_tensor(f"{name}_parts", [P, nodes.tiles, 6], F32))
        root = ctx.enter_context(nc.sbuf_tensor(f"{name}_root", [P, nodes.tiles], F32))
        half = ctx.enter_context(nc.sbuf_tensor(f"{name}_half", [P, nodes.tiles], F32))
        s_parts, s_stats, s_root, s_own = (nc.alloc_semaphore(f"{name}_{n}") for n in ("parts", "stats", "root", "steps"))
        block = ctx.enter_context(nc.Block())

        @block.vector
        def _(dve):
            nc.vector.memset(nodes.eps[:, :], LN_EPS)
            with dve.Fori(0, nodes.tiles) as n:
                nc.vector.bn_stats(parts[:, bass.ds(n, 1), :].rearrange("p o c -> p (o c)"),
                                   nodes.x[:, bass.ds(n, 1), :].rearrange("p o c -> p (o c)")).then_inc(s_parts, 1)
            dve.wait_ge(s_parts, nodes.tiles)
            own = Steps(dve, s_own)
            V = nc.vector
            mean, var = nodes.mean_var[:, :, 0], nodes.mean_var[:, :, 1]
            own.link(V.tensor_tensor(half[:, :], parts[:, :, 1], parts[:, :, 4], ALU.subtract))
            own.link(V.tensor_tensor(var, half[:, :], half[:, :], ALU.mult))
            own.link(V.tensor_tensor(half[:, :], parts[:, :, 2], parts[:, :, 5], ALU.add))
            own.link(V.tensor_scalar(var, var, 0.25, None, ALU.mult))
            own.link(V.tensor_scalar(half[:, :], half[:, :], 1.0 / nodes.dim, None, ALU.mult))
            own.link(V.tensor_tensor(var, var, half[:, :], ALU.add))
            own.link(V.tensor_tensor(mean, parts[:, :, 1], parts[:, :, 4], ALU.add))
            V.tensor_scalar(mean, mean, 0.5, None, ALU.mult).then_inc(s_stats, 1)
            dve.wait_ge(s_root, 1)
            nc.vector.reciprocal(nodes.rstd[:, :], root[:, :])

        @block.scalar
        def _(act):
            act.wait_ge(s_stats, 1)
            nc.scalar.activation(root[:, :], nodes.mean_var[:, :, 1], ACT.Sqrt, bias=nodes.eps[:, :]).then_inc(s_root, 1)


def normalised(nc, nodes, out, n):
    return nc.vector.tensor_scalar(out, nodes.x[:, bass.ds(n, 1), :].rearrange("p o c -> p (o c)"),
                                   nodes.mean_var[:, bass.ds(n, 1), 0], nodes.rstd[:, bass.ds(n, 1)],
                                   ALU.subtract, ALU.mult)


def load_nodes(nc, nodes, x):
    full = nodes.count // P
    rest = nodes.count - full * P
    with ExitStack() as ctx:
        s_in, s_pad = nc.alloc_semaphore("x_in"), nc.alloc_semaphore("x_pad")
        block = ctx.enter_context(nc.Block())

        @block.sync
        def _(sp):
            sp.dma_start(nodes.x[:, 0:full, :], x[0:full * P, :].rearrange("(i p) c -> p i c", p=P)).then_inc(s_in, 16)
            if rest:
                sp.wait_ge(s_pad, 1)
                sp.dma_start(nodes.x[0:rest, full, :], x[full * P:nodes.count, :]).then_inc(s_in, 16)
            sp.wait_ge(s_in, 16 * (2 if rest else 1))

        @block.vector
        def _(dve):
            nc.vector.memset(nodes.x[:, nodes.tiles - 1, :], 0.0).then_inc(s_pad, 1)


def project(nc, consts, nodes, w, src_table, dst_table):
    D, tiles = nodes.dim, nodes.tiles
    KT = D // P
    H = w["rel_pri"].shape[0]
    DK = D // H
    INNER = w["Wout"].shape[1]
    DH = 64
    MH = INNER // DH
    PAIRS = INNER // P
    KV, Q, MK = 2 * D, 3 * D, 3 * D
    MV = MK + INNER
    COLS = MV + INNER
    EPS = 1e-5
    with ExitStack() as ctx:
        sb = lambda n, s: ctx.enter_context(nc.sbuf_tensor(f"p_{n}", s, F32))
        w_all = sb("w_all", [P, KT, COLS])
        bias = sb("bias", [P, 3 * D])
        wout_t = sb("wout_t", [P, PAIRS, D])
        wq_mix = sb("wq_mix", [P, PAIRS, D])
        alpha = sb("alpha", [P, 2])

        with ExitStack() as own_ctx:
            sbw = lambda n, s: own_ctx.enter_context(nc.sbuf_tensor(f"w_{n}", s, F32))
            sem = lambda n: nc.alloc_semaphore(f"w_{n}")
            wk, wv, wq, wa = sbw("k", [P, KT, D]), sbw("v", [P, KT, D]), sbw("q", [P, KT, D]), sbw("a", [P, KT, D])
            mixed = sbw("mixed", [P, 2 * PAIRS, D])
            wout = sbw("out", [P, KT, INNER])
            rel = sbw("rel", [P, 2, KT, D])
            pri = sbw("pri", [P, H])
            bcol = sbw("bcol", [P, 2, KT])
            bwide = sbw("bwide", [P, 2, KT, P])
            brow = sbw("brow", [P, 3, D])
            skip = sbw("skip", [P, 3])
            mean = sbw("mean", [P, KT * 2 * MH])
            p_w = [own_ctx.enter_context(nc.psum_tensor(f"w_prod{k}", [P, BANK], F32)) for k in range(2)]
            s_in, s_zero, s_rel, s_ready, s_taken = sem("in"), sem("zeroed"), sem("rel_in"), sem("turned"), sem("taken")
            s_own, s_scaled, s_prod, s_pt, s_exp = sem("steps"), sem("scaled"), sem("products"), sem("products_taken"), sem("exp")
            loads = [(wk[:, :, :], w["Wk"].rearrange("(i p) c -> p i c", p=P)), (wv[:, :, :], w["Wv"].rearrange("(i p) c -> p i c", p=P)),
                     (wq[:, :, :], w["Wq"].rearrange("(i p) c -> p i c", p=P)), (wa[:, :, :], w["Wa"].rearrange("(i p) c -> p i c", p=P)),
                     (wq_mix[:, :, :], w["Wqkv"][0:INNER, :].rearrange("(i p) c -> p i c", p=P)),
                     (mixed[:, :, :], w["Wqkv"][INNER:3 * INNER, :].rearrange("(i p) c -> p i c", p=P)),
                     (wout[:, :, :], w["Wout"].rearrange("(i p) c -> p i c", p=P)),
                     (pri[:, :], on_all(w["rel_pri"], H)), (brow[:, 0, :], on_all(w["bq"], D)),
                     (brow[:, 1, :], on_all(w["ba"], D)), (brow[:, 2, :], on_all(w["bout"], D)),
                     (skip[:, 0:1], on_all(w["skip"], 1))]
            cols_in = [(bcol[:, a, :], w[n].rearrange("(i p) -> p i", p=P)) for a, n in enumerate(("bk", "bv"))]
            blocks_in = [(rel[h * DK % P:h * DK % P + DK, a, h * DK // P, h * DK:(h + 1) * DK], w[n][h, :, :])
                         for a, n in enumerate(("rel_att", "rel_msg")) for h in range(H)]
            jobs = [(w_all[:, kt, KV + o * P:KV + (o + 1) * P], wq[:, o, kt * P:(kt + 1) * P]) for o in range(KT) for kt in range(KT)]
            jobs += [(w_all[:, kt, MK + o * P:MK + (o + 1) * P], mixed[:, o, kt * P:(kt + 1) * P]) for o in range(2 * PAIRS) for kt in range(KT)]
            jobs += [(wout_t[:, f, o * P:(o + 1) * P], wout[:, o, f * P:(f + 1) * P]) for o in range(KT) for f in range(PAIRS)]
            jobs += [(nodes.wa_t[:, kt, o * P:(o + 1) * P], wa[:, o, kt * P:(kt + 1) * P]) for o in range(KT) for kt in range(KT)]
            turn_pe, turn_dve = turn_all(nc, "w", own_ctx, jobs, consts.ident, s_ready, s_taken)
            block = own_ctx.enter_context(nc.Block())

            @block.sync
            def _(sp):
                for out, in_ in loads:
                    sp.dma_start(out, in_).then_inc(s_in, 16)
                for out, in_ in cols_in:
                    sp.dma_start(out, in_, allow_slow_non_contiguous=True).then_inc(s_in, 16)
                sp.wait_ge(s_zero, 1)
                for out, in_ in blocks_in:
                    sp.dma_start(out, in_).then_inc(s_rel, 16)

            @block.scalar
            def _(act):
                act.wait_ge(s_in, 16 * (len(loads) + len(cols_in)))
                nc.scalar.activation(skip[:, 1:2], skip[:, 0:1], ACT.Exp, scale=-1.0).then_inc(s_exp, 1)

            @block.tensor
            def _(pe):
                pe.wait_ge(s_in, 16 * (len(loads) + len(cols_in)))
                turn_pe(pe)
                pe.wait_ge(s_scaled, 1)
                for a, wt in enumerate((wk, wv)):
                    for kt in range(KT):
                        n = a * KT + kt
                        if n >= 2:
                            pe.wait_ge(s_pt, n - 1)
                        for o in range(KT):
                            mm = pe.matmul(p_w[n % 2][:, 0:D], wt[:, o, kt * P:(kt + 1) * P], rel[:, a, o, :],
                                           start=(o == 0), stop=(o == KT - 1))
                        mm.then_inc(s_prod, 1)
                for a in range(2):
                    pe.wait_ge(s_pt, 2 * KT - 1 + a)
                    for o in range(KT):
                        mm = pe.matmul(p_w[a][:, 0:D], bwide[:, a, o, :], rel[:, a, o, :], start=(o == 0), stop=(o == KT - 1))
                    mm.then_inc(s_prod, 1)

            @block.vector
            def _(dve):
                own = Steps(dve, s_own)
                nc.vector.memset(rel[:, :, :, :], 0.0).then_inc(s_zero, 1)
                dve.wait_ge(s_in, 16 * (len(loads) + len(cols_in)))
                for a in range(2):
                    for kt in range(KT):
                        nc.vector.tensor_copy(bwide[:, a, kt, :], bcol[:, a, kt:kt + 1].broadcast_to([P, P]))
                nc.vector.tensor_copy(bias[:, KV:3 * D], brow[:, 0, :])
                dve.wait_ge(s_exp, 1)
                own.link(nc.vector.tensor_scalar(skip[:, 2:3], skip[:, 1:2], 1.0, None, ALU.add))
                own.link(nc.vector.reciprocal(alpha[:, 0:1], skip[:, 2:3]))
                nc.vector.tensor_scalar(alpha[:, 1:2], alpha[:, 0:1], -1.0, 1.0, ALU.mult, ALU.add)
                nc.vector.scalar_tensor_tensor(nodes.bias[:, :], brow[:, 1, :], alpha[:, 0:1], brow[:, 2, :], ALU.mult, ALU.add)
                dve.wait_ge(s_rel, 16 * len(blocks_in))
                for kt in range(KT):
                    r = rel[:, 0, kt, :].rearrange("p (h e) -> p h e", h=H)
                    last = nc.vector.tensor_tensor(r, r, pri[:, :].unsqueeze(2).broadcast_to([P, H, DK]), ALU.mult)
                own.link(last)
                nc.vector.tensor_scalar(rel[:, 0, :, :], rel[:, 0, :, :], float(DK) ** -0.5, None, ALU.mult).then_inc(s_scaled, 1)
                turn_dve(dve)
                nc.vector.tensor_scalar(nodes.wa_t[:, :, :], nodes.wa_t[:, :, :], alpha[:, 0:1], None, ALU.mult)
                m4 = w_all[:, :, MK:COLS].rearrange("p k (g d) -> p k g d", d=DH)
                for kt in range(KT):
                    last = nc.vector.tensor_reduce(mean[:, kt * 2 * MH:(kt + 1) * 2 * MH], m4[:, kt, :, :], AX.X, ALU.add)
                own.link(last)
                own.link(nc.vector.tensor_scalar(mean[:, :], mean[:, :], 1.0 / DH, None, ALU.mult))
                for kt in range(KT):
                    nc.vector.tensor_tensor(m4[:, kt, :, :], m4[:, kt, :, :],
                                            mean[:, kt * 2 * MH:(kt + 1) * 2 * MH].unsqueeze(2).broadcast_to([P, 2 * MH, DH]), ALU.subtract)
                for a in range(2):
                    for kt in range(KT):
                        n = a * KT + kt
                        dve.wait_ge(s_prod, n + 1)
                        nc.vector.tensor_copy(w_all[:, kt, a * D:(a + 1) * D], p_w[n % 2][:, 0:D]).then_inc(s_pt, 1)
                for a in range(2):
                    dve.wait_ge(s_prod, 2 * KT + a + 1)
                    nc.vector.tensor_copy(bias[:, a * D:(a + 1) * D], p_w[a][:, 0:D])

        with ExitStack() as own_ctx:
            sbn = lambda n, s: own_ctx.enter_context(nc.sbuf_tensor(f"n_{n}", s, F32))
            ps = lambda n: own_ctx.enter_context(nc.psum_tensor(f"n_p_{n}", [P, BANK], F32))
            sem = lambda n: nc.alloc_semaphore(f"n_{n}")
            xn = sbn("xn", [P, 2, D])
            xt = sbn("xt", [P, 2, D])
            kv_o, q_o = sbn("kv_out", [P, 2, 2 * D]), sbn("q_out", [P, 2, D])
            square = sbn("square", [P, 2 * INNER])
            power = sbn("power", [P, 2 * MH])
            root = sbn("root", [P, 2 * MH])
            inv = sbn("inv", [P, 2 * MH])
            both = sbn("both", [P, MH])
            mk = sbn("mk", [P, 2, INNER])
            mv = sbn("mv", [P, 2, INNER])
            dots = sbn("dots", [P, PAIRS, P])
            folded = sbn("folded", [P, PAIRS, D])
            p_t, p_kv, p_q, p_mk, p_mv, p_dots, p_end = (ps(n) for n in ("t", "kv", "q", "mk", "mv", "dots", "end"))
            (s_xn, s_turn, s_xt, s_kv, s_q, s_mk, s_mv, s_kvo, s_qo, s_sq, s_pow, s_root, s_mks, s_mvs, s_dots, s_own,
             s_end, s_ended) = (sem(n) for n in ("xn", "turned", "xt", "kv", "q", "mk", "mv", "kv_kept", "q_kept", "squares",
                                                 "power", "root", "mk_kept", "mv_kept", "dots", "steps", "end", "ended"))
            s_out = [sem(f"out{b}") for b in range(2)]
            block = own_ctx.enter_context(nc.Block())

            @block.sync
            def _(sp):
                def store(i, b, first):
                    n = 2 * i + b
                    sp.wait_ge(s_kvo, n + 1)
                    sp.dma_start(src_table[bass.ds(n * P, P), :], kv_o[:, b, :]).then_inc(s_out[b], 16)
                    sp.wait_ge(s_qo, n + 1)
                    sp.dma_start(dst_table[bass.ds(n * P, P), :], q_o[:, b, :]).then_inc(s_out[b], 16)

                group_loop(sp, tiles, store)
                sp.wait_ge(s_out[0], 32 * (tiles - tiles // 2))
                sp.wait_ge(s_out[1], 32 * (tiles // 2))

            @block.vector
            def _(dve):
                own = Steps(dve, s_own)

                def tile(i, b, first):
                    n = 2 * i + b
                    if not first:
                        dve.wait_ge(s_turn, n - 1)
                    normalised(nc, nodes, xn[:, b, :], n).then_inc(s_xn, 1)
                    if not first:
                        dve.wait_ge(s_out[b], 32 * i)
                    dve.wait_ge(s_kv, n + 1)
                    nc.vector.tensor_tensor(kv_o[:, b, :], p_kv[:, :], bias[:, 0:KV], ALU.add).then_inc(s_kvo, 1)
                    dve.wait_ge(s_q, n + 1)
                    nc.vector.tensor_tensor(q_o[:, b, :], p_q[:, 0:D], bias[:, KV:3 * D], ALU.add).then_inc(s_qo, 1)
                    dve.wait_ge(s_sq, n + 1)
                    nc.vector.tensor_reduce(power[:, :], square[:, :].rearrange("p (g d) -> p g d", d=DH), AX.X, ALU.add).then_inc(s_pow, 1)
                    dve.wait_ge(s_root, n + 1)
                    own.link(nc.vector.reciprocal(inv[:, :], root[:, :]))
                    own.link(nc.vector.tensor_tensor(both[:, :], inv[:, 0:MH], inv[:, MH:2 * MH], ALU.mult))
                    if not first:
                        dve.wait_ge(s_dots, n - 1)
                    nc.vector.tensor_tensor(mk[:, b, :].rearrange("p (h d) -> p h d", d=DH), p_mk[:, :].rearrange("p (h d) -> p h d", d=DH),
                                            both[:, :].unsqueeze(2).broadcast_to([P, MH, DH]), ALU.mult).then_inc(s_mks, 1)

                group_loop(dve, tiles, tile, own, 4)
                own.link(nc.vector.memset(dots[:, :, :], 0.0))
                dve.wait_ge(s_dots, tiles)
                pd = p_dots[:, :].rearrange("p (a c) -> p a c", c=P)
                nc.vector.tensor_copy(dots[0:DH, :, 0:DH], pd[0:DH, :, 0:DH])
                nc.vector.tensor_copy(dots[DH:P, :, DH:P], pd[DH:P, :, DH:P]).then_inc(s_ended, 1)
                for a in range(PAIRS):
                    dve.wait_ge(s_end, a + 1)
                    nc.vector.tensor_copy(folded[:, a, :], p_end[:, 0:D]).then_inc(s_ended, 1)
                for kt in range(KT):
                    dve.wait_ge(s_end, PAIRS + kt + 1)
                    own.link(nc.vector.tensor_scalar(nodes.gx[:, kt, :], p_end[:, 0:D], 1.0 / nodes.count, None, ALU.mult))
                    d = nodes.gx[:, kt, kt * P:(kt + 1) * P]
                    nc.vector.scalar_tensor_tensor(d, consts.ident[:, :], alpha[:, 1:2], d, ALU.mult, ALU.add).then_inc(s_ended, 1)

            @block.scalar
            def _(act):
                def tile(i, b, first):
                    n = 2 * i + b
                    act.wait_ge(s_turn, n + 1)
                    if not first:
                        act.wait_ge(s_mv, n - 1)
                    nc.scalar.copy(xt[:, b, :], p_t[:, 0:D]).then_inc(s_xt, 1)
                    act.wait_ge(s_mk, n + 1)
                    if not (first and b == 0):
                        act.wait_ge(s_pow, n)
                    nc.scalar.activation(square[:, 0:INNER], p_mk[:, :], ACT.Square)
                    act.wait_ge(s_mv, n + 1)
                    nc.scalar.activation(square[:, INNER:2 * INNER], p_mv[:, :], ACT.Square).then_inc(s_sq, 1)
                    if not first:
                        act.wait_ge(s_dots, n - 1)
                    nc.scalar.copy(mv[:, b, :], p_mv[:, :]).then_inc(s_mvs, 1)
                    act.wait_ge(s_pow, n + 1)
                    nc.scalar.activation(root[:, :], power[:, :], ACT.Sqrt, bias=nodes.eps[:, :], scale=1.0 / DH).then_inc(s_root, 1)

                group_loop(act, tiles, tile)

            @block.tensor
            def _(pe):
                def tile(i, b, first):
                    n = 2 * i + b
                    pe.wait_ge(s_xn, n + 1)
                    for kt in range(KT):
                        t = pe.transpose(p_t[:, kt * P:(kt + 1) * P], xn[:, b, kt * P:(kt + 1) * P], consts.ident[:, :])
                    t.then_inc(s_turn, 1)
                    pe.wait_ge(s_xt, n + 1)
                    for bank, c0, c1, done, kept in ((p_kv, 0, KV, s_kv, s_kvo), (p_q, KV, 3 * D, s_q, s_qo),
                                                     (p_mk, MK, MV, s_mk, s_mks), (p_mv, MV, COLS, s_mv, s_mvs)):
                        if not (first and b == 0):
                            pe.wait_ge(kept, n)
                        for kt in range(KT):
                            mm = pe.matmul(bank[:, 0:c1 - c0], xt[:, b, kt * P:(kt + 1) * P], w_all[:, kt, c0:c1],
                                           start=(kt == 0), stop=(kt == KT - 1))
                        mm.then_inc(done, 1)
                    pe.wait_ge(s_mks, n + 1)
                    pe.wait_ge(s_mvs, n + 1)
                    for a in range(PAIRS):
                        mm = pe.matmul(p_dots[:, a * P:(a + 1) * P], mv[:, b, a * P:(a + 1) * P], mk[:, b, a * P:(a + 1) * P],
                                       start=(first and b == 0 and a == 0), stop=False, skip_group_check=True)
                    mm.then_inc(s_dots, 1)

                group_loop(pe, tiles, tile)
                for a in range(PAIRS):
                    pe.wait_ge(s_ended, a + 1)
                    pe.matmul(p_end[:, 0:D], dots[:, a, :], wout_t[:, a, :], start=True, stop=True).then_inc(s_end, 1)
                for kt in range(KT):
                    pe.wait_ge(s_ended, PAIRS + kt + 1)
                    for a in range(PAIRS):
                        mm = pe.matmul(p_end[:, 0:D], wq_mix[:, a, kt * P:(kt + 1) * P], folded[:, a, :],
                                       start=(a == 0), stop=(a == PAIRS - 1))
                    mm.then_inc(s_end, 1)


def gather_sums(nc, name, consts, nodes, lists, partial, counts, ends, heads, width, before, at_end):
    batches = lists.batches
    tiles_b = spans(batches, P)
    nt, tiles = len(tiles_b), nodes.tiles
    sums = heads * (width + 1)
    cols = sums + heads
    with ExitStack() as outer:
        ends_of = outer.enter_context(nc.sbuf_tensor(f"{name}_ends_of", [P, nt, cols], F32))
        edge_i = outer.enter_context(nc.sbuf_tensor(f"{name}_edge_i", [P, 3, tiles], I32))
        with ExitStack() as ctx:
            sb = lambda n, s: ctx.enter_context(nc.sbuf_tensor(f"{name}_{n}", s, F32))
            sem = lambda n: nc.alloc_semaphore(f"{name}_{n}")
            wide = sb("wide", [P, nt, heads])
            line = sb("line", [heads, 2, batches])
            cut = sb("cut", [heads, 2, batches])
            top = sb("top", [heads, 3, batches])
            back = sb("back", [P, nt, 2, heads])
            weight = sb("weight", [P, nt, heads])
            edge = sb("edge", [P, 4, tiles])
            zero = sb("zero", [1, cols])
            s_in, s_wide, s_t1, s_k1, s_t2, s_k2 = (sem(n) for n in ("in", "wide", "turned", "taken", "turned_back", "taken_back"))
            s_own, s_top, s_diff, s_w, s_zero, s_zout = (sem(n) for n in ("steps", "tops", "diffs", "weights", "zero", "zero_out"))
            jobs1 = [(line[:, 0, t0:t0 + k], ends_of[0:k, i, sums:cols]) for i, (t0, k) in enumerate(tiles_b)]
            jobs1 += [(line[:, 1, t0:t0 + k], wide[0:k, i, :]) for i, (t0, k) in enumerate(tiles_b)]
            jobs2 = [(back[0:k, i, a, :], top[:, a + 1, t0:t0 + k]) for i, (t0, k) in enumerate(tiles_b) for a in range(2)]
            pe1, dve1 = turn_all(nc, f"{name}_a", ctx, jobs1, consts.ident, s_t1, s_k1)
            pe2, dve2 = turn_all(nc, f"{name}_b", ctx, jobs2, consts.ident, s_t2, s_k2)
            block = ctx.enter_context(nc.Block())

            @block.sync
            def _(sp):
                for i, (t0, k) in enumerate(tiles_b):
                    sp.dma_start(ends_of[0:k, i, :], partial[(P - 1) * batches + t0:(P - 1) * batches + t0 + k, :]).then_inc(s_in, 16)
                sp.wait_ge(s_zero, 1)
                sp.dma_start(partial[P * batches:P * batches + 1, :], zero[:, :]).then_inc(s_zout, 16)
                sp.wait_ge(s_zout, 16)

            @block.tensor
            def _(pe):
                pe.wait_ge(s_in, 16 * nt)
                pe.wait_ge(s_wide, 1)
                pe1(pe)
                pe.wait_ge(s_top, 1)
                pe2(pe)

            @block.scalar
            def _(act):
                act.wait_ge(s_diff, 1)
                nc.scalar.activation(weight[:, :, :], weight[:, :, :], ACT.Exp).then_inc(s_w, 1)

            @block.vector
            def _(dve):
                own = Steps(dve, s_own)
                nc.vector.memset(zero[:, :], 0.0).then_inc(s_zero, 1)
                own.link(nc.vector.tensor_scalar(edge[:, 0, :], ends[:, 0:tiles], -1.0, 0.0, ALU.add, ALU.max))
                own.link(nc.vector.tensor_copy(edge_i[:, 0, :], edge[:, 0, :]))
                nc.vector.tensor_scalar(edge_i[:, 1, :], edge_i[:, 0, :], P - 1, None, ALU.bitwise_and)
                own.link(nc.vector.tensor_scalar(edge_i[:, 2, :], edge_i[:, 0, :], 7, None, ALU.logical_shift_right))
                nc.vector.tensor_copy(edge[:, 0, :], edge_i[:, 1, :])
                own.link(nc.vector.tensor_copy(edge[:, 1, :], edge_i[:, 2, :]))
                nc.vector.tensor_scalar(edge[:, 2, :], counts[:, 0:tiles], 0.0, None, ALU.is_equal)
                own.link(nc.vector.tensor_scalar(edge[:, 3, :], edge[:, 0, :], float(P - 1), None, ALU.is_equal))
                own.link(nc.vector.tensor_tensor(edge[:, 2, :], edge[:, 2, :], edge[:, 3, :], ALU.max))
                own.link(nc.vector.scalar_tensor_tensor(edge[:, 1, :], edge[:, 0, :], float(batches), edge[:, 1, :], ALU.mult, ALU.add))
                own.link(nc.vector.tensor_scalar(edge[:, 0, :], edge[:, 1, :], -1.0, float(P * batches), ALU.mult, ALU.add))
                own.link(nc.vector.tensor_tensor(edge[:, 0, :], edge[:, 0, :], edge[:, 2, :], ALU.mult))
                own.link(nc.vector.tensor_tensor(edge_i[:, 0, :], edge[:, 1, :], edge[:, 0, :], ALU.add))

                nc.vector.tensor_copy(wide[:, :, :], lists.last[:, :].unsqueeze(2).broadcast_to([P, nt, heads])).then_inc(s_wide, 1)
                nc.vector.memset(cut[:, :, :], -FAR)
                own.link(nc.vector.memset(weight[:, :, :], 0.0))
                dve.wait_ge(s_in, 16 * nt)
                dve1(dve)
                own.link(nc.vector.tensor_tensor(cut[:, 0, 1:], line[:, 1, 1:], line[:, 1, 0:batches - 1], ALU.not_equal))
                own.link(nc.vector.tensor_scalar(cut[:, 0, 1:], cut[:, 0, 1:], -FAR, None, ALU.mult))
                own.link(nc.vector.tensor_copy(cut[:, 1, 0:batches - 1], cut[:, 0, 1:]))
                own.link(nc.vector.tensor_tensor_scan(top[:, 0, :], cut[:, 0, :], line[:, 0, :], 0.0, ALU.add, ALU.max))
                own.link(nc.vector.tensor_tensor_scan(top[:, 1, ::-1], cut[:, 1, ::-1], top[:, 0, ::-1], 0.0, ALU.add, ALU.max))
                own.link(nc.vector.tensor_scalar(top[:, 2, :], cut[:, 0, :], 0.0, None, ALU.is_lt))
                nc.vector.tensor_tensor(top[:, 2, :], top[:, 2, :], top[:, 1, :], ALU.mult).then_inc(s_top, 1)
                dve2(dve)
                for i, (t0, k) in enumerate(tiles_b):
                    last = nc.vector.tensor_tensor(weight[0:k, i, :], ends_of[0:k, i, sums:cols], back[0:k, i, 0, :], ALU.subtract)
                last.then_inc(s_diff, 1)
                dve.wait_ge(s_diff, 1)
                dve.wait_ge(s_w, 1)
                for i, (t0, k) in enumerate(tiles_b):
                    e = ends_of[0:k, i, 0:sums].rearrange("p (h w) -> p h w", h=heads)
                    nc.vector.tensor_tensor(e, e, weight[0:k, i, :].unsqueeze(2).broadcast_to([k, heads, width + 1]), ALU.mult)
                    nc.vector.tensor_copy(ends_of[0:k, i, sums:cols], back[0:k, i, 1, :])

        with ExitStack() as ctx:
            sb = lambda n, s, d=F32: ctx.enter_context(nc.sbuf_tensor(f"{name}_{n}", s, d))
            sem = lambda n: nc.alloc_semaphore(f"{name}_{n}")
            ids = sb("ids", [P, 2, P])
            chosen = sb("chosen", [P, 2, nt, P])
            ring = sb("ring", [P, 2, 1], I32)
            row = sb("row", [P, 2, cols])
            bank_s = [ctx.enter_context(nc.psum_tensor(f"{name}_sum{b}", [P, BANK], F32)) for b in range(2)]
            s_step, s_rows, s_ring, s_chosen, s_sum, s_kept = (sem(n) for n in ("ids_step", "rows", "ring", "chosen", "sums", "kept"))
            s_got = [sem(f"got{b}") for b in range(2)]
            block = ctx.enter_context(nc.Block())

            @block.gpsimd
            def _(pool):
                def fetch(i, b, first):
                    n = 2 * i + b
                    if not first:
                        pool.wait_ge(s_rows, n - 1)
                    pool.tensor_copy(ring[:, b, :], edge_i[:, 0, bass.ds(n, 1)]).then_inc(s_ring, 1)
                    pool.wait_ge(s_ring, n + 1)
                    pool.nop(nofuse=True)
                    pool.indirect_dma_start(row[:, b, :], None, partial[:, :],
                                            bass.IndirectOffsetOnAxis(ap=ring[:, b, :], axis=0)).then_inc(s_got[b], 16)

                group_loop(pool, tiles, fetch)

            @block.tensor
            def _(pe):
                def tile(i, b, first):
                    n = 2 * i + b
                    pe.wait_ge(s_chosen, n + 1)
                    if not first:
                        pe.wait_ge(s_kept, n - 1)
                    for kt, (t0, k) in enumerate(tiles_b):
                        if k < P:
                            pe.nop(nofuse=True)
                        mm = pe.matmul(bank_s[b][:, 0:cols], chosen[0:k, b, kt, :], ends_of[0:k, kt, :], start=(kt == 0), stop=(kt == nt - 1))
                    mm.then_inc(s_sum, 1)

                group_loop(pe, tiles, tile)

            @block.scalar
            def _(act):
                def keep(i, b, first):
                    n = 2 * i + b
                    act.wait_ge(s_sum, n + 1)
                    nc.scalar.copy(before[:, bass.ds(n, 1), :].rearrange("p o c -> p (o c)"), bank_s[b][:, 0:cols]).then_inc(s_kept, 1)

                group_loop(act, tiles, keep)

            @block.vector
            def _(dve):
                own = Steps(dve, s_step)
                own.link(nc.vector.tensor_copy(ids[:, 0, :], consts.lane_b[:, :]))

                def choose(i, b, first):
                    n = 2 * i + b
                    if not first:
                        dve.wait_ge(s_sum, n - 1)
                    nc.vector.tensor_tensor(chosen[:, b, :, :], ids[:, b, :].unsqueeze(1).broadcast_to([P, nt, P]),
                                            lists.last[:, :].unsqueeze(2).broadcast_to([P, nt, P]), ALU.is_equal).then_inc(s_chosen, 1)
                    own.link(nc.vector.tensor_scalar(ids[:, 1 - b, :], ids[:, b, :], float(P), None, ALU.add))
                    dve.wait_ge(s_got[b], 16 * i + 16)
                    nc.vector.tensor_copy(at_end[:, bass.ds(n, 1), :].rearrange("p o c -> p (o c)"), row[:, b, :]).then_inc(s_rows, 1)

                group_loop(dve, tiles, choose, own, 2)


def weights_of(nc, own, marks, before, at_end, heads, width, more=None):
    sums = heads * (width + 1)
    parts = [before, at_end]
    for k, part in enumerate(parts):
        z = part[:, :, 0:sums].rearrange("p n (h w) -> p n h w", h=heads)[:, :, :, width]
        own.link(nc.vector.tensor_scalar(marks[:, k], z, 0.0, 1.0, ALU.is_gt, ALU.subtract))
        own.link(nc.vector.tensor_scalar(marks[:, k], marks[:, k], FAR, None, ALU.mult))
        own.link(nc.vector.tensor_tensor(marks[:, k], marks[:, k], part[:, :, sums:sums + heads], ALU.add))
    used = 2 + (more is not None)
    if more is not None:
        own.link(nc.vector.tensor_copy(marks[:, 2], more))
    own.link(nc.vector.tensor_tensor(marks[:, 3], marks[:, 0], marks[:, 1], ALU.max))
    if more is not None:
        own.link(nc.vector.tensor_tensor(marks[:, 3], marks[:, 3], marks[:, 2], ALU.max))
    for k in range(used):
        last = nc.vector.tensor_tensor(marks[:, k], marks[:, k], marks[:, 3], ALU.subtract)
    return last


def first_residual(nc, consts, nodes, before, at_end, heads, width):
    D, tiles = nodes.dim, nodes.tiles
    KT = D // P
    sums = heads * (width + 1)
    with ExitStack() as ctx:
        sb = lambda n, s: ctx.enter_context(nc.sbuf_tensor(f"r_{n}", s, F32))
        sem = lambda n: nc.alloc_semaphore(f"r_{n}")
        marks = sb("marks", [P, 4, tiles, heads])
        xn = sb("xn", [P, 2, D])
        t_now = sb("t", [P, 2, D])
        turned = sb("turned", [P, 2, 2 * D])
        p_t = [ctx.enter_context(nc.psum_tensor(f"r_t{b}", [P, BANK], F32)) for b in range(2)]
        p_y = [ctx.enter_context(nc.psum_tensor(f"r_y{b}", [P, BANK], F32)) for b in range(2)]
        s_own, s_marks, s_w, s_ready, s_turn, s_kept, s_y, s_x = (sem(n) for n in (
            "steps", "marks", "weights", "inputs", "turned", "turned_kept", "product", "x"))
        block = ctx.enter_context(nc.Block())
        whole = lambda part: part[:, :, 0:sums].rearrange("p n (h w) -> p n h w", h=heads)

        @block.vector
        def _(dve):
            own = Steps(dve, s_own)
            weights_of(nc, own, marks, before, at_end, heads, width).then_inc(s_marks, 1)
            dve.wait_ge(s_w, 1)
            for k, part in enumerate((before, at_end)):
                last = nc.vector.tensor_tensor(whole(part), whole(part), marks[:, k].unsqueeze(3)
                                               .broadcast_to([P, tiles, heads, width + 1]), ALU.mult)
            own.link(last)
            own.link(nc.vector.tensor_tensor(before[:, :, 0:sums], before[:, :, 0:sums], at_end[:, :, 0:sums], ALU.add))
            own.link(nc.vector.tensor_scalar(marks[:, 2], whole(before)[:, :, :, width], 1.0e-30, None, ALU.max))
            own.link(nc.vector.reciprocal(marks[:, 3], marks[:, 2]))

            def tile(i, b, first):
                n = 2 * i + b
                if not first:
                    dve.wait_ge(s_turn, n - 1)
                normalised(nc, nodes, xn[:, b, :], n)
                nc.vector.tensor_tensor(t_now[:, b, :].rearrange("p (h w) -> p h w", h=heads),
                                        before[:, bass.ds(n, 1), 0:sums].rearrange("p o (h w) -> p (o h) w", h=heads)[:, :, 0:width],
                                        marks[:, 3, bass.ds(n, 1), :].rearrange("p o h -> p (o h)").unsqueeze(2)
                                        .broadcast_to([P, heads, width]), ALU.mult).then_inc(s_ready, 1)
                x = nodes.x[:, bass.ds(n, 1), :].rearrange("p o c -> p (o c)")
                dve.wait_ge(s_ready, n + 1)
                own.link(nc.vector.tensor_tensor(x, x, nodes.bias[:, :], ALU.add))
                dve.wait_ge(s_y, n + 1)
                nc.vector.tensor_tensor(x, x, p_y[b][:, 0:D], ALU.add).then_inc(s_x, 1)

            group_loop(dve, tiles, tile, own, 2)

        @block.scalar
        def _(act):
            act.wait_ge(s_marks, 1)
            nc.scalar.activation(marks[:, 0:2], marks[:, 0:2], ACT.Exp).then_inc(s_w, 1)

            def tile(i, b, first):
                n = 2 * i + b
                act.wait_ge(s_turn, n + 1)
                if not first:
                    act.wait_ge(s_y, n - 1)
                nc.scalar.copy(turned[:, b, :], p_t[b][:, :]).then_inc(s_kept, 1)

            group_loop(act, tiles, tile)

        @block.tensor
        def _(pe):
            def tile(i, b, first):
                n = 2 * i + b
                pe.wait_ge(s_ready, n + 1)
                if not first:
                    pe.wait_ge(s_kept, n - 1)
                for a, part in enumerate((t_now, xn)):
                    for kt in range(KT):
                        c = (a * KT + kt) * P
                        mm = pe.transpose(p_t[b][:, c:c + P], part[:, b, kt * P:(kt + 1) * P], consts.ident[:, :])
                mm.then_inc(s_turn, 1)
                pe.wait_ge(s_kept, n + 1)
                if not first:
                    pe.wait_ge(s_x, n - 1)
                for a, w in enumerate((nodes.wa_t, nodes.gx)):
                    for kt in range(KT):
                        c = (a * KT + kt) * P
                        mm = pe.matmul(p_y[b][:, 0:D], turned[:, b, c:c + P], w[:, kt, :], start=(c == 0), stop=(c == (2 * KT - 1) * P))
                mm.then_inc(s_y, 1)

            group_loop(pe, tiles, tile)


def gat_inputs(nc, consts, nodes, w, y_t, feats, src_table, dst_table):
    D, tiles = nodes.dim, nodes.tiles
    KT = D // P
    H, E = w["att_src"].shape
    HE = H * E
    F = HE + 2 * H
    with ExitStack() as ctx:
        sb = lambda n, s: ctx.enter_context(nc.sbuf_tensor(f"y_{n}", s, F32))
        sem = lambda n: nc.alloc_semaphore(f"y_{n}")
        wg = sb("wg", [P, KT, F])
        att = sb("att", [P, 2, HE])
        prod = sb("prod", [P, KT, HE])
        y = sb("y", [P, 2, D])
        yt = sb("yt", [P, 2, D])
        p_t = [ctx.enter_context(nc.psum_tensor(f"y_t{b}", [P, BANK], F32)) for b in range(2)]
        p_f = [ctx.enter_context(nc.psum_tensor(f"y_f{b}", [P, BANK], F32)) for b in range(2)]
        s_in, s_own, s_w, s_y, s_turn, s_kept, s_f, s_fk, s_out = (sem(n) for n in (
            "in", "steps", "weights", "rows", "turned", "turned_kept", "feats", "feats_kept", "out"))
        block = ctx.enter_context(nc.Block())

        @block.sync
        def _(sp):
            sp.dma_start(wg[:, :, 0:HE], w["W_gat"].rearrange("(k p) c -> p k c", p=P)).then_inc(s_in, 16)
            for a, n in enumerate(("att_src", "att_dst")):
                sp.dma_start(att[:, a, :], on_all(w[n].rearrange("h e -> (h e)"), HE)).then_inc(s_in, 16)
            sp.wait_ge(s_fk, tiles)
            sp.dma_start(src_table.rearrange("(i p) c -> p i c", p=P), feats[:, :, 0:HE + H]).then_inc(s_out, 16)
            sp.dma_start(dst_table.rearrange("(i p) c -> p i c", p=P), feats[:, :, HE + H:F]).then_inc(s_out, 16)
            sp.wait_ge(s_out, 32)

        @block.vector
        def _(dve):
            own = Steps(dve, s_own)
            dve.wait_ge(s_in, 48)
            for a in range(2):
                own.link(nc.vector.tensor_tensor(prod[:, :, :], wg[:, :, 0:HE], att[:, a, :].unsqueeze(1).broadcast_to([P, KT, HE]), ALU.mult))
                c = HE + a * H
                last = nc.vector.tensor_reduce(wg[:, :, c:c + H], prod[:, :, :].rearrange("p k (h e) -> p k h e", h=H), AX.X, ALU.add)
                own.link(last)
            nc.vector.memset(prod[:, 0, 0:1], 0.0).then_inc(s_w, 1)

            def tile(i, b, first):
                n = 2 * i + b
                if not first:
                    dve.wait_ge(s_turn, n - 1)
                normalised(nc, nodes, y[:, b, :], n).then_inc(s_y, 1)
                dve.wait_ge(s_f, n + 1)
                nc.vector.tensor_copy(feats[:, bass.ds(n, 1), :].rearrange("p o c -> p (o c)"), p_f[b][:, 0:F]).then_inc(s_fk, 1)

            group_loop(dve, tiles, tile)

        @block.scalar
        def _(act):
            def tile(i, b, first):
                n = 2 * i + b
                act.wait_ge(s_turn, n + 1)
                if not first:
                    act.wait_ge(s_f, n - 1)
                nc.scalar.copy(yt[:, b, :], p_t[b][:, 0:D])
                nc.scalar.copy(y_t[:, :, bass.ds(n * P, P)], p_t[b][:, 0:D].rearrange("p (k c) -> p k c", k=KT)).then_inc(s_kept, 1)

            group_loop(act, tiles, tile)

        @block.tensor
        def _(pe):
            pe.wait_ge(s_w, 1)

            def tile(i, b, first):
                n = 2 * i + b
                pe.wait_ge(s_y, n + 1)
                if not first:
                    pe.wait_ge(s_kept, n - 1)
                for kt in range(KT):
                    mm = pe.transpose(p_t[b][:, kt * P:(kt + 1) * P], y[:, b, kt * P:(kt + 1) * P], consts.ident[:, :])
                mm.then_inc(s_turn, 1)
                pe.wait_ge(s_kept, n + 1)
                if not first:
                    pe.wait_ge(s_fk, n - 1)
                for kt in range(KT):
                    mm = pe.matmul(p_f[b][:, 0:F], yt[:, b, kt * P:(kt + 1) * P], wg[:, kt, :], start=(kt == 0), stop=(kt == KT - 1))
                mm.then_inc(s_f, 1)

            group_loop(pe, tiles, tile)


def gates(nc, nodes, w, feats, before, at_end, gate):
    tiles = nodes.tiles
    H, E = w["att_src"].shape
    HE = H * E
    sums = H * (E + 1)
    with ExitStack() as ctx:
        sb = lambda n, s: ctx.enter_context(nc.sbuf_tensor(f"g_{n}", s, F32))
        sem = lambda n: nc.alloc_semaphore(f"g_{n}")
        marks = sb("marks", [P, 4, tiles, H])
        vec = sb("vec", [P, 3, HE])
        own_score = sb("own_score", [P, tiles, H])
        own_raw = sb("own_raw", [P, tiles, H])
        tmp = sb("tmp", [P, tiles, HE])
        agg = sb("agg", [P, tiles, HE])
        one = sb("one", [P, 4, tiles])
        score = sb("score", [P, tiles, E])
        lost = sb("lost", [P, tiles, E])
        beat = sb("beat", [P, tiles])
        s_in, s_own, s_marks, s_w, s_var, s_root, s_top, s_ex = (sem(n) for n in (
            "in", "steps", "marks", "weights", "var", "root", "top", "exp"))
        block = ctx.enter_context(nc.Block())

        @block.sync
        def _(sp):
            for a, n in enumerate(("b_gat", "ln_gamma", "ln_beta")):
                sp.dma_start(vec[:, a, :], on_all(w[n], HE)).then_inc(s_in, 16)

        @block.scalar
        def _(act):
            act.wait_ge(s_marks, 1)
            nc.scalar.activation(marks[:, 0:3], marks[:, 0:3], ACT.Exp).then_inc(s_w, 1)
            act.wait_ge(s_var, 1)
            nc.scalar.activation(one[:, 1, :], one[:, 0, :], ACT.Sqrt, bias=nodes.eps[:, :], scale=1.0 / HE).then_inc(s_root, 1)
            act.wait_ge(s_top, 1)
            nc.scalar.activation(score[:, :, :], score[:, :, :], ACT.Exp).then_inc(s_ex, 1)

        @block.vector
        def _(dve):
            own = Steps(dve, s_own)
            V = nc.vector
            own.link(V.tensor_tensor(own_raw[:, :, :], feats[:, :, HE:HE + H], feats[:, :, HE + H:HE + 2 * H], ALU.add))
            own.link(V.tensor_scalar(own_score[:, :, :], own_raw[:, :, :], 0.2, None, ALU.mult))
            own.link(V.tensor_tensor(own_score[:, :, :], own_score[:, :, :], own_raw[:, :, :], ALU.max))
            weights_of(nc, own, marks, before, at_end, H, E, own_score[:, :, :]).then_inc(s_marks, 1)
            dve.wait_ge(s_w, 1)
            whole = lambda part: part[:, :, 0:sums].rearrange("p n (h w) -> p n h w", h=H)
            h4 = lambda t: t.rearrange("p n (h e) -> p n h e", h=H)
            for k, part in enumerate((before, at_end)):
                last = V.tensor_tensor(whole(part), whole(part), marks[:, k].unsqueeze(3).broadcast_to([P, tiles, H, E + 1]), ALU.mult)
            own.link(last)
            own.link(V.tensor_tensor(before[:, :, 0:sums], before[:, :, 0:sums], at_end[:, :, 0:sums], ALU.add))
            wide = lambda t: t.unsqueeze(3).broadcast_to([P, tiles, H, E])
            own.link(V.tensor_tensor(h4(tmp[:, :, :]), h4(feats[:, :, 0:HE]), wide(marks[:, 2]), ALU.mult))
            own.link(V.tensor_tensor(h4(agg[:, :, :]), whole(before)[:, :, :, 0:E], h4(tmp[:, :, :]), ALU.add))
            own.link(V.tensor_tensor(own_raw[:, :, :], whole(before)[:, :, :, E], marks[:, 2], ALU.add))
            own.link(V.tensor_scalar(own_raw[:, :, :], own_raw[:, :, :], 1.0e-16, None, ALU.add))
            own.link(V.reciprocal(own_score[:, :, :], own_raw[:, :, :]))
            own.link(V.tensor_tensor(h4(agg[:, :, :]), h4(agg[:, :, :]), wide(own_score[:, :, :]), ALU.mult))
            dve.wait_ge(s_in, 48)
            along = lambda a: vec[:, a, :].unsqueeze(1).broadcast_to([P, tiles, HE])
            each = lambda t: t.unsqueeze(2).broadcast_to([P, tiles, HE])
            own.link(V.tensor_tensor(agg[:, :, :], agg[:, :, :], along(0), ALU.add))
            own.link(V.tensor_reduce(one[:, 2, :], agg[:, :, :], AX.X, ALU.add))
            own.link(V.tensor_scalar(one[:, 2, :], one[:, 2, :], 1.0 / HE, None, ALU.mult))
            own.link(V.tensor_tensor(agg[:, :, :], agg[:, :, :], each(one[:, 2, :]), ALU.subtract))
            own.link(V.tensor_tensor(tmp[:, :, :], agg[:, :, :], agg[:, :, :], ALU.mult))
            V.tensor_reduce(one[:, 0, :], tmp[:, :, :], AX.X, ALU.add).then_inc(s_var, 1)
            dve.wait_ge(s_root, 1)
            own.link(V.reciprocal(one[:, 3, :], one[:, 1, :]))
            own.link(V.tensor_tensor(agg[:, :, :], agg[:, :, :], each(one[:, 3, :]), ALU.mult))
            own.link(V.tensor_tensor(agg[:, :, :], agg[:, :, :], along(1), ALU.mult))
            own.link(V.tensor_tensor(agg[:, :, :], agg[:, :, :], along(2), ALU.add))
            own.link(V.tensor_reduce(score[:, :, :], agg[:, :, :].rearrange("p n (h e) -> p n e h", h=H), AX.X, ALU.add))
            own.link(V.tensor_scalar(score[:, :, :], score[:, :, :], 1.0 / H, None, ALU.mult))
            own.link(V.memset(lost[:, :, :], 0.0))
            for e in range(E):
                for o in range(E):
                    if o != e:
                        own.link(V.tensor_tensor(beat[:, :], score[:, :, o], score[:, :, e], ALU.is_ge if o < e else ALU.is_gt))
                        own.link(V.tensor_tensor(lost[:, :, e], lost[:, :, e], beat[:, :], ALU.add))
            own.link(V.tensor_scalar(lost[:, :, :], lost[:, :, :], 1.5, None, ALU.is_lt))
            own.link(V.tensor_reduce(one[:, 0, :], score[:, :, :], AX.X, ALU.max))
            V.tensor_tensor(score[:, :, :], score[:, :, :], one[:, 0, :].unsqueeze(2).broadcast_to([P, tiles, E]), ALU.subtract)\
                .then_inc(s_top, 1)
            dve.wait_ge(s_ex, 1)
            own.link(V.tensor_tensor(score[:, :, :], score[:, :, :], lost[:, :, :], ALU.mult))
            own.link(V.tensor_reduce(one[:, 1, :], score[:, :, :], AX.X, ALU.add))
            own.link(V.reciprocal(one[:, 2, :], one[:, 1, :]))
            V.tensor_tensor(gate[:, :, :], score[:, :, :], one[:, 2, :].unsqueeze(2).broadcast_to([P, tiles, E]), ALU.mult)


def experts(nc, nodes, w, y_t, gate, out):
    D, tiles = nodes.dim, nodes.tiles
    E, _, HID = w["W1"].shape
    KT, MT = D // P, HID // P
    CH = BANK // P
    chunks, tail = tiles // CH, tiles % CH
    assert chunks % 2 == 0
    full = nodes.count // P
    rest = nodes.count - full * P
    with ExitStack() as ctx:
        sb = lambda n, s: ctx.enter_context(nc.sbuf_tensor(f"e_{n}", s, F32))
        sem = lambda n: nc.alloc_semaphore(f"e_{n}")
        w1 = sb("w1", [P, E, KT, HID])
        w2 = sb("w2", [P, E, MT, D])
        b1 = sb("b1", [P, E, MT])
        b2 = sb("b2", [P, E, D])
        hid = sb("hid", [P, 2, MT, BANK])
        p_h = [ctx.enter_context(nc.psum_tensor(f"e_h{b}", [P, BANK], F32)) for b in range(2)]
        p_o = [ctx.enter_context(nc.psum_tensor(f"e_o{b}", [P, BANK], F32)) for b in range(2)]
        s_in, s_h, s_gelu, s_o, s_acc, s_bias = (sem(n) for n in ("in", "hidden", "gelu", "product", "added", "bias"))
        s_out = sem("out")
        per_h, per_o = E * MT, E * CH
        block = ctx.enter_context(nc.Block())

        @block.sync
        def _(sp):
            sp.dma_start(w1[:, :, :, :], w["W1"].rearrange("e (k p) h -> p (e k) h", p=P)).then_inc(s_in, 16)
            sp.dma_start(w2[:, :, :, :], w["W2"].rearrange("e (m p) d -> p (e m) d", p=P)).then_inc(s_in, 16)
            for e in range(E):
                sp.dma_start(b1[:, e, :], w["b1"][e, :].rearrange("(m p) -> p m", p=P), allow_slow_non_contiguous=True).then_inc(s_in, 16)
            sp.dma_start(b2[:, :, :].rearrange("p e d -> p (e d)"), on_all(w["b2"].rearrange("e d -> (e d)"), E * D)).then_inc(s_in, 16)
            with sp.Fori(0, chunks) as c:
                sp.wait_ge(s_acc, c * per_o + per_o)
                sp.dma_start(out[bass.ds(c * (CH * P), CH * P), :].rearrange("(i p) d -> p i d", p=P),
                             nodes.x[:, bass.ds(c * CH, CH), :]).then_inc(s_out, 16)
            sp.wait_ge(s_acc, chunks * per_o + tail * E)
            stores = chunks
            for t in range(chunks * CH, tiles):
                k = P if t < full else rest
                sp.dma_start(out[t * P:t * P + k, :], nodes.x[0:k, t, :]).then_inc(s_out, 16)
                stores += 1
            sp.wait_ge(s_out, 16 * stores)

        def bank_h(c, k):
            return k % 2

        def bank_o(c, k):
            return k % 2

        def run(eng, chunk):
            chunk(0, CH, True)
            with eng.Fori(1, chunks) as c:
                chunk(c, CH, False)
            if tail:
                chunk(chunks, tail, False)

        @block.tensor
        def _(pe):
            pe.wait_ge(s_in, 16 * (E + 3))

            def hidden(c, e, size, first):
                cols = size * P
                for m in range(MT):
                    n = c * per_h + e * MT + m
                    if not (first and e * MT + m < 2):
                        pe.wait_ge(s_gelu, n - 1)
                    for kt in range(KT):
                        mm = pe.matmul(p_h[bank_h(c, e * MT + m)][:, 0:cols], w1[:, e, kt, m * P:(m + 1) * P],
                                       y_t[:, kt, bass.ds(c * (CH * P), cols)], start=(kt == 0), stop=(kt == KT - 1))
                    mm.then_inc(s_h, 1)

            def product(c, e, size, first):
                pe.wait_ge(s_gelu, c * per_h + (e + 1) * MT)
                for j in range(size):
                    n = c * per_o + e * size + j
                    if not (first and e * size + j < 2):
                        pe.wait_ge(s_acc, n - 1)
                    for m in range(MT):
                        mm = pe.matmul(p_o[bank_o(c, e * size + j)][:, 0:D], hid[:, e % 2, m, j * P:(j + 1) * P], w2[:, e, m, :],
                                       start=(m == 0), stop=(m == MT - 1))
                    mm.then_inc(s_o, 1)

            def chunk(c, size, first):
                hidden(c, 0, size, first)
                for e in range(1, E):
                    hidden(c, e, size, first)
                    product(c, e - 1, size, first)
                product(c, E - 1, size, first)

            run(pe, chunk)

        @block.scalar
        def _(act):
            act.wait_ge(s_in, 16 * (E + 3))

            def chunk(c, size, first):
                for e in range(E):
                    if not (first and e < 2):
                        done = c * per_o + (e - 1) * size
                        act.wait_ge(s_o, done)
                    for m in range(MT):
                        act.wait_ge(s_h, c * per_h + e * MT + m + 1)
                        nc.scalar.activation(hid[:, e % 2, m, 0:size * P], p_h[bank_h(c, e * MT + m)][:, 0:size * P], ACT.Gelu,
                                             bias=b1[:, e, m:m + 1]).then_inc(s_gelu, 1)

            run(act, chunk)

        @block.vector
        def _(dve):
            dve.wait_ge(s_in, 16 * (E + 3))
            with dve.Fori(0, tiles) as n:
                for e in range(E):
                    x = nodes.x[:, bass.ds(n, 1), :].rearrange("p o c -> p (o c)")
                    nc.vector.scalar_tensor_tensor(x, b2[:, e, :], gate[:, bass.ds(n, 1), e], x, ALU.mult, ALU.add).then_inc(s_bias, 1)
                    dve.wait_ge(s_bias, n * E + (e + 1))

            def chunk(c, size, first):
                for e in range(E):
                    for j in range(size):
                        n = c * per_o + e * size + j
                        if e > 0:
                            dve.wait_ge(s_acc, n - size + 1)
                        dve.wait_ge(s_o, n + 1)
                        x = nodes.x[:, bass.ds(c * CH + j, 1), :].rearrange("p o c -> p (o c)")
                        nc.vector.scalar_tensor_tensor(x, p_o[bank_o(c, e * size + j)][:, 0:D], gate[:, bass.ds(c * CH + j, 1), e], x,
                                                       ALU.mult, ALU.add).then_inc(s_acc, 1)

            run(dve, chunk)
GNN = ("Wk", "bk", "Wq", "bq", "Wv", "bv", "Wa", "ba", "rel_att", "rel_msg", "rel_pri", "skip")
MIX = ("Wqkv", "Wout", "bout")
FFN = ("W_gat", "att_src", "att_dst", "b_gat", "ln_gamma", "ln_beta", "W1", "b1", "W2", "b2", "edge_index")
NAMES = ["x", "src", "dst"] + [f"L0_gnn_{n}" for n in GNN] + [f"L0_mix_{n}" for n in MIX] + [f"L0_ffn_{n}" for n in FFN]


def stage_of(nc, stage, *given):
    with nc.cleanup_on_exit():
        stage(nc, *given)
    nc.all_engine_barrier()


def build(nc, args, out):
    x, src, dst = (args[n] for n in ("x", "src", "dst"))
    w = {n: args[f"L0_gnn_{n}"] for n in GNN} | {n: args[f"L0_mix_{n}"] for n in MIX}
    f = {n: args[f"L0_ffn_{n}"] for n in FFN}
    N, D = x.shape
    H = w["rel_pri"].shape[0]
    DK = D // H
    FH, FE = f["att_src"].shape
    step = 2 * GRP * P
    batches = [-(-n // step) * 2 * GRP for n in (dst.shape[0], f["edge_index"].shape[1])]
    dram = lambda n, s, d=F32: nc.dram_tensor(n, s, d, kind="Internal").ap()
    tiles = -(-N // P)
    src_t, dst_t = dram("kv_table", [tiles * P, 2 * D]), dram("q_table", [tiles * P, D])
    fsrc_t, fdst_t = dram("gat_src_table", [tiles * P, FH * FE + FH]), dram("gat_dst_table", [tiles * P, FH])
    with ExitStack() as ctx:
        consts = Consts(nc, ctx)
        nodes = Nodes(nc, ctx, N, D)
        stage_of(nc, load_nodes, nodes, x)
        stage_of(nc, layer_norm_stats, "ln1", nodes)
        stage_of(nc, project, consts, nodes, w, src_t, dst_t)

        def edge_sums(stage, name, s, d, T, heads, width, s_table, d_table, node_values):
            pairs, rows = dram(f"{name}_pairs", [T * P, 2], I32), dram(f"{name}_dst_rows", [T, P])
            partial = dram(f"{name}_partial", [T * P + 1, heads * (width + 2)])
            counts = stage.enter_context(nc.sbuf_tensor(f"{name}_counts", [P, HIS], F32))
            ends = stage.enter_context(nc.sbuf_tensor(f"{name}_ends", [P, HIS], F32))
            last = stage.enter_context(nc.sbuf_tensor(f"{name}_last", [P, -(-T // P)], F32))
            stage_of(nc, sort_edges, f"{name}s", consts, s, d, T, N, pairs, rows, counts, ends, name == "a")
            with ExitStack() as own:
                lists = EdgeLists(nc, own, name, T, heads, last)
                stage_of(nc, read_sorted, f"{name}r", consts, lists, pairs, N)
                spread = None
                if node_values is not None:
                    spread = own.enter_context(nc.sbuf_tensor(f"{name}_spread", [P, T, heads], F32))
                    stage_of(nc, spread_over_runs, f"{name}p", consts, nodes, lists, counts, ends, node_values, d_table, spread)
                stage_of(nc, edge_pass, f"{name}e", consts, lists, s_table, d_table, width, partial, spread)
            cols = heads * (width + 2)
            b, e = (stage.enter_context(nc.sbuf_tensor(f"{name}_{n}", [P, tiles, cols], F32)) for n in ("before", "at_end"))
            stage_of(nc, gather_sums, f"{name}c", consts, nodes, lists, partial, counts, ends, heads, width, b, e)
            return b, e

        with ExitStack() as stage:
            b, e = edge_sums(stage, "a", src, dst, batches[0], H, DK, src_t, dst_t, None)
            stage_of(nc, first_residual, consts, nodes, b, e, H, DK)
        stage_of(nc, layer_norm_stats, "ln2", nodes)
        with ExitStack() as stage:
            y_t = stage.enter_context(nc.sbuf_tensor("y_t", [P, D // P, tiles * P], F32))
            feats = stage.enter_context(nc.sbuf_tensor("feats", [P, tiles, FH * FE + 2 * FH], F32))
            gate = stage.enter_context(nc.sbuf_tensor("gate", [P, tiles, FE], F32))
            stage_of(nc, gat_inputs, consts, nodes, f, y_t, feats, fsrc_t, fdst_t)
            with ExitStack() as inner:
                b, e = edge_sums(inner, "f", f["edge_index"][0, :], f["edge_index"][1, :], batches[1], FH, FE, fsrc_t, fdst_t,
                                 feats[:, :, FH * FE + FH:FH * FE + 2 * FH])
                stage_of(nc, gates, nodes, f, feats, b, e, gate)
            stage_of(nc, experts, nodes, f, y_t, gate, out)


def kernel(**inputs):
    import numpy as _np
    import concourse.bacc as _bacc
    from concourse import mybir as _mybir
    from concourse.bass_utils import run_bass_kernel_spmd as _run

    nc = _bacc.Bacc("TRN2", target_bir_lowering=False, num_devices=1)
    arrays, args = {}, {}
    for name in NAMES:
        a = _np.ascontiguousarray(inputs[name])
        if a.ndim == 0:
            a = a.reshape(1)
        arrays[f"in_{name}_dram"] = a
        args[name] = nc.dram_tensor(f"in_{name}_dram", a.shape, _mybir.dt.from_np(a.dtype), kind="ExternalInput").ap()
    out = nc.dram_tensor("out_0_dram", inputs["x"].shape, _mybir.dt.float32, kind="ExternalOutput").ap()
    build(nc, args, out)
    r = _run(nc, [arrays], core_ids=[0])
    return r.results[0]["out_0_dram"]
```

```python
from contextlib import ExitStack

import concourse.bass as bass
from concourse import mybir

ALU = mybir.AluOpType
ACT = mybir.ActivationFunctionType
AX = mybir.AxisListType
F32 = mybir.dt.float32
BF16 = mybir.dt.bfloat16
I32 = mybir.dt.int32
BANK = 512


class Consts:

    def __init__(self, nc, ctx):
        sb = lambda n, s, d: ctx.enter_context(nc.sbuf_tensor(n, s, d))
        self.ident = sb("ident", [P, P], F32)
        self.ident_b = sb("ident_b", [P, P], BF16)
        self.upto = sb("upto", [P, P], F32)
        self.ones = sb("ones", [P, P], F32)
        self.after = sb("after", [P, P], F32)
        self.lane_b = sb("lane_b", [P, P], BF16)
        self.lane_c = sb("lane_c", [P, 1], F32)
        lane_i = sb("lane_i", [P, P], I32)
        lane_ci = sb("lane_ci", [P, 1], I32)
        with ExitStack() as own:
            s_base = nc.alloc_semaphore("consts_base")
            s_made = nc.alloc_semaphore("consts_made")
            block = own.enter_context(nc.Block())

            @block.gpsimd
            def _(pool):
                pool.iota(lane_i[:, :], pattern=[[1, P]], base=0, channel_multiplier=0).then_inc(s_base, 1)
                pool.iota(lane_ci[:, :], pattern=[[0, 1]], base=0, channel_multiplier=1).then_inc(s_base, 1)
                pool.memset(self.ident[:, :], 0.0).then_inc(s_base, 1)
                pool.memset(self.upto[:, :], 1.0).then_inc(s_base, 1)
                pool.memset(self.after[:, :], 1.0).then_inc(s_base, 1)
                pool.wait_ge(s_base, 5)
                pool.affine_select(out=self.ident[:, :], in_=self.ident[:, :], compare_op=ALU.not_equal, fill=1.0,
                                   base=0, pattern=[[-1, P]], channel_multiplier=1).then_inc(s_made, 1)
                pool.affine_select(out=self.upto[:, :], in_=self.upto[:, :], compare_op=ALU.is_ge, fill=0.0,
                                   base=0, pattern=[[1, P]], channel_multiplier=-1).then_inc(s_made, 1)
                pool.affine_select(out=self.after[:, :], in_=self.after[:, :], compare_op=ALU.is_gt, fill=0.0,
                                   base=0, pattern=[[-1, P]], channel_multiplier=1).then_inc(s_made, 1)

            @block.vector
            def _(dve):
                nc.vector.memset(self.ones[:, :], 1.0)
                dve.wait_ge(s_made, 3)
                nc.vector.tensor_copy(self.ident_b[:, :], self.ident[:, :])
                nc.vector.tensor_copy(self.lane_b[:, :], lane_i[:, :])
                nc.vector.tensor_copy(self.lane_c[:, :], lane_ci[:, :])


P = 128
GRP = 8
HIS = 64
HOLE = P * HIS - 1


class Steps:

    def __init__(self, eng, sem):
        self.eng, self.sem, self.n, self.base = eng, sem, 0, 0

    def link(self, ins):
        ins.then_inc(self.sem, 1)
        self.n += 1
        self.eng.wait_ge(self.sem, self.base + self.n)

    def loop(self, i, start, per):
        self.base, self.n, self.kept = (i - start) * per + self.n, 0, self.n
        self.per = per

    def loop_end(self, passes):
        assert self.n == self.per, (self.n, self.per)
        self.base, self.n = 0, self.kept + passes * self.per


def spans(total, size):
    return [(a, min(size, total - a)) for a in range(0, total, size)]


def sort_step(c, k, each):
    return c * (each // 2) + k // 2, k % 2, min(k, 2) if isinstance(c, int) and c == 0 else 2


def after_step(i, b, early):
    return (i, 1, min(early + 1, 2)) if b == 0 else (i + 1, 0, 2)


def before_step(i, b, early):
    return (i - 1, 1, 1 if isinstance(i, int) and i == 1 else 2) if b == 0 else (i, 0, 0 if early == 1 else 2)


def loop_steps(eng, groups, step, tiles=0, tile=None, parts=0, steps=None, per_step=0, per_tile=0, in_pass=4):
    if tiles:
        passes = (tiles - 1) // in_pass
        each = (groups - 1) // passes // 2 * 2
    else:
        in_pass, each = 0, 2
        passes = (groups - 1) // 2

    def spread(c, k, slots, n_tiles, t0):
        def extra(half):
            s, n = 2 * k + half, n_tiles * parts
            for f in range(s * n // slots, (s + 1) * n // slots):
                t = t0 + f // parts
                first = isinstance(c, int) and c == 0 and t < 2
                tile(c * (in_pass // 2) + t // 2, t % 2, first, f % parts)
        return extra

    def one_pass(c):
        for k in range(each):
            step(*sort_step(c, k, each), False, spread(c, k, 2 * each, in_pass, 0))

    one_pass(0)
    with eng.Fori(1, passes) as c:
        if steps:
            steps.loop(c, 1, per_step * each + per_tile * in_pass)
        one_pass(c)
        if steps:
            steps.loop_end(passes - 1)
    left, left_tiles = groups - passes * each, tiles - passes * in_pass
    for k in range(left):
        step(*sort_step(passes, k, each), k == left - 1, spread(passes, k, 2 * left, left_tiles, 0))


class EdgeSort:

    def __init__(self, nc, ctx, name, consts, src, dst, batches, nodes, pairs_out, dst_rows, counts, ends, often_sorted=False):
        self.nc, self.name, self.consts, self.src, self.dst, self.batches, self.nodes = nc, name, consts, src, dst, batches, nodes
        self.pairs_out, self.dst_rows, self.counts, self.ends, self.often_sorted = pairs_out, dst_rows, counts, ends, often_sorted
        self.tiles = spans(batches, P)
        self.groups = batches // GRP
        assert self.groups % 2 == 0
        sb = lambda n, s, d: ctx.enter_context(nc.sbuf_tensor(f"{name}_{n}", s, d))
        self.pairs = sb("pairs", [P, batches, 2], I32)
        self.dst_c = sb("dst_c", [P, batches], F32)
        self.lo_c = sb("lo_c", [P, batches], BF16)
        self.hi_c = sb("hi_c", [P, batches], BF16)
        self.one_lo = sb("one_lo", [P, 2, GRP, P], BF16)
        self.one_hi = sb("one_hi", [P, 2, GRP, HIS], BF16)
        self.table = sb("table", [P, 2, (GRP + 1) * HIS], F32)
        self.unsorted = sb("unsorted", [P, 1], I32) if often_sorted else None
        self.pair_rows = sb("pair_rows", [P, len(self.tiles), P, 2], I32) if often_sorted else None

    def onehots(self, g, b, done):
        t0 = g * GRP
        V = self.nc.vector
        V.tensor_tensor(self.one_lo[:, b, :, :], self.consts.lane_b[:, 0:P].unsqueeze(1).broadcast_to([P, GRP, P]),
                        self.lo_c[:, bass.ds(t0, GRP)].unsqueeze(2).broadcast_to([P, GRP, P]), ALU.is_equal)
        V.tensor_tensor(self.one_hi[:, b, :, :], self.consts.lane_b[:, 0:HIS].unsqueeze(1).broadcast_to([P, GRP, HIS]),
                        self.hi_c[:, bass.ds(t0, GRP)].unsqueeze(2).broadcast_to([P, GRP, HIS]), ALU.is_equal).then_inc(done, 1)

    def count(self):
        nc, name, consts, src, dst, batches, nodes = self.nc, self.name, self.consts, self.src, self.dst, self.batches, self.nodes
        tiles, groups, often_sorted, dst_rows = self.tiles, self.groups, self.often_sorted, self.dst_rows
        pairs, dst_c, lo_c, hi_c, one_lo, one_hi = self.pairs, self.dst_c, self.lo_c, self.hi_c, self.one_lo, self.one_hi
        edges = dst.shape[0]
        with ExitStack() as ctx:
            sb = lambda n, s, d: ctx.enter_context(nc.sbuf_tensor(f"{name}_{n}", s, d))
            ps = lambda n, s, d: ctx.enter_context(nc.psum_tensor(f"{name}_{n}", s, d))
            sem = lambda n: nc.alloc_semaphore(f"{name}_c_{n}")
            nt = len(tiles)
            raw = sb("raw", [P, 2, nt, P], I32)
            rawf = sb("rawf", [P, 2, nt, P], F32)
            part_i = sb("part_i", [P, 2, batches], I32)
            sums = sb("sums", [P, 3, HIS], F32)
            total = sb("total", [P, HIS], F32)
            zero = sb("zero", [P, HIS], F32)
            ps_rows = [ps(f"ps_rows{b}", [P, BANK], F32) for b in range(2)]
            ps_cnt = ps("ps_cnt", [P, BANK], F32)
            ps_off = ps("ps_off", [P, BANK], F32)

            s_pad, s_in, s_float, s_rows = sem("padded"), sem("lists_in"), sem("as_float"), sem("rows_out")
            s_turned, s_taken = sem("turned"), sem("taken")
            s_own = sem("vector_steps")
            s_onehot, s_counted = sem("onehot"), sem("counted")
            s_tot, s_off = sem("totals"), sem("offsets")
            s_pad_flat = sem("flat_padded")
            s_flat, s_cmp, s_bad = sem("flat_in"), sem("compared"), sem("disorder")
            n_turns = 2 * nt
            if often_sorted:
                lines = max(k for k in range(1, P + 1) if edges % k == 0)
                per = edges // lines
                flat = sb("flat", [lines, per + 1], I32)
                less = sb("less", [lines, per], F32)
                falls = sb("falls", [lines, 1], F32)

            full, rest = edges // P, edges % P
            nfull = full // P
            loads = []
            for a, arr in enumerate((src, dst)):
                if nfull:
                    loads.append((raw[:, a, 0:nfull, :], arr[0:nfull * P * P].rearrange("(i p e) -> p i e", p=P, e=P)))
                if full > nfull * P:
                    k = full - nfull * P
                    loads.append((raw[0:k, a, nfull, :], arr[nfull * P * P:full * P].rearrange("(p e) -> p e", e=P)))
                if rest:
                    loads.append((raw[full - nfull * P:full - nfull * P + 1, a, nfull, 0:rest],
                                  arr[full * P:edges].rearrange("(p e) -> p e", p=1)))
            block = ctx.enter_context(nc.Block())

            @block.sync
            def _(sp):
                if nfull < nt:
                    sp.wait_ge(s_pad, 1)
                for on_chip, in_dram in loads:
                    sp.dma_start(on_chip, in_dram).then_inc(s_in, 16)
                if often_sorted:
                    sp.wait_ge(s_pad_flat, 1)
                    sp.dma_start(flat[:, 0:per], dst.rearrange("(q e) -> q e", e=per)).then_inc(s_flat, 16)
                    sp.dma_start(flat[0:lines - 1, per:per + 1], dst.rearrange("(q e) -> q e", e=per)[1:lines, 0:1],
                                 allow_slow_non_contiguous=True).then_inc(s_flat, 16)
                sp.wait_ge(s_float, 1)
                for i, (t0, k) in enumerate(tiles):
                    sp.dma_start(dst_rows[t0:t0 + k, :], rawf[0:k, 1, i, :]).then_inc(s_rows, 16)
                sp.wait_ge(s_rows, 16 * nt)

            @block.tensor
            def _(pe):
                pe.wait_ge(s_float, 1)
                n = 0
                for a in range(2):
                    for i, (t0, k) in enumerate(tiles):
                        if n >= 2:
                            pe.wait_ge(s_taken, n - 1)
                        pe.transpose(ps_rows[n % 2][:, 0:k], rawf[0:k, a, i, :], consts.ident[0:k, 0:k]).then_inc(s_turned, 1)
                        n += 1

                def count(i, b, first):
                    g = 2 * i + b
                    pe.wait_ge(s_onehot, g + 1)
                    for j in range(GRP):
                        mm = pe.matmul(ps_cnt[:, 0:HIS], one_lo[:, b, j, :], one_hi[:, b, j, :],
                                       start=(first and b == 0 and j == 0), stop=False, skip_group_check=True)
                    mm.then_inc(s_counted, 1)

                for b in range(2):
                    count(0, b, True)
                with pe.Fori(1, groups // 2) as i:
                    for b in range(2):
                        count(i, b, False)
                pe.wait_ge(s_tot, 1)
                pe.matmul(ps_off[:, 0:HIS], consts.upto[:, :], total[:, :], start=True, stop=True)
                pe.matmul(ps_off[:, HIS:2 * HIS], consts.ones[:, :], total[:, :], start=True, stop=True).then_inc(s_off, 1)
                if often_sorted:
                    pe.wait_ge(s_cmp, 1)
                    pe.matmul(ps_cnt[:, 0:1], consts.ones[0:lines, :], falls[:, :], start=True, stop=True).then_inc(s_bad, 1)

            @block.vector
            def _(dve):
                own = Steps(dve, s_own)
                if nfull < nt:
                    own.link(nc.vector.memset(raw[:, 0, nt - 1, :], 0))
                    nc.vector.memset(raw[:, 1, nt - 1, :], HOLE).then_inc(s_pad, 1)
                if often_sorted:
                    nc.vector.memset(flat[:, per:per + 1], HOLE).then_inc(s_pad_flat, 1)
                own.link(nc.vector.memset(zero[:, :], 0.0))
                dve.wait_ge(s_in, 16 * len(loads))
                k_last = tiles[-1][1]
                if k_last < P and nt > 1:
                    nc.vector.tensor_copy(rawf[:, :, 0:nt - 1, :], raw[:, :, 0:nt - 1, :])
                    nc.vector.tensor_copy(rawf[0:k_last, :, nt - 1, :], raw[0:k_last, :, nt - 1, :]).then_inc(s_float, 1)
                else:
                    nc.vector.tensor_copy(rawf[:, :, :, :], raw[:, :, :, :]).then_inc(s_float, 1)
                if often_sorted:
                    dve.wait_ge(s_float, 1)
                    for i, (t0, k) in enumerate(tiles):
                        nc.vector.tensor_copy(self.pair_rows[0:k, i, :, 1], raw[0:k, 1, i, :])
                        nc.vector.tensor_scalar(self.pair_rows[0:k, i, :, 0], rawf[0:k, 0, i, :], float(nodes - 1), None, ALU.min)
                    dve.wait_ge(s_flat, 32)
                    own.link(nc.vector.tensor_tensor(less[:, :], flat[:, 1:per + 1], flat[:, 0:per], ALU.is_lt))
                    nc.vector.tensor_reduce(falls[:, :], less[:, :], AX.X, ALU.add).then_inc(s_cmp, 1)
                n = 0
                for a in range(2):
                    for i, (t0, k) in enumerate(tiles):
                        dve.wait_ge(s_turned, n + 1)
                        if a == 0:
                            nc.vector.tensor_scalar(pairs[:, t0:t0 + k, 0], ps_rows[n % 2][:, 0:k], float(nodes - 1), None,
                                                    ALU.min).then_inc(s_taken, 1)
                        else:
                            nc.vector.tensor_copy(dst_c[:, t0:t0 + k], ps_rows[n % 2][:, 0:k])
                            nc.vector.tensor_copy(pairs[:, t0:t0 + k, 1], ps_rows[n % 2][:, 0:k]).then_inc(s_taken, 1)
                        n += 1
                dve.wait_ge(s_taken, n_turns)
                nc.vector.tensor_scalar(part_i[:, 0, :], pairs[:, :, 1], P - 1, None, ALU.bitwise_and)
                own.link(nc.vector.tensor_scalar(part_i[:, 1, :], pairs[:, :, 1], 7, None, ALU.logical_shift_right))
                nc.vector.tensor_copy(lo_c[:, :], part_i[:, 0, :])
                own.link(nc.vector.tensor_copy(hi_c[:, :], part_i[:, 1, :]))

                for b in range(2):
                    self.onehots(b, b, s_onehot)
                with dve.Fori(1, groups // 2) as i:
                    for b in range(2):
                        dve.wait_ge(s_counted, 2 * i + b - 1)
                        self.onehots(2 * i + b, b, s_onehot)
                dve.wait_ge(s_counted, groups)
                nc.vector.tensor_copy(total[:, :], ps_cnt[:, 0:HIS]).then_inc(s_tot, 1)
                dve.wait_ge(s_tot, 1)
                nc.vector.tensor_copy(self.counts[:, :], total[:, :])
                dve.wait_ge(s_off, 1)
                own.link(nc.vector.tensor_copy(sums[:, 0, :], ps_off[:, HIS:2 * HIS]))
                own.link(nc.vector.tensor_tensor_scan(sums[:, 1, :], sums[:, 0, :], zero[:, :], 0.0, ALU.add, ALU.add))
                own.link(nc.vector.tensor_tensor(sums[:, 2, :], sums[:, 1, :], sums[:, 0, :], ALU.subtract))
                own.link(nc.vector.tensor_tensor(self.ends[:, :], ps_off[:, 0:HIS], sums[:, 2, :], ALU.add))
                own.link(nc.vector.tensor_tensor(self.table[:, 0, 0:HIS], self.ends[:, :], self.counts[:, :], ALU.subtract))
                if often_sorted:
                    dve.wait_ge(s_bad, 1)
                    nc.vector.tensor_copy(self.unsorted[:, :], ps_cnt[:, 0:1])

    def prepare(self, ctx):
        nc, name = self.nc, self.name
        sb = lambda n, s, d: ctx.enter_context(nc.sbuf_tensor(f"{name}_{n}", s, d))
        ps = lambda n, s, d: ctx.enter_context(nc.psum_tensor(f"{name}_{n}", s, d))
        sem = lambda n: nc.alloc_semaphore(f"{name}_{n}")
        self.lo_t = sb("lo_t", [P, GRP * P], F32)
        self.rows = sb("rows", [P, 2, GRP * P], F32)
        self.scrap = sb("scrap", [P, GRP, P], F32)
        self.rank = sb("rank", [P, 2, GRP], F32)
        self.looked = sb("looked", [P, GRP, HIS], F32)
        self.found = sb("found", [P, GRP], F32)
        self.slot = sb("slot", [P, 2, GRP], I32)
        self.pair_ring = sb("pair_ring", [P, 2, GRP, 2], I32)
        self.ps_t = ps("ps_t", [P, GRP * P], BF16)
        self.ps_pre = ps("ps_pre", [P, GRP * HIS], F32)
        self.ps_look = ps("ps_look", [P, GRP * HIS], F32)
        self.s_row = [sem(f"row_in{b}") for b in range(2)]
        self.s_onehot, self.s_rank, self.s_olt, self.s_pre, self.s_tab, self.s_look, self.s_mul = (
            sem(n) for n in ("onehot", "ranked", "onehot_t", "prefix", "table", "looked_up", "look_read"))
        self.s_slot, self.s_ring = sem("slots"), sem("pairs_in_ring")
        self.s_scat = [sem(f"scattered{b}") for b in range(2)]


    def sync_start(self, sp):
        self.rows_in(sp, 0, 0, 0)

    def rows_in(self, sp, i, b, early):
        if early == 2:
            sp.wait_ge(self.s_rank, 2 * i + b - 1)
        sp.dma_start(self.rows[:, b, :], self.dst_rows[bass.ds((2 * i + b) * GRP, GRP), :]
                     .rearrange("(o t) e -> o (t e)", o=1).broadcast_to([P, GRP * P])).then_inc(self.s_row[b], 16)

    def sync_step(self, sp, i, b, early, last, extra):
        extra(0)
        if not last:
            self.rows_in(sp, *after_step(i, b, early))
        extra(1)

    def tensor_step(self, pe, i, b, early, last, extra):
        g = 2 * i + b
        extra(0)
        pe.wait_ge(self.s_onehot, g + 1)
        if early:
            pe.wait_ge(self.s_tab, g)
        for j in range(GRP):
            pe.transpose(self.ps_t[:, j * P:(j + 1) * P], self.one_lo[:, b, j, :], self.consts.ident_b[:, :])
        for j in range(GRP):
            mm = pe.matmul(self.ps_pre[:, j * HIS:], self.one_lo[:, b, j, :],
                           self.one_hi[:, b, j:j + 1, :].broadcast_to([P, GRP - j, HIS]),
                           start=(j == 0), stop=(j == GRP - 1), skip_group_check=True)
        mm.then_inc(self.s_pre, 1)
        extra(1)
        pe.wait_ge(self.s_olt, g + 1)
        pe.wait_ge(self.s_tab, g + 1)
        if early:
            pe.wait_ge(self.s_mul, g)
        for j in range(GRP):
            mm = pe.matmul(self.ps_look[:, j * HIS:(j + 1) * HIS], self.lo_t[:, j * P:(j + 1) * P],
                           self.table[:, b, j * HIS:(j + 1) * HIS], start=True, stop=True)
        mm.then_inc(self.s_look, 1)

    def scalar_step(self, act, i, b, early, last, extra):
        extra(0)
        act.wait_ge(self.s_pre, 2 * i + b + 1)
        self.nc.scalar.copy(self.lo_t[:, :], self.ps_t[:, :]).then_inc(self.s_olt, 1)
        extra(1)

    def edges_in(self, dve, i, b, early):
        g = 2 * i + b
        if early == 2:
            dve.wait_ge(self.s_pre, g - 1)
        self.onehots(g, b, self.s_onehot)
        dve.wait_ge(self.s_row[b], 16 * i + 16)
        for j in range(GRP):
            rk = self.nc.vector.scalar_tensor_tensor(self.scrap[:, j, :], self.rows[:, b, j * P:(j + 1) * P],
                                                     self.dst_c[:, bass.ds(g * GRP + j, 1)], self.consts.after[:, :],
                                                     ALU.is_equal, ALU.mult, accum_out=self.rank[:, b, j:j + 1])
        rk.then_inc(self.s_rank, 1)

    def slots_out(self, dve, own, i, b, early):
        g = 2 * i + b
        V = self.nc.vector
        dve.wait_ge(self.s_look, g + 1)
        V.tensor_tensor(self.looked[:, :, :], self.ps_look[:, :].rearrange("p (j h) -> p j h", h=HIS),
                        self.one_hi[:, b, :, :], ALU.mult).then_inc(self.s_mul, 1)
        dve.wait_ge(self.s_mul, g + 1)
        own.link(V.tensor_reduce(self.found[:, :], self.looked[:, :, :], AX.X, ALU.add))
        if early == 2:
            dve.wait_ge(self.s_scat[b], 16 * GRP * i)
        V.tensor_tensor(self.slot[:, b, :], self.found[:, :], self.rank[:, b, :], ALU.add).then_inc(self.s_slot, 1)

    def vector_step(self, dve, own, i, b, early, last, extra):
        g = 2 * i + b
        V = self.nc.vector
        if early:
            self.slots_out(dve, own, *before_step(i, b, early))
        extra(0)
        if early:
            dve.wait_ge(self.s_tab, g)
        dve.wait_ge(self.s_pre, g + 1)
        own.link(V.tensor_tensor(self.table[:, b, HIS:], self.ps_pre[:, :].rearrange("p (j h) -> p j h", h=HIS),
                                 self.table[:, b, 0:HIS].unsqueeze(1).broadcast_to([P, GRP, HIS]), ALU.add))
        V.tensor_copy(self.table[:, 1 - b, 0:HIS], self.table[:, b, GRP * HIS:]).then_inc(self.s_tab, 1)
        if not last:
            self.edges_in(dve, *after_step(i, b, early))
        extra(1)

    PER_STEP = 2

    def vector_end(self, dve, own):
        self.slots_out(dve, own, self.groups // 2 - 1, 1, 2)

    def pairs_in(self, pool, i, b, early):
        if early == 2:
            pool.wait_ge(self.s_scat[b], 16 * GRP * i)
        pool.tensor_copy(self.pair_ring[:, b, :, :], self.pairs[:, bass.ds((2 * i + b) * GRP, GRP), :]).then_inc(self.s_ring, 1)

    def pool_step(self, pool, i, b, early, last, extra):
        g = 2 * i + b
        if early == 0:
            self.pairs_in(pool, i, b, early)
        pool.wait_ge(self.s_ring, g + 1)
        pool.nop(nofuse=True)
        pool.wait_ge(self.s_slot, g + 1)
        pool.nop(nofuse=True)
        for j in range(GRP):
            if j == GRP // 2 and not last:
                self.pairs_in(pool, *after_step(i, b, early))
            pool.indirect_dma_start(self.pairs_out[:, :], bass.IndirectOffsetOnAxis(ap=self.slot[:, b, j:j + 1], axis=0),
                                    self.pair_ring[:, b, j, :], None).then_inc(self.s_scat[b], 16)

    def pool_end(self, pool):
        for b in range(2):
            pool.wait_ge(self.s_scat[b], 16 * GRP * (self.groups // 2))

    def place(self):
        nc = self.nc
        with ExitStack() as ctx:
            self.prepare(ctx)
            s_own, s_same = nc.alloc_semaphore(f"{self.name}_place_steps"), nc.alloc_semaphore(f"{self.name}_copied")
            block = ctx.enter_context(nc.Block())

            def either(eng, place, copy=None):
                if not self.often_sorted:
                    place()
                    return
                flag = eng.value_load(self.unsorted[0:1, 0:1])
                with eng.If(flag):
                    place()
                if copy is not None:
                    with eng.Else():
                        copy()

            @block.sync
            def _(sp):
                def place():
                    self.sync_start(sp)
                    loop_steps(sp, self.groups, lambda *a: self.sync_step(sp, *a))

                def copy():
                    for i, (t0, k) in enumerate(self.tiles):
                        sp.dma_start(self.pairs_out[t0 * P:(t0 + k) * P, :].rearrange("(p e) c -> p e c", e=P),
                                     self.pair_rows[0:k, i, :, :]).then_inc(s_same, 16)
                    sp.wait_ge(s_same, 16 * len(self.tiles))

                either(sp, place, copy)

            @block.tensor
            def _(pe):
                either(pe, lambda: loop_steps(pe, self.groups, lambda *a: self.tensor_step(pe, *a)))

            @block.scalar
            def _(act):
                either(act, lambda: loop_steps(act, self.groups, lambda *a: self.scalar_step(act, *a)))

            @block.vector
            def _(dve):
                own = Steps(dve, s_own)

                def place():
                    self.edges_in(dve, 0, 0, 0)
                    loop_steps(dve, self.groups, lambda *a: self.vector_step(dve, own, *a), steps=own, per_step=self.PER_STEP)
                    self.vector_end(dve, own)

                either(dve, place)

            @block.gpsimd
            def _(pool):
                def place():
                    loop_steps(pool, self.groups, lambda *a: self.pool_step(pool, *a))
                    self.pool_end(pool)

                either(pool, place)
FAR = 1.0e30


def group_loop(eng, count, body, steps=None, per=0):
    for b in range(2):
        body(0, b, True)
    with eng.Fori(1, count // 2) as i:
        if steps:
            steps.loop(i, 1, per)
        for b in range(2):
            body(i, b, False)
        if steps:
            steps.loop_end(count // 2 - 1)
    if count % 2:
        body(count // 2, 0, False)


def loop_beside(eng, groups, body, beside, steps=None, per=0):
    if beside is None:
        group_loop(eng, groups, lambda i, b, first: body(i, b, first, lambda part: None), steps, per)
        return
    each = beside.groups_per_pass

    for k in range(each):
        body(k // 2, k % 2, k < 2, lambda part: beside.slice(eng, 0, k, part))
    with eng.Fori(1, beside.passes) as c:
        if steps:
            steps.loop(c, 1, per * each // 2)
        for k in range(each):
            body(c * (each // 2) + k // 2, k % 2, False, lambda part: beside.slice(eng, c, k, part))
        if steps:
            steps.loop_end(beside.passes - 1)
    done = beside.passes * each // 2
    with eng.Fori(done, groups // 2) as i:
        if steps:
            steps.loop(i, done, per)
        for b in range(2):
            body(i, b, False, lambda part: None)
        if steps:
            steps.loop_end(groups // 2 - done)


def one_before(i, b):
    return (i, 0, isinstance(i, int) and i == 0) if b else (i - 1, 1, isinstance(i, int) and i == 1)


def lagged_loop(eng, count, front, back, lag=1):
    def both(i, b):
        front(i, b, isinstance(i, int) and i == 0)
        if lag == 2 and not (isinstance(i, int) and i == 0):
            back(i - 1, b, isinstance(i, int) and i == 1)
        if lag == 1 and not (isinstance(i, int) and i == 0 and b == 0):
            back(*one_before(i, b))

    for n in range(4):
        both(n // 2, n % 2)
    with eng.Fori(2, count // 2) as i:
        for b in range(2):
            both(i, b)
    if count % 2:
        both(count // 2, 0)
    for n in range(count - lag, count):
        back(n // 2, n % 2, False)


class EdgeLists:

    def __init__(self, nc, ctx, name, batches, heads, last, gathered):
        self.batches, self.heads = batches, heads
        self.src_c = ctx.enter_context(nc.sbuf_tensor(f"{name}_src_c", [P, batches + GRP], I32))
        self.dst_c = ctx.enter_context(nc.sbuf_tensor(f"{name}_dst_c", [P, batches], F32))
        self.node_c = None
        if gathered:
            self.node_c = ctx.enter_context(nc.sbuf_tensor(f"{name}_node_c", [P, batches + GRP], I32))
            self.window = ctx.enter_context(nc.sbuf_tensor(f"{name}_window", [P, batches // GRP], F32))
            self.window_i = ctx.enter_context(nc.sbuf_tensor(f"{name}_window_i", [P, batches // GRP], I32))
            self.wide = ctx.enter_context(nc.sbuf_tensor(f"{name}_wide", [P, 1], I32))
        self.last = last
        self.rows = nc.dram_tensor(f"{name}_sorted_rows", [batches, P], F32, kind="Internal").ap()
        self.cuts = nc.dram_tensor(f"{name}_cuts", [batches, heads, 2 * P], F32, kind="Internal").ap()


def read_sorted(nc, name, consts, lists, pairs, nodes):
    batches, heads = lists.batches, lists.heads
    tiles = spans(batches, P)
    nt = len(tiles)
    with ExitStack() as ctx:
        sb = lambda n, s, d: ctx.enter_context(nc.sbuf_tensor(f"{name}_{n}", s, d))
        sem = lambda n: nc.alloc_semaphore(f"{name}_{n}")
        raw = sb("sorted", [P, nt, P, 2], I32)
        val = sb("sorted_f", [P, 2, nt, P], F32)
        cut = sb("cut", [P, nt, 2, P], F32)
        bank = [ctx.enter_context(nc.psum_tensor(f"{name}_turn{b}", [P, BANK], F32)) for b in range(2)]
        s_in, s_val, s_cut, s_out = sem("sorted_in"), sem("sorted_float"), sem("cuts"), sem("rows_out")
        s_turned, s_taken, s_own = sem("turned"), sem("taken"), sem("vector_steps")
        if lists.node_c is not None:
            groups = batches // GRP
            first_lane = sb("first_lane", [P, P], F32)
            base = sb("base", [P, groups], F32)
            far = sb("far", [P, batches], F32)
            far_sum = sb("far_sum", [P, 1], F32)
            s_base, s_far, s_wide = sem("window_base"), sem("far_edges"), sem("far_sum")
        block = ctx.enter_context(nc.Block())

        @block.sync
        def _(sp):
            for i, (t0, k) in enumerate(tiles):
                sp.dma_start(raw[0:k, i, :, :], pairs[t0 * P:(t0 + k) * P, :].rearrange("(p e) c -> p e c", e=P)).then_inc(s_in, 16)
            sp.wait_ge(s_val, nt)
            for i, (t0, k) in enumerate(tiles):
                sp.dma_start(lists.rows[t0:t0 + k, :], val[0:k, 1, i, :]).then_inc(s_out, 16)
            sp.wait_ge(s_cut, nt)
            for i, (t0, k) in enumerate(tiles):
                sp.dma_start(lists.cuts[t0:t0 + k, :, :],
                             cut[0:k, i, :, :].rearrange("p a e -> p (a e)").unsqueeze(1).broadcast_to([k, heads, 2 * P]))\
                    .then_inc(s_out, 16)
            sp.wait_ge(s_out, 16 * 2 * nt)

        @block.tensor
        def _(pe):
            pe.wait_ge(s_val, nt)
            n = 0
            for a in range(2):
                for i, (t0, k) in enumerate(tiles):
                    if n >= 2:
                        pe.wait_ge(s_taken, n - 1)
                    pe.transpose(bank[n % 2][:, 0:k], val[0:k, a, i, :], consts.ident[0:k, 0:k]).then_inc(s_turned, 1)
                    n += 1
            if lists.node_c is not None:
                pe.wait_ge(s_taken, n)
                pe.matmul(bank[0][:, 0:groups], first_lane[:, :], lists.dst_c[:, :].rearrange("p (g t) -> p g t", t=GRP)[:, :, 0],
                          start=True, stop=True).then_inc(s_base, 1)
                pe.wait_ge(s_far, 1)
                pe.matmul(bank[1][:, 0:1], consts.ones[:, :], far_sum[:, :], start=True, stop=True).then_inc(s_wide, 1)

        @block.vector
        def _(dve):
            own = Steps(dve, s_own)
            nc.vector.memset(lists.last[:, :], -1.0)
            nc.vector.memset(lists.src_c[:, batches:], 0)
            if lists.node_c is not None:
                nc.vector.memset(lists.node_c[:, batches:], 0)
                own.link(nc.vector.memset(first_lane[:, :], 0.0))
                own.link(nc.vector.memset(first_lane[0:1, :], 1.0))
            own.link(nc.vector.memset(cut[:, :, :, :], -FAR))
            dve.wait_ge(s_in, 16 * nt)
            for i, (t0, k) in enumerate(tiles):
                nc.vector.tensor_copy(val[0:k, 0, i, :], raw[0:k, i, :, 0])
                nc.vector.tensor_copy(val[0:k, 1, i, :], raw[0:k, i, :, 1]).then_inc(s_val, 1)
            dve.wait_ge(s_val, nt)
            for i, (t0, k) in enumerate(tiles):
                d = val[0:k, 1, i, :]
                nc.vector.tensor_copy(lists.last[0:k, i:i + 1], d[:, P - 1:P])
                nc.vector.tensor_tensor(cut[0:k, i, 0, 1:P], d[:, 1:P], d[:, 0:P - 1], ALU.not_equal)
                own.link(nc.vector.tensor_tensor(cut[0:k, i, 1, 0:P - 1], d[:, 1:P], d[:, 0:P - 1], ALU.not_equal))
                nc.vector.tensor_scalar(cut[0:k, i, 0, 1:P], cut[0:k, i, 0, 1:P], -FAR, None, ALU.mult)
                nc.vector.tensor_scalar(cut[0:k, i, 1, 0:P - 1], cut[0:k, i, 1, 0:P - 1], -FAR, None, ALU.mult).then_inc(s_cut, 1)
            n = 0
            for a in range(2):
                for i, (t0, k) in enumerate(tiles):
                    dve.wait_ge(s_turned, n + 1)
                    if a == 0:
                        nc.vector.tensor_copy(lists.src_c[:, t0:t0 + k], bank[n % 2][:, 0:k]).then_inc(s_taken, 1)
                    else:
                        if lists.node_c is not None:
                            nc.vector.tensor_scalar(lists.node_c[:, t0:t0 + k], bank[n % 2][:, 0:k], float(nodes - 1), None, ALU.min)
                        nc.vector.tensor_copy(lists.dst_c[:, t0:t0 + k], bank[n % 2][:, 0:k]).then_inc(s_taken, 1)
                    n += 1
            if lists.node_c is not None:
                dve.wait_ge(s_taken, n)
                nc.vector.tensor_copy(far[:, :], lists.node_c[:, 0:batches])
                dve.wait_ge(s_base, 1)
                own.link(nc.vector.tensor_scalar(base[:, :], bank[0][:, 0:groups], float(nodes - 1), None, ALU.min))
                own.link(nc.vector.tensor_scalar(lists.window[:, :], base[:, :], consts.lane_c[:, :], None, ALU.add))
                nc.vector.tensor_scalar(lists.window_i[:, :], lists.window[:, :], float(nodes - 1), None, ALU.min)
                far_g = far[:, :].rearrange("p (g t) -> p g t", t=GRP)
                own.link(nc.vector.tensor_tensor(far_g, far_g, base[:, :].unsqueeze(2).broadcast_to([P, groups, GRP]), ALU.subtract))
                own.link(nc.vector.tensor_scalar(far[:, :], far[:, :], P - 0.5, None, ALU.is_gt))
                nc.vector.tensor_reduce(far_sum[:, :], far[:, :], AX.X, ALU.add).then_inc(s_far, 1)
                dve.wait_ge(s_wide, 1)
                nc.vector.tensor_copy(lists.wide[:, :], bank[1][:, 0:1])


def edge_pass(nc, name, consts, lists, src_table, dst_table, width, partial, spread=None, beside=None):
    batches, heads = lists.batches, lists.heads
    groups = batches // GRP
    s_cols = src_table.shape[1]
    vals = heads * width
    dot = spread is None
    per_batch = 2 if dot else 1
    lag = beside is not None
    val0 = s_cols - vals if dot else 0
    sums = heads * (width + 1)
    cols = sums + heads
    gh = GRP * heads
    per_bank = 1 if sums * 2 > BANK else GRP
    n_banks = 2 if per_bank == 1 else 1
    with ExitStack() as ctx:
        sb = lambda n, s, d: ctx.enter_context(nc.sbuf_tensor(f"{name}_{n}", s, d))
        ps = lambda n: ctx.enter_context(nc.psum_tensor(f"{name}_{n}", [P, BANK], F32))
        sem = lambda n: nc.alloc_semaphore(f"{name}_{n}")
        ring = sb("index_ring", [P, 2, 2, GRP], I32)
        s_row = sb("src_rows", [P, 2, GRP, s_cols], F32)
        d_row = sb("dst_rows", [P, 2, GRP, vals], F32) if dot else None
        q_win = sb("query_window", [P, 2, vals], F32) if dot else None
        pick = sb("pick", [P, GRP, P], F32) if dot else None
        rows = sb("rows", [P, 2, GRP, P], F32)
        same = sb("same", [P, 2, GRP, P], F32) if dot else rows
        cuts = sb("cuts", [gh, 2, 2, P], F32)
        prod = sb("prod", [P, GRP, vals], F32)
        score = sb("score", [P, 2, gh], F32)
        up = sb("up", [gh, P], F32)
        top = sb("top", [gh, 2, P], F32)
        rel = sb("rel", [gh, 2, P], F32)
        ex = sb("ex", [gh, 2, P], F32)
        kept = sb("kept_values", [P, 2, GRP, vals], F32) if lag else None
        msg = sb("msg", [P, 2, GRP, heads, width + 1], F32)
        out = sb("out", [P, 2, GRP, cols], F32)
        p_turn = ps("p_turn")
        p_back = ps("p_back")
        p_max = ps("p_max")
        p_sum = [ps(f"p_sum{k}") for k in range(n_banks)]
        per_q = BANK // vals if dot else 1
        p_q = [ps(f"p_query{k}") for k in range(2)] if dot else None
        s_pick, s_q, s_qr = sem("picks"), sem("queries"), sem("queries_used")
        s_win = [sem(f"window_in{b}") for b in range(2)]
        s_ring = sem("ring")
        s_got = [sem(f"gathered{b}") for b in range(2)]
        s_list = [sem(f"rows_in{b}") for b in range(2)]
        s_own = sem("vector_steps")
        s_score, s_turn, s_rel, s_ex, s_back, s_msg, s_same = (
            sem("scores"), sem("scores_turned"), sem("scores_less_max"),
            sem("exps"), sem("turned_back"), sem("messages"), sem("same_run"))
        s_sum, s_kept, s_max = sem("sums"), sem("sums_kept"), sem("maxima_kept")
        s_out = [sem(f"stored{b}") for b in range(2)]
        if beside is not None:
            beside.semaphores()
        half = groups // 2
        sums_per_group = GRP // per_bank
        part_v = partial[0:P * batches, :].rearrange("(p t) c -> p t c", t=batches)

        def p_sum_of(b, j):
            return p_sum[j % 2]

        def either(eng, wide, narrow):
            if not dot:
                wide()
                return
            flag = eng.value_load(lists.wide[0:1, 0:1])
            with eng.If(flag):
                wide()
            with eng.Else():
                narrow()

        block = ctx.enter_context(nc.Block())

        @block.gpsimd
        def _(pool):
            def gather_narrow(i, b, first):
                g = 2 * i + b
                if not first:
                    pool.wait_ge(s_got[b], 16 * GRP * i)
                    pool.wait_ge(s_win[b], 16 * i)
                pool.tensor_copy(ring[:, b, 1, 0:1], lists.window_i[:, bass.ds(g, 1)])
                pool.tensor_copy(ring[:, b, 0, :], lists.src_c[:, bass.ds(g * GRP, GRP)]).then_inc(s_ring, 1)
                pool.wait_ge(s_ring, g + 1)
                pool.nop(nofuse=True)
                if not first:
                    pool.wait_ge(s_msg, g - 1)
                    pool.nop(nofuse=True)
                pool.indirect_dma_start(q_win[:, b, :], None, dst_table[:, :],
                                        bass.IndirectOffsetOnAxis(ap=ring[:, b, 1, 0:1], axis=0)).then_inc(s_win[b], 16)
                for j in range(GRP):
                    pool.indirect_dma_start(s_row[:, b, j, :], None, src_table[:, :],
                                            bass.IndirectOffsetOnAxis(ap=ring[:, b, 0, j:j + 1], axis=0)).then_inc(s_got[b], 16)

            def indices(i, b):
                if not (isinstance(i, int) and i == 0):
                    pool.wait_ge(s_got[b], 16 * per_batch * GRP * i)
                if dot:
                    pool.tensor_copy(ring[:, b, 1, :], lists.node_c[:, bass.ds((2 * i + b) * GRP, GRP)])
                pool.tensor_copy(ring[:, b, 0, :], lists.src_c[:, bass.ds((2 * i + b) * GRP, GRP)]).then_inc(s_ring, 1)

            def gather(i, b, first):
                g = 2 * i + b
                if first and b == 0:
                    indices(0, 0)
                pool.wait_ge(s_ring, g + 1)
                pool.nop(nofuse=True)
                if not first:
                    pool.wait_ge(s_score if lag else s_msg, g - 1)
                    pool.nop(nofuse=True)
                for j in range(GRP):
                    if j == GRP // 2:
                        indices(i, 1) if b == 0 else indices(i + 1, 0)
                    if dot:
                        pool.indirect_dma_start(d_row[:, b, j, :], None, dst_table[:, :],
                                                bass.IndirectOffsetOnAxis(ap=ring[:, b, 1, j:j + 1], axis=0)).then_inc(s_got[b], 16)
                    pool.indirect_dma_start(s_row[:, b, j, :], None, src_table[:, :],
                                            bass.IndirectOffsetOnAxis(ap=ring[:, b, 0, j:j + 1], axis=0)).then_inc(s_got[b], 16)

            either(pool, lambda: group_loop(pool, groups, gather), lambda: group_loop(pool, groups, gather_narrow))

        @block.sync
        def _(sp):
            def load(i, b, first):
                g = 2 * i + b
                if not first and dot:
                    sp.wait_ge(s_same, g - 1)
                    sp.wait_ge(s_rel, g - 1)
                    sp.nop(nofuse=True)
                elif not first:
                    sp.wait_ge(s_sum, (g - 1) * sums_per_group)
                sp.dma_start(rows[:, b, :, :].rearrange("p t e -> p (t e)"),
                             lists.rows[bass.ds(g * GRP, GRP), :].rearrange("(o t) e -> o (t e)", o=1)
                             .broadcast_to([P, GRP * P])).then_inc(s_list[b], 16)
                sp.dma_start(cuts[:, b, :, :].rearrange("p a e -> p (a e)"),
                             lists.cuts[bass.ds(g * GRP, GRP), :, :].rearrange("t h e -> (t h) e")).then_inc(s_list[b], 16)

            def store(i, b):
                g = 2 * i + b
                sp.wait_ge(s_kept, (g + 1) * sums_per_group)
                sp.wait_ge(s_max, g + 1)
                sp.dma_start(part_v[:, bass.ds(g * GRP, GRP), :], out[:, b, :, :]).then_inc(s_out[b], 16)

            def group(i, b, first, extra):
                if dot:
                    load(i, b, first)
                if not first:
                    store(i - 1, b)
                if not dot:
                    load(i, b, first)
                extra(0)
                extra(1)

            loop_beside(sp, groups, group, beside)
            for b in range(2):
                store(half - 1, b)
            if lag:
                beside.rest(sp)
            for b in range(2):
                sp.wait_ge(s_out[b], 16 * half)

        @block.vector
        def _(dve):
            own = Steps(dve, s_own)

            def scores(i, b, first):
                g = 2 * i + b
                dve.wait_ge(s_got[b], 16 * per_batch * GRP * (i + 1))
                if lag:
                    nc.vector.tensor_copy(kept[:, b, :, :], s_row[:, b, :, val0:val0 + vals])
                if dot:
                    own.link(nc.vector.tensor_tensor(prod[:, :, :], s_row[:, b, :, 0:vals], d_row[:, b, :, :], ALU.mult))
                    nc.vector.tensor_reduce(score[:, b, :], prod[:, :, :].rearrange("p t (h w) -> p (t h) w", w=width),
                                            AX.X, ALU.add).then_inc(s_score, 1)
                else:
                    raw = prod[:, :, 0:heads]
                    own.link(nc.vector.tensor_tensor(raw, s_row[:, b, :, vals:s_cols], spread[:, bass.ds(g * GRP, GRP), :], ALU.add))
                    nc.vector.scalar_tensor_tensor(score[:, b, :].rearrange("p (t h) -> p t h", h=heads), raw, 0.2, raw,
                                                   ALU.mult, ALU.max).then_inc(s_score, 1)
                dve.wait_ge(s_list[b], 32 * (i + 1))
                if dot and not first:
                    dve.wait_ge(s_sum, (g - 1) * sums_per_group)
                nc.vector.tensor_tensor(same[:, b, :, :], rows[:, b, :, :],
                                        lists.dst_c[:, bass.ds(g * GRP, GRP)].unsqueeze(2).broadcast_to([P, GRP, P]),
                                        ALU.is_equal).then_inc(s_same, 1)

            def scores_narrow(i, b, first):
                g = 2 * i + b
                dve.wait_ge(s_got[b], 16 * GRP * (i + 1))
                if not (first and b == 0):
                    dve.wait_ge(s_score, g)
                for u in range(GRP // per_q):
                    js = slice(u * per_q, (u + 1) * per_q)
                    dve.wait_ge(s_q, g * (GRP // per_q) + u + 1)
                    nc.vector.tensor_tensor(prod[:, js, :], s_row[:, b, js, 0:vals],
                                            p_q[u % 2][:, :].rearrange("p (t c) -> p t c", c=vals), ALU.mult).then_inc(s_qr, 1)
                dve.wait_ge(s_qr, (g + 1) * (GRP // per_q))
                nc.vector.tensor_reduce(score[:, b, :], prod[:, :, :].rearrange("p t (h w) -> p (t h) w", w=width),
                                        AX.X, ALU.add).then_inc(s_score, 1)

            def picks(i, b, first):
                g = 2 * i + b
                dve.wait_ge(s_list[b], 32 * (i + 1))
                nc.vector.tensor_scalar(pick[:, :, :], rows[:, b, :, :], lists.window[:, bass.ds(g, 1)], None, ALU.is_equal)\
                    .then_inc(s_pick, 1)

            def same_run(i, b, first):
                g = 2 * i + b
                if not first:
                    dve.wait_ge(s_sum, (g - 1) * sums_per_group)
                nc.vector.tensor_tensor(same[:, b, :, :], rows[:, b, :, :],
                                        lists.dst_c[:, bass.ds(g * GRP, GRP)].unsqueeze(2).broadcast_to([P, GRP, P]),
                                        ALU.is_equal).then_inc(s_same, 1)

            def maxima(own, i, b):
                g = 2 * i + b
                dve.wait_ge(s_turn, g + 1)
                own.link(nc.vector.tensor_tensor_scan(up[:, :], cuts[:, b, 0, :], p_turn[0:gh, 0:P], 0.0, ALU.add, ALU.max))
                own.link(nc.vector.tensor_tensor_scan(top[:, b, ::-1], cuts[:, b, 1, ::-1], up[:, ::-1], 0.0, ALU.add, ALU.max))
                nc.vector.tensor_tensor(rel[:, b, :], p_turn[0:gh, 0:P], top[:, b, :], ALU.subtract).then_inc(s_rel, 1)

            def messages(i, b):
                g = 2 * i + b
                dve.wait_ge(s_back, g + 1)
                e = p_back[:, 0:gh].rearrange("p (t h) -> p t h", h=heads)
                nc.vector.tensor_copy(msg[:, b, :, :, width], e)
                nc.vector.tensor_tensor(msg[:, b, :, :, 0:width],
                                        (kept[:, b, :, :] if lag else s_row[:, b, :, val0:val0 + vals]).rearrange("p t (h w) -> p t h w", w=width),
                                        e.unsqueeze(3).broadcast_to([P, GRP, heads, width]), ALU.mult).then_inc(s_msg, 1)

            def group(i, b, first, extra):
                scores(i, b, first)
                if not lag:
                    maxima(own, i, b)
                    messages(i, b)
                    return
                if not (first and b == 0):
                    messages(*one_before(i, b)[0:2])
                maxima(own, i, b)
                extra(0)
                extra(1)

            def narrow():
                own = Steps(dve, s_own)

                def group(i, b, first):
                    picks(i, b, first)
                    if not (first and b == 0):
                        messages(*one_before(i, b)[0:2])
                    scores_narrow(i, b, first)
                    maxima(own, i, b)
                    same_run(i, b, first)

                group_loop(dve, groups, group, own, 4)
                messages(half - 1, 1)

            either(dve, lambda: loop_beside(dve, groups, group, beside, own, 6), narrow)
            if lag:
                messages(half - 1, 1)
                beside.rest(dve)

        @block.scalar
        def _(act):
            def exps(i, b, first):
                g = 2 * i + b
                act.wait_ge(s_rel, g + 1)
                if not first:
                    act.wait_ge(s_back, g - 1)
                nc.scalar.activation(ex[:, b, :], rel[:, b, :], ACT.Exp).then_inc(s_ex, 1)

            def keep_max(i, b, first):
                g = 2 * i + b
                act.wait_ge(s_back, g + 1)
                if not first:
                    act.wait_ge(s_out[b], 16 * i)
                nc.scalar.copy(out[:, b, :, sums:cols], p_max[:, 0:gh].rearrange("p (t h) -> p t h", h=heads)).then_inc(s_max, 1)

            def keep_sums(i, b, js=range(sums_per_group)):
                g = 2 * i + b
                for j in js:
                    act.wait_ge(s_sum, g * sums_per_group + j + 1)
                    if per_bank == 1:
                        nc.scalar.copy(out[:, b, j, 0:sums], p_sum_of(b, j)[:, 0:sums]).then_inc(s_kept, 1)
                    else:
                        nc.scalar.copy(out[:, b, :, 0:sums], p_sum[0][:, 0:GRP * sums].rearrange("p (t c) -> p t c", c=sums))\
                            .then_inc(s_kept, 1)

            def group(i, b, first, extra):
                if not lag:
                    exps(i, b, first)
                    keep_max(i, b, first)
                    keep_sums(i, b)
                    return
                started = not (first and b == 0)
                if started:
                    keep_max(*one_before(i, b))
                extra(0)
                if started:
                    keep_sums(*one_before(i, b)[0:2])
                extra(1)
                exps(i, b, first)

            def narrow():
                def group(i, b, first):
                    started = not (first and b == 0)
                    if started:
                        keep_sums(*one_before(i, b)[0:2], range(5))
                    exps(i, b, first)
                    if started:
                        keep_sums(*one_before(i, b)[0:2], range(5, GRP))
                    keep_max(i, b, first)

                group_loop(act, groups, group)
                keep_sums(half - 1, 1)

            either(act, lambda: loop_beside(act, groups, group, beside), narrow)
            if lag:
                keep_max(half - 1, 1, False)
                keep_sums(half - 1, 1)
                beside.rest(act)

        @block.tensor
        def _(pe):
            def turn(i, b, first):
                g = 2 * i + b
                pe.wait_ge(s_score, g + 1)
                if not (first and b == 0):
                    pe.wait_ge(s_rel, g)
                pe.nop(nofuse=True)
                pe.transpose(p_turn[0:gh, 0:P], score[:, b, :], consts.ident[:, :]).then_inc(s_turn, 1)

            def turn_back(i, b, first):
                g = 2 * i + b
                pe.wait_ge(s_ex, g + 1)
                if not (first and b == 0):
                    pe.wait_ge(s_msg, g)
                    pe.wait_ge(s_max, g)
                pe.nop(nofuse=True)
                pe.transpose(p_back[:, 0:gh], ex[:, b, :], consts.ident[0:gh, 0:gh])
                pe.transpose(p_max[:, 0:gh], top[:, b, :], consts.ident[0:gh, 0:gh]).then_inc(s_back, 1)

            def sum_up(i, b, first, js=range(GRP)):
                g = 2 * i + b
                if js[0] == 0:
                    pe.wait_ge(s_same, g + 1)
                    pe.wait_ge(s_msg, g + 1)
                if per_bank == 1:
                    for j in js:
                        if not (first and b == 0 and j < 2):
                            pe.wait_ge(s_kept, g * GRP + j - 1)
                        pe.matmul(p_sum_of(b, j)[:, 0:sums], same[:, b, j, :],
                                  msg[:, b, j, :, :].rearrange("p h w -> p (h w)"), start=True, stop=True).then_inc(s_sum, 1)
                else:
                    if not (first and b == 0):
                        pe.wait_ge(s_kept, g)
                    for j in range(GRP):
                        mm = pe.matmul(p_sum[0][:, j * sums:(j + 1) * sums], same[:, b, j, :],
                                       msg[:, b, j, :, :].rearrange("p h w -> p (h w)"), start=True, stop=True)
                    mm.then_inc(s_sum, 1)

            def group(i, b, first, extra):
                turn(i, b, first)
                if not lag:
                    turn_back(i, b, first)
                    sum_up(i, b, first)
                    return
                started = not (first and b == 0)
                if started:
                    turn_back(*one_before(i, b))
                extra(0)
                if started:
                    sum_up(*one_before(i, b))
                extra(1)

            def queries(i, b, first):
                g = 2 * i + b
                units = GRP // per_q
                pe.wait_ge(s_win[b], 16 * (i + 1))
                pe.wait_ge(s_pick, g + 1)
                for u in range(units):
                    if not (first and b == 0 and u < 2):
                        pe.wait_ge(s_qr, g * units + u - 1)
                    for k in range(per_q):
                        mm = pe.matmul(p_q[u % 2][:, k * vals:(k + 1) * vals], pick[:, u * per_q + k, :], q_win[:, b, :],
                                       start=True, stop=True)
                    mm.then_inc(s_q, 1)

            def narrow():
                def group(i, b, first):
                    started = not (first and b == 0)
                    queries(i, b, first)
                    if started:
                        sum_up(*one_before(i, b), range(3))
                    turn(i, b, first)
                    if started:
                        sum_up(*one_before(i, b), range(3, 6))
                    turn_back(i, b, first)
                    if started:
                        sum_up(*one_before(i, b), range(6, GRP))

                group_loop(pe, groups, group)
                sum_up(half - 1, 1, False)

            either(pe, lambda: loop_beside(pe, groups, group, beside), narrow)
            if lag:
                turn_back(half - 1, 1, False)
                sum_up(half - 1, 1, False)
                beside.rest(pe)
def spread_over_runs(nc, name, consts, nodes, lists, counts, ends, values, table, spread):
    H = values.shape[2]
    T = lists.batches
    C = P // H
    L = T // C
    tiles = nodes.tiles
    starts = nc.dram_tensor(f"{name}_starts", [P * T + P, H], F32, kind="Internal").ap()
    with ExitStack() as ctx:
        sb = lambda n, s, d=F32: ctx.enter_context(nc.sbuf_tensor(f"{name}_{n}", s, d))
        sem = lambda n: nc.alloc_semaphore(f"{name}_{n}")
        run = sb("run", [P, L * P])
        hold = sb("hold", [P, L * P])
        first_at = sb("first_at", [P, L * P])
        edge = sb("edge", [P, 4, tiles])
        edge_i = sb("edge_i", [P, 3, tiles], I32)
        by_chunk = sb("by_chunk", [P, 2, BANK])
        ring = sb("ring", [P, 2, 1], I32)
        val_ring = sb("val_ring", [P, 2, H])
        head = sb("head", [C, 1])
        head_i = sb("head_i", [C, 1], I32)
        head_v = sb("head_v", [C, H])
        begin = sb("begin", [P, 1])
        bank = [ctx.enter_context(nc.psum_tensor(f"{name}_bank{b}", [P, BANK], F32)) for b in range(2)]
        (s_run, s_head, s_zero, s_cleared, s_idx, s_ring, s_hi, s_hv, s_begin, s_in, s_own, s_perm, s_t, s_k, s_fill, s_t2, s_k2) = (
            sem(n) for n in ("run_in", "head_in", "zero", "cleared", "indices", "ring", "head_index", "head_value", "begin",
                             "starts_in", "steps", "by_chunk", "turned", "taken", "filled", "turned_back", "taken_back"))
        s_sc = [sem(f"scattered{b}") for b in range(2)]
        quads = BANK // P
        passes = L // quads
        block = ctx.enter_context(nc.Block())

        @block.sync
        def _(sp):
            for h in range(H):
                sp.dma_start(run[h * C:(h + 1) * C, :], lists.rows.rearrange("(c l) e -> c (l e)", c=C)).then_inc(s_run, 16)
            sp.dma_start(head[:, :], lists.rows.rearrange("(c l) e -> c (l e)", c=C)[:, 0:1],
                         allow_slow_non_contiguous=True).then_inc(s_head, 16)
            sp.wait_ge(s_zero, 1)
            sp.dma_start(starts[0:P * T, :].rearrange("(p t) h -> p (t h)", p=P), hold[:, :]).then_inc(s_cleared, 16)
            sp.wait_ge(s_hv, 16)
            for h in range(H):
                sp.dma_start(begin[h * C:(h + 1) * C, :], head_v[:, h:h + 1]).then_inc(s_begin, 16)
            for b in range(2):
                sp.wait_ge(s_sc[b], 16 * ((tiles + 1 - b) // 2))
            sp.dma_start(spread[:, :, :], starts[0:P * T, :].rearrange("(p t) h -> p t h", p=P)).then_inc(s_in, 16)

        @block.gpsimd
        def _(pool):
            pool.wait_ge(s_hi, 1)
            pool.indirect_dma_start(head_v[:, :], None, table[:, :], bass.IndirectOffsetOnAxis(ap=head_i[:, :], axis=0)).then_inc(s_hv, 16)
            pool.wait_ge(s_idx, 1)
            pool.wait_ge(s_cleared, 16)

            def scatter(i, b, first):
                n = 2 * i + b
                if not first:
                    pool.wait_ge(s_sc[b], 16 * i)
                pool.tensor_copy(val_ring[:, b, :], values[:, bass.ds(n, 1), :].rearrange("p o h -> p (o h)"))
                pool.tensor_copy(ring[:, b, :], edge_i[:, 0, bass.ds(n, 1)]).then_inc(s_ring, 1)
                pool.wait_ge(s_ring, n + 1)
                pool.nop(nofuse=True)
                pool.indirect_dma_start(starts[:, :], bass.IndirectOffsetOnAxis(ap=ring[:, b, :], axis=0), val_ring[:, b, :], None)\
                    .then_inc(s_sc[b], 16)

            group_loop(pool, tiles, scatter)

        @block.tensor
        def _(pe):
            for q in range(passes):
                pe.wait_ge(s_perm, q + 1)
                if q >= 2:
                    pe.wait_ge(s_k, q - 1)
                for j in range(quads):
                    mm = pe.transpose(bank[q % 2][:, j * P:(j + 1) * P], by_chunk[:, q % 2, j * P:(j + 1) * P], consts.ident[:, :])
                mm.then_inc(s_t, 1)
            pe.wait_ge(s_fill, 1)
            for q in range(passes):
                if q >= 2:
                    pe.wait_ge(s_k2, q - 1)
                for j in range(quads):
                    l = q * quads + j
                    mm = pe.transpose(bank[q % 2][:, j * P:(j + 1) * P], run[:, l * P:(l + 1) * P], consts.ident[:, :])
                mm.then_inc(s_t2, 1)

        @block.vector
        def _(dve):
            own = Steps(dve, s_own)
            V = nc.vector
            V.memset(hold[:, :], 0.0).then_inc(s_zero, 1)
            dve.wait_ge(s_head, 16)
            own.link(V.tensor_scalar(head[:, :], head[:, :], float(nodes.count - 1), None, ALU.min))
            V.tensor_copy(head_i[:, :], head[:, :]).then_inc(s_hi, 1)
            own.link(V.tensor_tensor(edge[:, 0, :], ends[:, 0:tiles], counts[:, 0:tiles], ALU.subtract))
            own.link(V.tensor_copy(edge_i[:, 0, :], edge[:, 0, :]))
            V.tensor_scalar(edge_i[:, 1, :], edge_i[:, 0, :], P - 1, None, ALU.bitwise_and)
            own.link(V.tensor_scalar(edge_i[:, 2, :], edge_i[:, 0, :], 7, None, ALU.logical_shift_right))
            V.tensor_copy(edge[:, 0, :], edge_i[:, 1, :])
            V.tensor_copy(edge[:, 1, :], edge_i[:, 2, :])
            own.link(V.tensor_scalar(edge[:, 2, :], counts[:, 0:tiles], 0.0, None, ALU.is_equal))
            own.link(V.scalar_tensor_tensor(edge[:, 1, :], edge[:, 0, :], float(T), edge[:, 1, :], ALU.mult, ALU.add))
            own.link(V.tensor_scalar(edge[:, 3, :], edge[:, 1, :], -1.0, float(P * T), ALU.mult, ALU.add))
            own.link(V.tensor_scalar(edge[:, 3, :], edge[:, 3, :], consts.lane_c[:, :], None, ALU.add))
            own.link(V.tensor_tensor(edge[:, 3, :], edge[:, 3, :], edge[:, 2, :], ALU.mult))
            V.tensor_tensor(edge_i[:, 0, :], edge[:, 1, :], edge[:, 3, :], ALU.add).then_inc(s_idx, 1)
            dve.wait_ge(s_run, 16 * H)
            dve.wait_ge(s_cleared, 16)
            V.memset(hold[:, 0:1], 1.0)
            own.link(V.tensor_tensor(hold[:, 1:], run[:, 1:], run[:, 0:L * P - 1], ALU.is_equal))
            back = spread[:, :, :].rearrange("p (c l) h -> p l h c", c=C)
            dve.wait_ge(s_in, 16)
            for q in range(passes + 1):
                if q < passes:
                    if q >= 2:
                        dve.wait_ge(s_t, q - 1)
                    V.tensor_copy(by_chunk[:, q % 2, :].rearrange("p (l h c) -> p l h c", l=quads, h=H),
                                  back[:, q * quads:(q + 1) * quads]).then_inc(s_perm, 1)
                if q == 0:
                    continue
                q -= 1
                dve.wait_ge(s_t, q + 1)
                V.tensor_copy(first_at[:, q * BANK:(q + 1) * BANK], bank[q % 2][:, :]).then_inc(s_k, 1)
            dve.wait_ge(s_k, passes)
            own.link(V.memset(first_at[:, 0:1], 0.0))
            dve.wait_ge(s_begin, 16 * H)
            V.tensor_tensor_scan(run[:, :], hold[:, :], first_at[:, :], begin[:, :], ALU.mult, ALU.add).then_inc(s_fill, 1)
            for q in range(passes):
                dve.wait_ge(s_t2, q + 1)
                V.tensor_copy(back[:, q * quads:(q + 1) * quads], bank[q % 2][:, :].rearrange("p (l h c) -> p l h c", l=quads, h=H))\
                    .then_inc(s_k2, 1)


def turn_all(nc, name, ctx, jobs, ident, ready, taken):
    bank = [ctx.enter_context(nc.psum_tensor(f"{name}_turn{b}", [P, BANK], F32)) for b in range(2)]

    def tensor_part(pe):
        for n, (_, in_) in enumerate(jobs):
            if n >= 2:
                pe.wait_ge(taken, n - 1)
            k = in_.shape[0]
            pe.transpose(bank[n % 2][0:in_.shape[1], 0:k], in_, ident[0:k, 0:k]).then_inc(ready, 1)

    def vector_part(dve):
        for n, (out, in_) in enumerate(jobs):
            dve.wait_ge(ready, n + 1)
            nc.vector.tensor_copy(out, bank[n % 2][0:in_.shape[1], 0:in_.shape[0]]).then_inc(taken, 1)
        dve.wait_ge(taken, len(jobs))

    return tensor_part, vector_part


class Nodes:

    def __init__(self, nc, ctx, nodes, dim):
        self.count, self.dim, self.tiles = nodes, dim, -(-nodes // P)
        sb = lambda n, s: ctx.enter_context(nc.sbuf_tensor(n, s, F32))
        self.x = sb("x", [P, self.tiles, dim])
        self.mean_var = sb("mean_var", [P, self.tiles, 2])
        self.rstd = sb("rstd", [P, self.tiles])
        self.gx = sb("gx", [P, dim // P, dim])
        self.wa_t = sb("wa_t", [P, dim // P, dim])
        self.bias = sb("bias", [P, dim])
        self.eps = sb("eps", [P, 1])


def on_all(row, n):
    return row.rearrange("(o n) -> o n", o=1).broadcast_to([P, n])


def layer_norm_stats(nc, name, nodes, LN_EPS=1e-5):
    with ExitStack() as ctx:
        parts = ctx.enter_context(nc.sbuf_tensor(f"{name}_parts", [P, nodes.tiles, 6], F32))
        root = ctx.enter_context(nc.sbuf_tensor(f"{name}_root", [P, nodes.tiles], F32))
        half = ctx.enter_context(nc.sbuf_tensor(f"{name}_half", [P, nodes.tiles], F32))
        s_parts, s_stats, s_root, s_own = (nc.alloc_semaphore(f"{name}_{n}") for n in ("parts", "stats", "root", "steps"))
        block = ctx.enter_context(nc.Block())

        @block.vector
        def _(dve):
            nc.vector.memset(nodes.eps[:, :], LN_EPS)
            each = 8

            def stats(n):
                nc.vector.bn_stats(parts[:, bass.ds(n, 1), :].rearrange("p o c -> p (o c)"),
                                   nodes.x[:, bass.ds(n, 1), :].rearrange("p o c -> p (o c)")).then_inc(s_parts, 1)

            with dve.Fori(0, nodes.tiles // each) as i:
                for k in range(each):
                    stats(i * each + k)
            for n in range(nodes.tiles // each * each, nodes.tiles):
                stats(n)
            dve.wait_ge(s_parts, nodes.tiles)
            own = Steps(dve, s_own)
            V = nc.vector
            mean, var = nodes.mean_var[:, :, 0], nodes.mean_var[:, :, 1]
            own.link(V.tensor_tensor(half[:, :], parts[:, :, 1], parts[:, :, 4], ALU.subtract))
            own.link(V.tensor_tensor(var, half[:, :], half[:, :], ALU.mult))
            own.link(V.tensor_tensor(half[:, :], parts[:, :, 2], parts[:, :, 5], ALU.add))
            own.link(V.tensor_scalar(var, var, 0.25, None, ALU.mult))
            own.link(V.tensor_scalar(half[:, :], half[:, :], 1.0 / nodes.dim, None, ALU.mult))
            own.link(V.tensor_tensor(var, var, half[:, :], ALU.add))
            own.link(V.tensor_tensor(mean, parts[:, :, 1], parts[:, :, 4], ALU.add))
            V.tensor_scalar(mean, mean, 0.5, None, ALU.mult).then_inc(s_stats, 1)
            dve.wait_ge(s_root, 1)
            nc.vector.reciprocal(nodes.rstd[:, :], root[:, :])

        @block.scalar
        def _(act):
            act.wait_ge(s_stats, 1)
            nc.scalar.activation(root[:, :], nodes.mean_var[:, :, 1], ACT.Sqrt, bias=nodes.eps[:, :]).then_inc(s_root, 1)


def normalised(nc, nodes, out, n):
    return nc.vector.tensor_scalar(out, nodes.x[:, bass.ds(n, 1), :].rearrange("p o c -> p (o c)"),
                                   nodes.mean_var[:, bass.ds(n, 1), 0], nodes.rstd[:, bass.ds(n, 1)],
                                   ALU.subtract, ALU.mult)


def load_nodes(nc, nodes, x):
    full = nodes.count // P
    rest = nodes.count - full * P
    with ExitStack() as ctx:
        s_in, s_pad = nc.alloc_semaphore("x_in"), nc.alloc_semaphore("x_pad")
        block = ctx.enter_context(nc.Block())

        @block.sync
        def _(sp):
            sp.dma_start(nodes.x[:, 0:full, :], x[0:full * P, :].rearrange("(i p) c -> p i c", p=P)).then_inc(s_in, 16)
            if rest:
                sp.wait_ge(s_pad, 1)
                sp.dma_start(nodes.x[0:rest, full, :], x[full * P:nodes.count, :]).then_inc(s_in, 16)
            sp.wait_ge(s_in, 16 * (2 if rest else 1))

        @block.vector
        def _(dve):
            nc.vector.memset(nodes.x[:, nodes.tiles - 1, :], 0.0).then_inc(s_pad, 1)


def project(nc, consts, nodes, w, src_table, dst_table, sort):
    D, tiles = nodes.dim, nodes.tiles
    KT = D // P
    H = w["rel_pri"].shape[0]
    DK = D // H
    INNER = w["Wout"].shape[1]
    DH = 64
    MH = INNER // DH
    PAIRS = INNER // P
    KV, MK = 2 * D, 3 * D
    MV = MK + INNER
    COLS = MV + INNER
    with ExitStack() as ctx:
        sb = lambda n, s: ctx.enter_context(nc.sbuf_tensor(f"p_{n}", s, F32))
        w_all = sb("w_all", [P, KT, COLS])
        bias = sb("bias", [P, 3 * D])
        wout_t = sb("wout_t", [P, PAIRS, D])
        wq_mix = sb("wq_mix", [P, PAIRS, D])
        alpha = sb("alpha", [P, 2])

        with ExitStack() as own_ctx:
            sbw = lambda n, s: own_ctx.enter_context(nc.sbuf_tensor(f"w_{n}", s, F32))
            sem = lambda n: nc.alloc_semaphore(f"w_{n}")
            wk, wv, wq, wa = sbw("k", [P, KT, D]), sbw("v", [P, KT, D]), sbw("q", [P, KT, D]), sbw("a", [P, KT, D])
            mixed = sbw("mixed", [P, 2 * PAIRS, D])
            wout = sbw("out", [P, KT, INNER])
            rel = sbw("rel", [P, 2, KT, D])
            pri = sbw("pri", [P, H])
            bcol = sbw("bcol", [P, 2, KT])
            bwide = sbw("bwide", [P, 2, KT, P])
            brow = sbw("brow", [P, 3, D])
            skip = sbw("skip", [P, 3])
            mean = sbw("mean", [P, KT * 2 * MH])
            p_w = [own_ctx.enter_context(nc.psum_tensor(f"w_prod{k}", [P, BANK], F32)) for k in range(2)]
            s_in, s_zero, s_rel, s_ready, s_taken = sem("in"), sem("zeroed"), sem("rel_in"), sem("turned"), sem("taken")
            s_own, s_scaled, s_prod, s_pt, s_exp = sem("steps"), sem("scaled"), sem("products"), sem("products_taken"), sem("exp")
            loads = [(wk[:, :, :], w["Wk"].rearrange("(i p) c -> p i c", p=P)), (wv[:, :, :], w["Wv"].rearrange("(i p) c -> p i c", p=P)),
                     (wq[:, :, :], w["Wq"].rearrange("(i p) c -> p i c", p=P)), (wa[:, :, :], w["Wa"].rearrange("(i p) c -> p i c", p=P)),
                     (wq_mix[:, :, :], w["Wqkv"][0:INNER, :].rearrange("(i p) c -> p i c", p=P)),
                     (mixed[:, :, :], w["Wqkv"][INNER:3 * INNER, :].rearrange("(i p) c -> p i c", p=P)),
                     (wout[:, :, :], w["Wout"].rearrange("(i p) c -> p i c", p=P)),
                     (pri[:, :], on_all(w["rel_pri"], H)), (brow[:, 0, :], on_all(w["bq"], D)),
                     (brow[:, 1, :], on_all(w["ba"], D)), (brow[:, 2, :], on_all(w["bout"], D)),
                     (skip[:, 0:1], on_all(w["skip"], 1))]
            cols_in = [(bcol[:, a, :], w[n].rearrange("(i p) -> p i", p=P)) for a, n in enumerate(("bk", "bv"))]
            blocks_in = [(rel[h * DK % P:h * DK % P + DK, a, h * DK // P, h * DK:(h + 1) * DK], w[n][h, :, :])
                         for a, n in enumerate(("rel_att", "rel_msg")) for h in range(H)]
            jobs = [(w_all[:, kt, KV + o * P:KV + (o + 1) * P], wq[:, o, kt * P:(kt + 1) * P]) for o in range(KT) for kt in range(KT)]
            jobs += [(w_all[:, kt, MK + o * P:MK + (o + 1) * P], mixed[:, o, kt * P:(kt + 1) * P]) for o in range(2 * PAIRS) for kt in range(KT)]
            jobs += [(wout_t[:, f, o * P:(o + 1) * P], wout[:, o, f * P:(f + 1) * P]) for o in range(KT) for f in range(PAIRS)]
            jobs += [(nodes.wa_t[:, kt, o * P:(o + 1) * P], wa[:, o, kt * P:(kt + 1) * P]) for o in range(KT) for kt in range(KT)]
            turn_pe, turn_dve = turn_all(nc, "w", own_ctx, jobs, consts.ident, s_ready, s_taken)
            block = own_ctx.enter_context(nc.Block())

            @block.sync
            def _(sp):
                for out, in_ in loads:
                    sp.dma_start(out, in_).then_inc(s_in, 16)
                for out, in_ in cols_in:
                    sp.dma_start(out, in_, allow_slow_non_contiguous=True).then_inc(s_in, 16)
                sp.wait_ge(s_zero, 1)
                for out, in_ in blocks_in:
                    sp.dma_start(out, in_).then_inc(s_rel, 16)

            @block.scalar
            def _(act):
                act.wait_ge(s_in, 16 * (len(loads) + len(cols_in)))
                nc.scalar.activation(skip[:, 1:2], skip[:, 0:1], ACT.Exp, scale=-1.0).then_inc(s_exp, 1)

            @block.tensor
            def _(pe):
                pe.wait_ge(s_in, 16 * (len(loads) + len(cols_in)))
                turn_pe(pe)
                pe.wait_ge(s_scaled, 1)
                for a, wt in enumerate((wk, wv)):
                    for kt in range(KT):
                        n = a * KT + kt
                        if n >= 2:
                            pe.wait_ge(s_pt, n - 1)
                        for o in range(KT):
                            mm = pe.matmul(p_w[n % 2][:, 0:D], wt[:, o, kt * P:(kt + 1) * P], rel[:, a, o, :],
                                           start=(o == 0), stop=(o == KT - 1))
                        mm.then_inc(s_prod, 1)
                for a in range(2):
                    pe.wait_ge(s_pt, 2 * KT - 1 + a)
                    for o in range(KT):
                        mm = pe.matmul(p_w[a][:, 0:D], bwide[:, a, o, :], rel[:, a, o, :], start=(o == 0), stop=(o == KT - 1))
                    mm.then_inc(s_prod, 1)

            @block.vector
            def _(dve):
                own = Steps(dve, s_own)
                nc.vector.memset(rel[:, :, :, :], 0.0).then_inc(s_zero, 1)
                dve.wait_ge(s_in, 16 * (len(loads) + len(cols_in)))
                for a in range(2):
                    for kt in range(KT):
                        nc.vector.tensor_copy(bwide[:, a, kt, :], bcol[:, a, kt:kt + 1].broadcast_to([P, P]))
                nc.vector.tensor_copy(bias[:, KV:3 * D], brow[:, 0, :])
                dve.wait_ge(s_exp, 1)
                own.link(nc.vector.tensor_scalar(skip[:, 2:3], skip[:, 1:2], 1.0, None, ALU.add))
                own.link(nc.vector.reciprocal(alpha[:, 0:1], skip[:, 2:3]))
                nc.vector.tensor_scalar(alpha[:, 1:2], alpha[:, 0:1], -1.0, 1.0, ALU.mult, ALU.add)
                nc.vector.scalar_tensor_tensor(nodes.bias[:, :], brow[:, 1, :], alpha[:, 0:1], brow[:, 2, :], ALU.mult, ALU.add)
                dve.wait_ge(s_rel, 16 * len(blocks_in))
                for kt in range(KT):
                    r = rel[:, 0, kt, :].rearrange("p (h e) -> p h e", h=H)
                    last = nc.vector.tensor_tensor(r, r, pri[:, :].unsqueeze(2).broadcast_to([P, H, DK]), ALU.mult)
                own.link(last)
                nc.vector.tensor_scalar(rel[:, 0, :, :], rel[:, 0, :, :], float(DK) ** -0.5, None, ALU.mult).then_inc(s_scaled, 1)
                turn_dve(dve)
                nc.vector.tensor_scalar(nodes.wa_t[:, :, :], nodes.wa_t[:, :, :], alpha[:, 0:1], None, ALU.mult)
                m4 = w_all[:, :, MK:COLS].rearrange("p k (g d) -> p k g d", d=DH)
                for kt in range(KT):
                    last = nc.vector.tensor_reduce(mean[:, kt * 2 * MH:(kt + 1) * 2 * MH], m4[:, kt, :, :], AX.X, ALU.add)
                own.link(last)
                own.link(nc.vector.tensor_scalar(mean[:, :], mean[:, :], 1.0 / DH, None, ALU.mult))
                for kt in range(KT):
                    nc.vector.tensor_tensor(m4[:, kt, :, :], m4[:, kt, :, :],
                                            mean[:, kt * 2 * MH:(kt + 1) * 2 * MH].unsqueeze(2).broadcast_to([P, 2 * MH, DH]), ALU.subtract)
                for a in range(2):
                    for kt in range(KT):
                        n = a * KT + kt
                        dve.wait_ge(s_prod, n + 1)
                        nc.vector.tensor_copy(w_all[:, kt, a * D:(a + 1) * D], p_w[n % 2][:, 0:D]).then_inc(s_pt, 1)
                for a in range(2):
                    dve.wait_ge(s_prod, 2 * KT + a + 1)
                    nc.vector.tensor_copy(bias[:, a * D:(a + 1) * D], p_w[a][:, 0:D])

        with ExitStack() as own_ctx:
            sbn = lambda n, s: own_ctx.enter_context(nc.sbuf_tensor(f"n_{n}", s, F32))
            ps = lambda n: own_ctx.enter_context(nc.psum_tensor(f"n_p_{n}", [P, BANK], F32))
            sem = lambda n: nc.alloc_semaphore(f"n_{n}")
            xn = sbn("xn", [P, 2, D])
            xt = sbn("xt", [P, 2, D])
            kv_o, q_o = sbn("kv_out", [P, 2, 2 * D]), sbn("q_out", [P, 2, D])
            square = sbn("square", [P, 2 * INNER])
            power = sbn("power", [P, 2 * MH])
            root = sbn("root", [P, 2 * MH])
            inv = sbn("inv", [P, 2 * MH])
            both = sbn("both", [P, MH])
            mk = sbn("mk", [P, 2, INNER])
            mv = sbn("mv", [P, 2, INNER])
            dots = sbn("dots", [P, PAIRS, P])
            folded = sbn("folded", [P, PAIRS, D])
            p_tq, p_kv, p_mk, p_mv, p_dots = (ps(n) for n in ("tq", "kv", "mk", "mv", "dots"))
            p_t, p_q, p_end = p_tq[:, 0:D], p_tq[:, D:2 * D], p_kv[:, 0:D]
            (s_xn, s_turn, s_xt, s_kv, s_q, s_mk, s_mv, s_kvo, s_qo, s_sq, s_pow, s_root, s_mks, s_mvs, s_dots, s_own,
             s_end, s_ended) = (sem(n) for n in ("xn", "turned", "xt", "kv", "q", "mk", "mv", "kv_kept", "q_kept", "squares",
                                                 "power", "root", "mk_kept", "mv_kept", "dots", "steps", "end", "ended"))
            s_out = [sem(f"out{b}") for b in range(2)]
            sort.prepare(own_ctx)
            block = own_ctx.enter_context(nc.Block())
            PARTS = 5
            earlier = lambda i, b: not (isinstance(i, int) and i == 0 and b == 0)

            @block.sync
            def _(sp):
                def tile(i, b, first, part):
                    n = 2 * i + b
                    if part == 1:
                        sp.wait_ge(s_kvo, n + 1)
                        sp.dma_start(src_table[bass.ds(n * P, P), :], kv_o[:, b, :]).then_inc(s_out[b], 16)
                    if part == 4:
                        sp.wait_ge(s_qo, n + 1)
                        sp.dma_start(dst_table[bass.ds(n * P, P), :], q_o[:, b, :]).then_inc(s_out[b], 16)

                sort.sync_start(sp)
                loop_steps(sp, sort.groups, lambda *a: sort.sync_step(sp, *a), tiles, tile, PARTS)
                sp.wait_ge(s_out[0], 32 * (tiles - tiles // 2))
                sp.wait_ge(s_out[1], 32 * (tiles // 2))

            @block.gpsimd
            def _(pool):
                loop_steps(pool, sort.groups, lambda *a: sort.pool_step(pool, *a), tiles, lambda *a: None, PARTS)
                sort.pool_end(pool)

            @block.vector
            def _(dve):
                own = Steps(dve, s_own)

                def tile(i, b, first, part):
                    n = 2 * i + b
                    if part == 1:
                        if not first:
                            dve.wait_ge(s_out[b], 32 * i)
                        dve.wait_ge(s_kv, n + 1)
                        nc.vector.tensor_tensor(kv_o[:, b, :], p_kv[:, :], bias[:, 0:KV], ALU.add).then_inc(s_kvo, 1)
                    if part == 3:
                        dve.wait_ge(s_sq, n + 1)
                        nc.vector.tensor_reduce(power[:, :], square[:, :].rearrange("p (g d) -> p g d", d=DH), AX.X, ALU.add).then_inc(s_pow, 1)
                    if part == 4:
                        dve.wait_ge(s_root, n + 1)
                        own.link(nc.vector.reciprocal(inv[:, :], root[:, :]))
                        own.link(nc.vector.tensor_tensor(both[:, :], inv[:, 0:MH], inv[:, MH:2 * MH], ALU.mult))
                        if not first:
                            dve.wait_ge(s_dots, n - 1)
                        nc.vector.tensor_tensor(mk[:, b, :].rearrange("p (h d) -> p h d", d=DH), p_mk[:, :].rearrange("p (h d) -> p h d", d=DH),
                                                both[:, :].unsqueeze(2).broadcast_to([P, MH, DH]), ALU.mult).then_inc(s_mks, 1)
                        if not (isinstance(i, int) and n == tiles - 1):
                            if earlier(i, b):
                                dve.wait_ge(s_turn, n)
                            normalised(nc, nodes, xn[:, 1 - b, :], n + 1).then_inc(s_xn, 1)
                        dve.wait_ge(s_q, n + 1)
                        nc.vector.tensor_tensor(q_o[:, b, :], p_q, bias[:, KV:3 * D], ALU.add).then_inc(s_qo, 1)

                sort.edges_in(dve, 0, 0, 0)
                normalised(nc, nodes, xn[:, 0, :], 0).then_inc(s_xn, 1)
                loop_steps(dve, sort.groups, lambda *a: sort.vector_step(dve, own, *a), tiles, tile, PARTS, own, sort.PER_STEP, 2)
                sort.vector_end(dve, own)
                own.link(nc.vector.memset(dots[:, :, :], 0.0))
                dve.wait_ge(s_dots, tiles)
                pd = p_dots[:, :].rearrange("p (a c) -> p a c", c=P)
                nc.vector.tensor_copy(dots[0:DH, :, 0:DH], pd[0:DH, :, 0:DH])
                nc.vector.tensor_copy(dots[DH:P, :, DH:P], pd[DH:P, :, DH:P]).then_inc(s_ended, 1)
                for a in range(PAIRS):
                    dve.wait_ge(s_end, a + 1)
                    nc.vector.tensor_copy(folded[:, a, :], p_end).then_inc(s_ended, 1)
                for kt in range(KT):
                    dve.wait_ge(s_end, PAIRS + kt + 1)
                    own.link(nc.vector.tensor_scalar(nodes.gx[:, kt, :], p_end, 1.0 / nodes.count, None, ALU.mult))
                    d = nodes.gx[:, kt, kt * P:(kt + 1) * P]
                    nc.vector.scalar_tensor_tensor(d, consts.ident[:, :], alpha[:, 1:2], d, ALU.mult, ALU.add).then_inc(s_ended, 1)

            @block.scalar
            def _(act):
                def tile(i, b, first, part):
                    n = 2 * i + b
                    if part == 0:
                        act.wait_ge(s_turn, n + 1)
                        if not first:
                            act.wait_ge(s_q, n - 1)
                        nc.scalar.copy(xt[:, b, :], p_t).then_inc(s_xt, 1)
                    if part == 2:
                        act.wait_ge(s_mk, n + 1)
                        if earlier(i, b):
                            act.wait_ge(s_pow, n)
                        nc.scalar.activation(square[:, 0:INNER], p_mk[:, :], ACT.Square)
                    if part == 3:
                        act.wait_ge(s_mv, n + 1)
                        nc.scalar.activation(square[:, INNER:2 * INNER], p_mv[:, :], ACT.Square).then_inc(s_sq, 1)
                        if not first:
                            act.wait_ge(s_dots, n - 1)
                        nc.scalar.copy(mv[:, b, :], p_mv[:, :]).then_inc(s_mvs, 1)
                        act.wait_ge(s_pow, n + 1)
                        nc.scalar.activation(root[:, :], power[:, :], ACT.Sqrt, bias=nodes.eps[:, :], scale=1.0 / DH).then_inc(s_root, 1)

                loop_steps(act, sort.groups, lambda *a: sort.scalar_step(act, *a), tiles, tile, PARTS)

            @block.tensor
            def _(pe):
                def products(i, b, bank, c0, c1, done):
                    for kt in range(KT):
                        mm = pe.matmul(bank, xt[:, b, kt * P:(kt + 1) * P], w_all[:, kt, c0:c1], start=(kt == 0), stop=(kt == KT - 1))
                    mm.then_inc(done, 1)

                def dots_of(i, b):
                    n = 2 * i + b
                    pe.wait_ge(s_mks, n + 1)
                    pe.wait_ge(s_mvs, n + 1)
                    for a in range(PAIRS):
                        mm = pe.matmul(p_dots[:, a * P:(a + 1) * P], mv[:, b, a * P:(a + 1) * P], mk[:, b, a * P:(a + 1) * P],
                                       start=(not earlier(i, b) and a == 0), stop=False, skip_group_check=True)
                    mm.then_inc(s_dots, 1)

                def tile(i, b, first, part):
                    n = 2 * i + b
                    if part == 0:
                        pe.wait_ge(s_xn, n + 1)
                        if earlier(i, b):
                            pe.wait_ge(s_qo, n)
                        for kt in range(KT):
                            t = pe.transpose(p_t[:, kt * P:(kt + 1) * P], xn[:, b, kt * P:(kt + 1) * P], consts.ident[:, :])
                        t.then_inc(s_turn, 1)
                        if earlier(i, b):
                            dots_of(i if b else i - 1, 1 - b)
                    if part == 1:
                        pe.wait_ge(s_xt, n + 1)
                        if earlier(i, b):
                            pe.wait_ge(s_kvo, n)
                        products(i, b, p_kv[:, :], 0, KV, s_kv)
                    if part == 2:
                        if earlier(i, b):
                            pe.wait_ge(s_mks, n)
                        products(i, b, p_mk[:, :], MK, MV, s_mk)
                    if part == 3:
                        if earlier(i, b):
                            pe.wait_ge(s_mvs, n)
                        products(i, b, p_mv[:, :], MV, COLS, s_mv)
                    if part == 4:
                        products(i, b, p_q, KV, 3 * D, s_q)

                loop_steps(pe, sort.groups, lambda *a: sort.tensor_step(pe, *a), tiles, tile, PARTS)
                dots_of((tiles - 1) // 2, (tiles - 1) % 2)
                pe.wait_ge(s_kvo, tiles)
                for a in range(PAIRS):
                    pe.wait_ge(s_ended, a + 1)
                    pe.matmul(p_end, dots[:, a, :], wout_t[:, a, :], start=True, stop=True).then_inc(s_end, 1)
                for kt in range(KT):
                    pe.wait_ge(s_ended, PAIRS + kt + 1)
                    for a in range(PAIRS):
                        mm = pe.matmul(p_end, wq_mix[:, a, kt * P:(kt + 1) * P], folded[:, a, :],
                                       start=(a == 0), stop=(a == PAIRS - 1))
                    mm.then_inc(s_end, 1)


def gather_sums(nc, name, consts, nodes, lists, partial, counts, ends, heads, width, before, at_end):
    batches = lists.batches
    tiles_b = spans(batches, P)
    nt, tiles = len(tiles_b), nodes.tiles
    sums = heads * (width + 1)
    cols = sums + heads
    with ExitStack() as outer:
        ends_of = outer.enter_context(nc.sbuf_tensor(f"{name}_ends_of", [P, nt, cols], F32))
        split = outer.enter_context(nc.sbuf_tensor(f"{name}_split", [P, nt, 3, cols], BF16))
        edge_i = outer.enter_context(nc.sbuf_tensor(f"{name}_edge_i", [P, 3, tiles], I32))
        with ExitStack() as ctx:
            sb = lambda n, s: ctx.enter_context(nc.sbuf_tensor(f"{name}_{n}", s, F32))
            sem = lambda n: nc.alloc_semaphore(f"{name}_{n}")
            wide = sb("wide", [P, nt, heads])
            line = sb("line", [heads, 2, batches])
            cut = sb("cut", [heads, 2, batches])
            top = sb("top", [heads, 3, batches])
            back = sb("back", [P, nt, 2, heads])
            weight = sb("weight", [P, nt, heads])
            edge = sb("edge", [P, 4, tiles])
            zero = sb("zero", [1, cols])
            s_in, s_wide, s_t1, s_k1, s_t2, s_k2 = (sem(n) for n in ("in", "wide", "turned", "taken", "turned_back", "taken_back"))
            s_own, s_top, s_diff, s_w, s_zero, s_zout = (sem(n) for n in ("steps", "tops", "diffs", "weights", "zero", "zero_out"))
            jobs1 = [(line[:, 0, t0:t0 + k], ends_of[0:k, i, sums:cols]) for i, (t0, k) in enumerate(tiles_b)]
            jobs1 += [(line[:, 1, t0:t0 + k], wide[0:k, i, :]) for i, (t0, k) in enumerate(tiles_b)]
            jobs2 = [(back[0:k, i, a, :], top[:, a + 1, t0:t0 + k]) for i, (t0, k) in enumerate(tiles_b) for a in range(2)]
            pe1, dve1 = turn_all(nc, f"{name}_a", ctx, jobs1, consts.ident, s_t1, s_k1)
            pe2, dve2 = turn_all(nc, f"{name}_b", ctx, jobs2, consts.ident, s_t2, s_k2)
            block = ctx.enter_context(nc.Block())

            @block.sync
            def _(sp):
                for i, (t0, k) in enumerate(tiles_b):
                    sp.dma_start(ends_of[0:k, i, :], partial[(P - 1) * batches + t0:(P - 1) * batches + t0 + k, :]).then_inc(s_in, 16)
                sp.wait_ge(s_zero, 1)
                sp.dma_start(partial[P * batches:P * batches + 1, :], zero[:, :]).then_inc(s_zout, 16)
                sp.wait_ge(s_zout, 16)

            @block.tensor
            def _(pe):
                pe.wait_ge(s_in, 16 * nt)
                pe.wait_ge(s_wide, 1)
                pe1(pe)
                pe.wait_ge(s_top, 1)
                pe2(pe)

            @block.scalar
            def _(act):
                act.wait_ge(s_diff, 1)
                nc.scalar.activation(weight[:, :, :], weight[:, :, :], ACT.Exp).then_inc(s_w, 1)

            @block.vector
            def _(dve):
                own = Steps(dve, s_own)
                nc.vector.memset(zero[:, :], 0.0).then_inc(s_zero, 1)
                own.link(nc.vector.tensor_scalar(edge[:, 0, :], ends[:, 0:tiles], -1.0, 0.0, ALU.add, ALU.max))
                own.link(nc.vector.tensor_copy(edge_i[:, 0, :], edge[:, 0, :]))
                nc.vector.tensor_scalar(edge_i[:, 1, :], edge_i[:, 0, :], P - 1, None, ALU.bitwise_and)
                own.link(nc.vector.tensor_scalar(edge_i[:, 2, :], edge_i[:, 0, :], 7, None, ALU.logical_shift_right))
                nc.vector.tensor_copy(edge[:, 0, :], edge_i[:, 1, :])
                own.link(nc.vector.tensor_copy(edge[:, 1, :], edge_i[:, 2, :]))
                nc.vector.tensor_scalar(edge[:, 2, :], counts[:, 0:tiles], 0.0, None, ALU.is_equal)
                own.link(nc.vector.tensor_scalar(edge[:, 3, :], edge[:, 0, :], float(P - 1), None, ALU.is_equal))
                own.link(nc.vector.tensor_tensor(edge[:, 2, :], edge[:, 2, :], edge[:, 3, :], ALU.max))
                own.link(nc.vector.scalar_tensor_tensor(edge[:, 1, :], edge[:, 0, :], float(batches), edge[:, 1, :], ALU.mult, ALU.add))
                own.link(nc.vector.tensor_scalar(edge[:, 0, :], edge[:, 1, :], -1.0, float(P * batches), ALU.mult, ALU.add))
                own.link(nc.vector.tensor_tensor(edge[:, 0, :], edge[:, 0, :], edge[:, 2, :], ALU.mult))
                own.link(nc.vector.tensor_tensor(edge_i[:, 0, :], edge[:, 1, :], edge[:, 0, :], ALU.add))

                nc.vector.tensor_copy(wide[:, :, :], lists.last[:, :].unsqueeze(2).broadcast_to([P, nt, heads])).then_inc(s_wide, 1)
                nc.vector.memset(cut[:, :, :], -FAR)
                own.link(nc.vector.memset(weight[:, :, :], 0.0))
                dve.wait_ge(s_in, 16 * nt)
                dve1(dve)
                own.link(nc.vector.tensor_tensor(cut[:, 0, 1:], line[:, 1, 1:], line[:, 1, 0:batches - 1], ALU.not_equal))
                own.link(nc.vector.tensor_scalar(cut[:, 0, 1:], cut[:, 0, 1:], -FAR, None, ALU.mult))
                own.link(nc.vector.tensor_copy(cut[:, 1, 0:batches - 1], cut[:, 0, 1:]))
                own.link(nc.vector.tensor_tensor_scan(top[:, 0, :], cut[:, 0, :], line[:, 0, :], 0.0, ALU.add, ALU.max))
                own.link(nc.vector.tensor_tensor_scan(top[:, 1, ::-1], cut[:, 1, ::-1], top[:, 0, ::-1], 0.0, ALU.add, ALU.max))
                own.link(nc.vector.tensor_scalar(top[:, 2, :], cut[:, 0, :], 0.0, None, ALU.is_lt))
                nc.vector.tensor_tensor(top[:, 2, :], top[:, 2, :], top[:, 1, :], ALU.mult).then_inc(s_top, 1)
                dve2(dve)
                for i, (t0, k) in enumerate(tiles_b):
                    last = nc.vector.tensor_tensor(weight[0:k, i, :], ends_of[0:k, i, sums:cols], back[0:k, i, 0, :], ALU.subtract)
                last.then_inc(s_diff, 1)
                dve.wait_ge(s_diff, 1)
                dve.wait_ge(s_w, 1)
                for i, (t0, k) in enumerate(tiles_b):
                    e = ends_of[0:k, i, 0:sums].rearrange("p (h w) -> p h w", h=heads)
                    nc.vector.tensor_tensor(e, e, weight[0:k, i, :].unsqueeze(2).broadcast_to([k, heads, width + 1]), ALU.mult)
                    last = nc.vector.tensor_copy(ends_of[0:k, i, sums:cols], back[0:k, i, 1, :])
                own.link(last)
                for part in range(3):
                    for i, (t0, k) in enumerate(tiles_b):
                        last = nc.vector.tensor_copy(split[0:k, i, part, :], ends_of[0:k, i, :])
                    own.link(last)
                    if part < 2:
                        for i, (t0, k) in enumerate(tiles_b):
                            last = nc.vector.tensor_tensor(ends_of[0:k, i, :], ends_of[0:k, i, :], split[0:k, i, part, :], ALU.subtract)
                        own.link(last)

        with ExitStack() as ctx:
            sb = lambda n, s, d=F32: ctx.enter_context(nc.sbuf_tensor(f"{name}_{n}", s, d))
            sem = lambda n: nc.alloc_semaphore(f"{name}_{n}")
            ids = sb("ids", [P, 2, P])
            chosen = sb("chosen", [P, 2, nt, P], BF16)
            each = 8
            ring = sb("ring", [P, each], I32)
            row = sb("row", [P, each, cols])
            bank_s = [ctx.enter_context(nc.psum_tensor(f"{name}_sum{b}", [P, BANK], F32)) for b in range(2)]
            s_step, s_ring, s_chosen, s_sum, s_kept, s_got, s_rows = (
                sem(n) for n in ("ids_step", "ring", "chosen", "sums", "kept", "got", "rows"))
            block = ctx.enter_context(nc.Block())

            @block.gpsimd
            def _(pool):
                def fetch(c, k):
                    t0 = c * each
                    pool.tensor_copy(ring[:, 0:k], edge_i[:, 0, bass.ds(t0, k)]).then_inc(s_ring, 1)
                    pool.wait_ge(s_ring, c + 1)
                    pool.nop(nofuse=True)
                    for j in range(k):
                        pool.indirect_dma_start(row[:, j, :], None, partial[:, :],
                                                bass.IndirectOffsetOnAxis(ap=ring[:, j:j + 1], axis=0)).then_inc(s_got, 16)
                    pool.wait_ge(s_got, 16 * (t0 + k))
                    pool.tensor_copy(at_end[:, bass.ds(t0, k), :], row[:, 0:k, :]).then_inc(s_rows, 1)
                    pool.wait_ge(s_rows, c + 1)

                with pool.Fori(0, tiles // each) as c:
                    fetch(c, each)
                if tiles % each:
                    fetch(tiles // each, tiles % each)

            @block.tensor
            def _(pe):
                def tile(i, b, first):
                    n = 2 * i + b
                    pe.wait_ge(s_chosen, n + 1)
                    if not first:
                        pe.wait_ge(s_kept, n - 1)
                    for kt, (t0, k) in enumerate(tiles_b):
                        if k < P:
                            pe.nop(nofuse=True)
                        for part in range(3):
                            mm = pe.matmul(bank_s[b][:, 0:cols], chosen[0:k, b, kt, :], split[0:k, kt, part, :],
                                           start=(kt == 0 and part == 0), stop=(kt == nt - 1 and part == 2))
                    mm.then_inc(s_sum, 1)

                group_loop(pe, tiles, tile)

            @block.scalar
            def _(act):
                def keep(i, b, first):
                    n = 2 * i + b
                    act.wait_ge(s_sum, n + 1)
                    nc.scalar.copy(before[:, bass.ds(n, 1), :].rearrange("p o c -> p (o c)"), bank_s[b][:, 0:cols]).then_inc(s_kept, 1)

                group_loop(act, tiles, keep)

            @block.vector
            def _(dve):
                own = Steps(dve, s_step)
                own.link(nc.vector.tensor_copy(ids[:, 0, :], consts.lane_b[:, :]))

                def choose(i, b, first):
                    n = 2 * i + b
                    if not first:
                        dve.wait_ge(s_sum, n - 1)
                    nc.vector.tensor_tensor(chosen[:, b, :, :], ids[:, b, :].unsqueeze(1).broadcast_to([P, nt, P]),
                                            lists.last[:, :].unsqueeze(2).broadcast_to([P, nt, P]), ALU.is_equal).then_inc(s_chosen, 1)
                    own.link(nc.vector.tensor_scalar(ids[:, 1 - b, :], ids[:, b, :], float(P), None, ALU.add))

                group_loop(dve, tiles, choose, own, 2)


def weights_of(nc, own, marks, before, at_end, heads, width, more=None):
    sums = heads * (width + 1)
    parts = [before, at_end]
    for k, part in enumerate(parts):
        z = part[:, :, 0:sums].rearrange("p n (h w) -> p n h w", h=heads)[:, :, :, width]
        own.link(nc.vector.tensor_scalar(marks[:, k], z, 0.0, 1.0, ALU.is_gt, ALU.subtract))
        own.link(nc.vector.tensor_scalar(marks[:, k], marks[:, k], FAR, None, ALU.mult))
        own.link(nc.vector.tensor_tensor(marks[:, k], marks[:, k], part[:, :, sums:sums + heads], ALU.add))
    used = 2 + (more is not None)
    if more is not None:
        own.link(nc.vector.tensor_copy(marks[:, 2], more))
    own.link(nc.vector.tensor_tensor(marks[:, 3], marks[:, 0], marks[:, 1], ALU.max))
    if more is not None:
        own.link(nc.vector.tensor_tensor(marks[:, 3], marks[:, 3], marks[:, 2], ALU.max))
    for k in range(used):
        last = nc.vector.tensor_tensor(marks[:, k], marks[:, k], marks[:, 3], ALU.subtract)
    return last


def first_residual(nc, consts, nodes, before, at_end, heads, width):
    D, tiles = nodes.dim, nodes.tiles
    KT = D // P
    sums = heads * (width + 1)
    with ExitStack() as ctx:
        sb = lambda n, s: ctx.enter_context(nc.sbuf_tensor(f"r_{n}", s, F32))
        sem = lambda n: nc.alloc_semaphore(f"r_{n}")
        marks = sb("marks", [P, 4, tiles, heads])
        xn = sb("xn", [P, 2, D])
        t_now = sb("t", [P, 2, D])
        turned = sb("turned", [P, 2, 2 * D])
        p_t = [ctx.enter_context(nc.psum_tensor(f"r_t{b}", [P, BANK], F32)) for b in range(2)]
        p_y = [ctx.enter_context(nc.psum_tensor(f"r_y{b}", [P, BANK], F32)) for b in range(2)]
        s_own, s_marks, s_w, s_ready, s_bias, s_turn, s_kept, s_y, s_x = (sem(n) for n in (
            "steps", "marks", "weights", "inputs", "bias_in", "turned", "turned_kept", "product", "x"))
        block = ctx.enter_context(nc.Block())
        whole = lambda part: part[:, :, 0:sums].rearrange("p n (h w) -> p n h w", h=heads)

        @block.vector
        def _(dve):
            own = Steps(dve, s_own)
            weights_of(nc, own, marks, before, at_end, heads, width).then_inc(s_marks, 1)
            dve.wait_ge(s_w, 1)
            for k, part in enumerate((before, at_end)):
                last = nc.vector.tensor_tensor(whole(part), whole(part), marks[:, k].unsqueeze(3)
                                               .broadcast_to([P, tiles, heads, width + 1]), ALU.mult)
            own.link(last)
            own.link(nc.vector.tensor_tensor(before[:, :, 0:sums], before[:, :, 0:sums], at_end[:, :, 0:sums], ALU.add))
            own.link(nc.vector.tensor_scalar(marks[:, 2], whole(before)[:, :, :, width], 1.0e-30, None, ALU.max))
            own.link(nc.vector.reciprocal(marks[:, 3], marks[:, 2]))

            def front(i, b, first):
                n = 2 * i + b
                if not first:
                    dve.wait_ge(s_turn, n - 1)
                x = nodes.x[:, bass.ds(n, 1), :].rearrange("p o c -> p (o c)")
                normalised(nc, nodes, xn[:, b, :], n)
                nc.vector.tensor_tensor(t_now[:, b, :].rearrange("p (h w) -> p h w", h=heads),
                                        before[:, bass.ds(n, 1), 0:sums].rearrange("p o (h w) -> p (o h) w", h=heads)[:, :, 0:width],
                                        marks[:, 3, bass.ds(n, 1), :].rearrange("p o h -> p (o h)").unsqueeze(2)
                                        .broadcast_to([P, heads, width]), ALU.mult).then_inc(s_ready, 1)
                dve.wait_ge(s_ready, n + 1)
                nc.vector.tensor_tensor(x, x, nodes.bias[:, :], ALU.add).then_inc(s_bias, 1)

            def back(i, b, first):
                n = 2 * i + b
                x = nodes.x[:, bass.ds(n, 1), :].rearrange("p o c -> p (o c)")
                dve.wait_ge(s_bias, n + 1)
                dve.wait_ge(s_y, n + 1)
                nc.vector.tensor_tensor(x, x, p_y[b][:, 0:D], ALU.add).then_inc(s_x, 1)

            lagged_loop(dve, tiles, front, back, lag=2)

        @block.scalar
        def _(act):
            act.wait_ge(s_marks, 1)
            nc.scalar.activation(marks[:, 0:2], marks[:, 0:2], ACT.Exp).then_inc(s_w, 1)

            def tile(i, b, first):
                n = 2 * i + b
                act.wait_ge(s_turn, n + 1)
                if not first:
                    act.wait_ge(s_y, n - 1)
                nc.scalar.copy(turned[:, b, :], p_t[b][:, :]).then_inc(s_kept, 1)

            group_loop(act, tiles, tile)

        @block.tensor
        def _(pe):
            def front(i, b, first):
                n = 2 * i + b
                pe.wait_ge(s_ready, n + 1)
                if not first:
                    pe.wait_ge(s_kept, n - 1)
                for a, part in enumerate((t_now, xn)):
                    for kt in range(KT):
                        c = (a * KT + kt) * P
                        mm = pe.transpose(p_t[b][:, c:c + P], part[:, b, kt * P:(kt + 1) * P], consts.ident[:, :])
                mm.then_inc(s_turn, 1)

            def back(i, b, first):
                n = 2 * i + b
                pe.wait_ge(s_kept, n + 1)
                if not first:
                    pe.wait_ge(s_x, n - 1)
                for a, w in enumerate((nodes.wa_t, nodes.gx)):
                    for kt in range(KT):
                        c = (a * KT + kt) * P
                        mm = pe.matmul(p_y[b][:, 0:D], turned[:, b, c:c + P], w[:, kt, :], start=(c == 0), stop=(c == (2 * KT - 1) * P))
                mm.then_inc(s_y, 1)

            lagged_loop(pe, tiles, front, back)


def gat_inputs(nc, consts, nodes, w, y_t, feats, src_table, dst_table):
    D, tiles = nodes.dim, nodes.tiles
    KT = D // P
    H, E = w["att_src"].shape
    HE = H * E
    F = HE + 2 * H
    with ExitStack() as ctx:
        sb = lambda n, s: ctx.enter_context(nc.sbuf_tensor(f"y_{n}", s, F32))
        sem = lambda n: nc.alloc_semaphore(f"y_{n}")
        wg = sb("wg", [P, KT, F])
        att = sb("att", [P, 2, HE])
        prod = sb("prod", [P, KT, HE])
        y = sb("y", [P, 2, D])
        yt = sb("yt", [P, 2, D])
        p_t = [ctx.enter_context(nc.psum_tensor(f"y_t{b}", [P, BANK], F32)) for b in range(2)]
        p_f = [ctx.enter_context(nc.psum_tensor(f"y_f{b}", [P, BANK], F32)) for b in range(2)]
        s_in, s_own, s_w, s_y, s_turn, s_kept, s_f, s_fk, s_out = (sem(n) for n in (
            "in", "steps", "weights", "rows", "turned", "turned_kept", "feats", "feats_kept", "out"))
        block = ctx.enter_context(nc.Block())

        @block.sync
        def _(sp):
            sp.dma_start(wg[:, :, 0:HE], w["W_gat"].rearrange("(k p) c -> p k c", p=P)).then_inc(s_in, 16)
            for a, n in enumerate(("att_src", "att_dst")):
                sp.dma_start(att[:, a, :], on_all(w[n].rearrange("h e -> (h e)"), HE)).then_inc(s_in, 16)
            sp.wait_ge(s_fk, tiles)
            sp.dma_start(src_table.rearrange("(i p) c -> p i c", p=P), feats[:, :, 0:HE + H]).then_inc(s_out, 16)
            sp.dma_start(dst_table.rearrange("(i p) c -> p i c", p=P), feats[:, :, HE + H:F]).then_inc(s_out, 16)
            sp.wait_ge(s_out, 32)

        @block.vector
        def _(dve):
            own = Steps(dve, s_own)
            dve.wait_ge(s_in, 48)
            for a in range(2):
                own.link(nc.vector.tensor_tensor(prod[:, :, :], wg[:, :, 0:HE], att[:, a, :].unsqueeze(1).broadcast_to([P, KT, HE]), ALU.mult))
                c = HE + a * H
                last = nc.vector.tensor_reduce(wg[:, :, c:c + H], prod[:, :, :].rearrange("p k (h e) -> p k h e", h=H), AX.X, ALU.add)
                own.link(last)
            nc.vector.memset(prod[:, 0, 0:1], 0.0).then_inc(s_w, 1)

            def front(i, b, first):
                n = 2 * i + b
                if not first:
                    dve.wait_ge(s_turn, n - 1)
                normalised(nc, nodes, y[:, b, :], n).then_inc(s_y, 1)

            def back(i, b, first):
                n = 2 * i + b
                dve.wait_ge(s_f, n + 1)
                nc.vector.tensor_copy(feats[:, bass.ds(n, 1), :].rearrange("p o c -> p (o c)"), p_f[b][:, 0:F]).then_inc(s_fk, 1)

            lagged_loop(dve, tiles, front, back, lag=2)

        @block.scalar
        def _(act):
            def tile(i, b, first):
                n = 2 * i + b
                act.wait_ge(s_turn, n + 1)
                if not first:
                    act.wait_ge(s_f, n - 1)
                nc.scalar.copy(yt[:, b, :], p_t[b][:, 0:D])
                nc.scalar.copy(y_t[:, :, bass.ds(n * P, P)], p_t[b][:, 0:D].rearrange("p (k c) -> p k c", k=KT)).then_inc(s_kept, 1)

            group_loop(act, tiles, tile)

        @block.tensor
        def _(pe):
            pe.wait_ge(s_w, 1)

            def front(i, b, first):
                n = 2 * i + b
                pe.wait_ge(s_y, n + 1)
                if not first:
                    pe.wait_ge(s_kept, n - 1)
                for kt in range(KT):
                    mm = pe.transpose(p_t[b][:, kt * P:(kt + 1) * P], y[:, b, kt * P:(kt + 1) * P], consts.ident[:, :])
                mm.then_inc(s_turn, 1)

            def back(i, b, first):
                n = 2 * i + b
                pe.wait_ge(s_kept, n + 1)
                if not first:
                    pe.wait_ge(s_fk, n - 1)
                for kt in range(KT):
                    mm = pe.matmul(p_f[b][:, 0:F], yt[:, b, kt * P:(kt + 1) * P], wg[:, kt, :], start=(kt == 0), stop=(kt == KT - 1))
                mm.then_inc(s_f, 1)

            lagged_loop(pe, tiles, front, back)


def gates(nc, nodes, w, feats, before, at_end, gate):
    tiles = nodes.tiles
    H, E = w["att_src"].shape
    HE = H * E
    sums = H * (E + 1)
    with ExitStack() as ctx:
        sb = lambda n, s: ctx.enter_context(nc.sbuf_tensor(f"g_{n}", s, F32))
        sem = lambda n: nc.alloc_semaphore(f"g_{n}")
        marks = sb("marks", [P, 4, tiles, H])
        vec = sb("vec", [P, 3, HE])
        own_score = sb("own_score", [P, tiles, H])
        own_raw = sb("own_raw", [P, tiles, H])
        tmp = sb("tmp", [P, tiles, HE])
        agg = sb("agg", [P, tiles, HE])
        one = sb("one", [P, 4, tiles])
        score = sb("score", [P, tiles, E])
        lost = sb("lost", [P, tiles, E])
        beat = sb("beat", [P, tiles])
        s_in, s_own, s_marks, s_w, s_var, s_root, s_top, s_ex = (sem(n) for n in (
            "in", "steps", "marks", "weights", "var", "root", "top", "exp"))
        block = ctx.enter_context(nc.Block())

        @block.sync
        def _(sp):
            for a, n in enumerate(("b_gat", "ln_gamma", "ln_beta")):
                sp.dma_start(vec[:, a, :], on_all(w[n], HE)).then_inc(s_in, 16)

        @block.scalar
        def _(act):
            act.wait_ge(s_marks, 1)
            nc.scalar.activation(marks[:, 0:3], marks[:, 0:3], ACT.Exp).then_inc(s_w, 1)
            act.wait_ge(s_var, 1)
            nc.scalar.activation(one[:, 1, :], one[:, 0, :], ACT.Sqrt, bias=nodes.eps[:, :], scale=1.0 / HE).then_inc(s_root, 1)
            act.wait_ge(s_top, 1)
            nc.scalar.activation(score[:, :, :], score[:, :, :], ACT.Exp).then_inc(s_ex, 1)

        @block.vector
        def _(dve):
            own = Steps(dve, s_own)
            V = nc.vector
            own.link(V.tensor_tensor(own_raw[:, :, :], feats[:, :, HE:HE + H], feats[:, :, HE + H:HE + 2 * H], ALU.add))
            own.link(V.tensor_scalar(own_score[:, :, :], own_raw[:, :, :], 0.2, None, ALU.mult))
            own.link(V.tensor_tensor(own_score[:, :, :], own_score[:, :, :], own_raw[:, :, :], ALU.max))
            weights_of(nc, own, marks, before, at_end, H, E, own_score[:, :, :]).then_inc(s_marks, 1)
            dve.wait_ge(s_w, 1)
            whole = lambda part: part[:, :, 0:sums].rearrange("p n (h w) -> p n h w", h=H)
            h4 = lambda t: t.rearrange("p n (h e) -> p n h e", h=H)
            for k, part in enumerate((before, at_end)):
                last = V.tensor_tensor(whole(part), whole(part), marks[:, k].unsqueeze(3).broadcast_to([P, tiles, H, E + 1]), ALU.mult)
            own.link(last)
            own.link(V.tensor_tensor(before[:, :, 0:sums], before[:, :, 0:sums], at_end[:, :, 0:sums], ALU.add))
            wide = lambda t: t.unsqueeze(3).broadcast_to([P, tiles, H, E])
            own.link(V.tensor_tensor(h4(tmp[:, :, :]), h4(feats[:, :, 0:HE]), wide(marks[:, 2]), ALU.mult))
            own.link(V.tensor_tensor(h4(agg[:, :, :]), whole(before)[:, :, :, 0:E], h4(tmp[:, :, :]), ALU.add))
            own.link(V.tensor_tensor(own_raw[:, :, :], whole(before)[:, :, :, E], marks[:, 2], ALU.add))
            own.link(V.tensor_scalar(own_raw[:, :, :], own_raw[:, :, :], 1.0e-16, None, ALU.add))
            own.link(V.reciprocal(own_score[:, :, :], own_raw[:, :, :]))
            own.link(V.tensor_tensor(h4(agg[:, :, :]), h4(agg[:, :, :]), wide(own_score[:, :, :]), ALU.mult))
            dve.wait_ge(s_in, 48)
            along = lambda a: vec[:, a, :].unsqueeze(1).broadcast_to([P, tiles, HE])
            each = lambda t: t.unsqueeze(2).broadcast_to([P, tiles, HE])
            own.link(V.tensor_tensor(agg[:, :, :], agg[:, :, :], along(0), ALU.add))
            own.link(V.tensor_reduce(one[:, 2, :], agg[:, :, :], AX.X, ALU.add))
            own.link(V.tensor_scalar(one[:, 2, :], one[:, 2, :], 1.0 / HE, None, ALU.mult))
            own.link(V.tensor_tensor(agg[:, :, :], agg[:, :, :], each(one[:, 2, :]), ALU.subtract))
            own.link(V.tensor_tensor(tmp[:, :, :], agg[:, :, :], agg[:, :, :], ALU.mult))
            V.tensor_reduce(one[:, 0, :], tmp[:, :, :], AX.X, ALU.add).then_inc(s_var, 1)
            dve.wait_ge(s_root, 1)
            own.link(V.reciprocal(one[:, 3, :], one[:, 1, :]))
            own.link(V.tensor_tensor(agg[:, :, :], agg[:, :, :], each(one[:, 3, :]), ALU.mult))
            own.link(V.tensor_tensor(agg[:, :, :], agg[:, :, :], along(1), ALU.mult))
            own.link(V.tensor_tensor(agg[:, :, :], agg[:, :, :], along(2), ALU.add))
            own.link(V.tensor_reduce(score[:, :, :], agg[:, :, :].rearrange("p n (h e) -> p n e h", h=H), AX.X, ALU.add))
            own.link(V.tensor_scalar(score[:, :, :], score[:, :, :], 1.0 / H, None, ALU.mult))
            own.link(V.memset(lost[:, :, :], 0.0))
            for e in range(E):
                for o in range(E):
                    if o != e:
                        own.link(V.tensor_tensor(beat[:, :], score[:, :, o], score[:, :, e], ALU.is_ge if o < e else ALU.is_gt))
                        own.link(V.tensor_tensor(lost[:, :, e], lost[:, :, e], beat[:, :], ALU.add))
            own.link(V.tensor_scalar(lost[:, :, :], lost[:, :, :], 1.5, None, ALU.is_lt))
            own.link(V.tensor_reduce(one[:, 0, :], score[:, :, :], AX.X, ALU.max))
            V.tensor_tensor(score[:, :, :], score[:, :, :], one[:, 0, :].unsqueeze(2).broadcast_to([P, tiles, E]), ALU.subtract)\
                .then_inc(s_top, 1)
            dve.wait_ge(s_ex, 1)
            own.link(V.tensor_tensor(score[:, :, :], score[:, :, :], lost[:, :, :], ALU.mult))
            own.link(V.tensor_reduce(one[:, 1, :], score[:, :, :], AX.X, ALU.add))
            own.link(V.reciprocal(one[:, 2, :], one[:, 1, :]))
            V.tensor_tensor(gate[:, :, :], score[:, :, :], one[:, 2, :].unsqueeze(2).broadcast_to([P, tiles, E]), ALU.mult)


class Experts:

    CH = 2

    def __init__(self, nc, ctx, nodes, w, y_t, out, groups):
        self.nc, self.nodes, self.w, self.y_t, self.out = nc, nodes, w, y_t, out
        self.E, _, HID = w["W1"].shape
        D = nodes.dim
        self.KT, self.MT = D // P, HID // P
        self.chunks, self.tail = nodes.tiles // self.CH, nodes.tiles % self.CH
        assert self.chunks % 2 == 0 and self.tail <= 1
        self.passes = self.chunks // 2
        self.groups_per_pass = groups // self.passes // 2 * 2
        sb = lambda n, s: ctx.enter_context(nc.sbuf_tensor(f"e_{n}", s, F32))
        self.w1 = sb("w1", [P, self.E, self.KT, HID])
        self.w2 = sb("w2", [P, self.E, self.MT, D])
        self.b1 = sb("b1", [P, self.E, self.MT])
        self.b2 = sb("b2", [P, self.E, D])
        self.hid = sb("hid", [P, 2, self.MT, self.CH * P])
        self.stash = sb("stash", [P, 2, self.CH, D])
        self.p_h = [ctx.enter_context(nc.psum_tensor(f"e_h{b}", [P, BANK], F32)) for b in range(2)]
        self.p_o = [ctx.enter_context(nc.psum_tensor(f"e_o{b}", [P, BANK], F32)) for b in range(2)]
        assert self.MT == 2 * self.CH
        self.units = []
        for q in range(2):
            for e in range(self.E):
                before = (q, e - 1) if e else (q - 1, self.E - 1)
                for m in range(self.MT):
                    self.units.append((q, ("h", e, m)))
                    if m % 2:
                        self.units.append((before[0], ("p", before[1], m // 2)))

    def semaphores(self):
        sem = lambda n: self.nc.alloc_semaphore(f"e_{n}")
        self.s_h, self.s_gelu, self.s_o, self.s_kept = sem("hidden"), sem("gelu"), sem("product"), sem("product_kept")
        self.s_stored = [sem(f"stored{b}") for b in range(2)]

    def load_weights(self):
        nc, w, E, D = self.nc, self.w, self.E, self.nodes.dim
        s_in = nc.alloc_semaphore("e_in")
        with nc.Block() as block:
            @block.sync
            def _(sp):
                sp.dma_start(self.w1[:, :, :, :], w["W1"].rearrange("e (k p) h -> p (e k) h", p=P)).then_inc(s_in, 16)
                sp.dma_start(self.w2[:, :, :, :], w["W2"].rearrange("e (m p) d -> p (e m) d", p=P)).then_inc(s_in, 16)
                for e in range(E):
                    sp.dma_start(self.b1[:, e, :], w["b1"][e, :].rearrange("(m p) -> p m", p=P),
                                 allow_slow_non_contiguous=True).then_inc(s_in, 16)
                sp.dma_start(self.b2[:, :, :].rearrange("p e d -> p (e d)"),
                             on_all(w["b2"].rearrange("e d -> (e d)"), E * D)).then_inc(s_in, 16)
                sp.wait_ge(s_in, 16 * (E + 3))

    def unit(self, eng, chunk, unit, size):
        nc, E, KT, MT, CH, D = self.nc, self.E, self.KT, self.MT, self.CH, self.nodes.dim
        kind, e, k = unit
        first = isinstance(chunk, int) and chunk == 0
        per_h, per_o = E * MT, E * CH
        if kind == "h":
            n, bank, cols = chunk * per_h + e * MT + k, self.p_h[k % 2], size * P
            if eng is nc.tensor:
                if not (first and e == 0 and k < 2):
                    eng.wait_ge(self.s_gelu, n - 1)
                for kt in range(KT):
                    mm = eng.matmul(bank[:, 0:cols], self.w1[:, e, kt, k * P:(k + 1) * P],
                                    self.y_t[:, kt, bass.ds(chunk * (CH * P), cols)], start=(kt == 0), stop=(kt == KT - 1))
                mm.then_inc(self.s_h, 1)
            elif eng is nc.scalar:
                if k == 0 and not (first and e < 2):
                    eng.wait_ge(self.s_o, chunk * per_o + (e - 1) * size)
                eng.wait_ge(self.s_h, n + 1)
                nc.scalar.activation(self.hid[:, e % 2, k, 0:cols], bank[:, 0:cols], ACT.Gelu,
                                     bias=self.b1[:, e, k:k + 1]).then_inc(self.s_gelu, 1)
            return
        n = chunk * per_o + e * size + k
        bank = self.p_o[(e * size + k) % 2]
        if eng is nc.tensor:
            eng.wait_ge(self.s_gelu, chunk * per_h + (e + 1) * MT)
            if not (first and e * size + k < 2):
                eng.wait_ge(self.s_kept, n - 1)
            for m in range(MT):
                mm = eng.matmul(bank[:, 0:D], self.hid[:, e % 2, m, k * P:(k + 1) * P], self.w2[:, e, m, :],
                                start=(m == 0), stop=(m == MT - 1))
            mm.then_inc(self.s_o, 1)
        elif eng is nc.vector:
            if k == 0 and not (first and e < 2):
                eng.wait_ge(self.s_stored[e % 2], (chunk * (E // 2) + e // 2) * 16)
            eng.wait_ge(self.s_o, n + 1)
            nc.vector.tensor_tensor(self.stash[:, e % 2, k, :], bank[:, 0:D], self.b2[:, e, :], ALU.add).then_inc(self.s_kept, 1)
        elif eng is nc.sync and k == size - 1:
            eng.wait_ge(self.s_kept, n + 1)
            eng.nop(nofuse=True)
            eng.dma_start(self.out[e, bass.ds(chunk * (CH * P), size * P), :].rearrange("(i p) d -> p i d", p=P),
                          self.stash[:, e % 2, 0:size, :]).then_inc(self.s_stored[e % 2], 16)

    def slot(self, eng, c, slot):
        if slot < 0:
            if isinstance(c, int) and c == 0:
                return
            c, slot = c - 1, slot + 2 * self.groups_per_pass
        slots = 2 * self.groups_per_pass
        work = sum(1 if u[0] == "h" else 2 for _, u in self.units)
        done = 0
        for q, u in self.units:
            if done * slots // work == slot and not (isinstance(c, int) and 2 * c + q < 0):
                self.unit(eng, c * 2 + q, u, self.CH)
            done += 1 if u[0] == "h" else 2

    def lag(self, eng):
        return {self.nc.vector: 1, self.nc.sync: 2}.get(eng, 0)

    def slice(self, eng, c, k, part):
        self.slot(eng, c, 2 * k + part - self.lag(eng))

    def rest(self, eng):
        for late in range(self.lag(eng), 0, -1):
            self.slot(eng, self.passes, -late)
        for j in range(self.CH):
            self.unit(eng, self.chunks - 1, ("p", self.E - 1, j), self.CH)
        if self.tail:
            for e in range(self.E):
                for m in range(self.MT):
                    self.unit(eng, self.chunks, ("h", e, m), self.tail)
                self.unit(eng, self.chunks, ("p", e, 0), self.tail)
        if eng is self.nc.sync:
            for b in range(2):
                eng.wait_ge(self.s_stored[b], 16 * (self.chunks + (self.tail > 0)) * (self.E // 2))


def mix_experts(nc, nodes, expert_out, gate, out):
    E, _, D = expert_out.shape
    tiles = nodes.tiles
    full = nodes.count // P
    rest = nodes.count - full * P
    duos = -(-tiles // 2)
    size = lambda u: 1 if isinstance(u, int) and 2 * u == tiles - 1 else 2
    with ExitStack() as ctx:
        got = ctx.enter_context(nc.sbuf_tensor("m_got", [P, 2, 2, E, D], F32))
        sem = lambda n: nc.alloc_semaphore(f"m_{n}")
        s_step, s_done, s_out = sem("step"), sem("done"), sem("out")
        s_in = [sem(f"in{b}") for b in range(2)]
        block = ctx.enter_context(nc.Block())

        @block.sync
        def _(sp):
            def load(i, b, first):
                u = 2 * i + b
                if not first:
                    sp.wait_ge(s_done, u - 1)
                for k in range(size(u)):
                    sp.dma_start(got[:, b, k, :, :], expert_out[:, bass.ds((2 * u + k) * P, P), :].rearrange("e p d -> p e d"))\
                        .then_inc(s_in[b], 16)

            group_loop(sp, duos, load)

        @block.scalar
        def _(act):
            def store(i, b, first):
                u = 2 * i + b
                act.wait_ge(s_done, u + 1)
                for k in range(size(u)):
                    n = 2 * u + k
                    rows = rest if isinstance(n, int) and n == full else P
                    act.dma_start(out[bass.ds(n * P, rows), :], nodes.x[0:rows, bass.ds(n, 1), :].rearrange("p o d -> p (o d)"))\
                        .then_inc(s_out, 16)

            group_loop(act, duos, store)
            act.wait_ge(s_out, 16 * tiles)

        @block.vector
        def _(dve):
            own = Steps(dve, s_step)

            def mix(i, b, first):
                u = 2 * i + b
                dve.wait_ge(s_in[b], 32 * i + 16 * size(u))
                for e in range(E):
                    for k in range(size(u)):
                        n = 2 * u + k
                        x = nodes.x[:, bass.ds(n, 1), :].rearrange("p o d -> p (o d)")
                        last = nc.vector.scalar_tensor_tensor(x, got[:, b, k, e, :], gate[:, bass.ds(n, 1), e], x, ALU.mult, ALU.add)
                    if e < E - 1:
                        own.link(last)
                last.then_inc(s_done, 1)

            group_loop(dve, duos, mix, own, 2 * (E - 1))
GNN = ("Wk", "bk", "Wq", "bq", "Wv", "bv", "Wa", "ba", "rel_att", "rel_msg", "rel_pri", "skip")
MIX = ("Wqkv", "Wout", "bout")
FFN = ("W_gat", "att_src", "att_dst", "b_gat", "ln_gamma", "ln_beta", "W1", "b1", "W2", "b2", "edge_index")
NAMES = ["x", "src", "dst"] + [f"L0_gnn_{n}" for n in GNN] + [f"L0_mix_{n}" for n in MIX] + [f"L0_ffn_{n}" for n in FFN]


def stage_of(nc, stage, *given):
    with nc.cleanup_on_exit():
        stage(nc, *given)
    nc.all_engine_barrier()


def build(nc, args, out):
    x, src, dst = (args[n] for n in ("x", "src", "dst"))
    w = {n: args[f"L0_gnn_{n}"] for n in GNN} | {n: args[f"L0_mix_{n}"] for n in MIX}
    f = {n: args[f"L0_ffn_{n}"] for n in FFN}
    N, D = x.shape
    H = w["rel_pri"].shape[0]
    DK = D // H
    FH, FE = f["att_src"].shape
    step = 2 * GRP * P
    batches = [-(-n // step) * 2 * GRP for n in (dst.shape[0], f["edge_index"].shape[1])]
    dram = lambda n, s, d=F32: nc.dram_tensor(n, s, d, kind="Internal").ap()
    tiles = -(-N // P)
    src_t, dst_t = dram("kv_table", [tiles * P, 2 * D]), dram("q_table", [tiles * P, D])
    fsrc_t, fdst_t = dram("gat_src_table", [tiles * P, FH * FE + FH]), dram("gat_dst_table", [tiles * P, FH])
    with ExitStack() as ctx:
        consts = Consts(nc, ctx)
        nodes = Nodes(nc, ctx, N, D)
        stage_of(nc, load_nodes, nodes, x)
        stage_of(nc, layer_norm_stats, "ln1", nodes)

        def lists_of(name, T, s, d, keep, buffers, often_sorted):
            pairs, rows = dram(f"{name}_pairs", [T * P, 2], I32), dram(f"{name}_dst_rows", [T, P])
            counts = keep.enter_context(nc.sbuf_tensor(f"{name}_counts", [P, HIS], F32))
            ends = keep.enter_context(nc.sbuf_tensor(f"{name}_ends", [P, HIS], F32))
            return EdgeSort(nc, buffers, f"{name}s", consts, s, d, T, N, pairs, rows, counts, ends, often_sorted)

        with ExitStack() as own:
            ffn_sort = lists_of("f", batches[1], f["edge_index"][0, :], f["edge_index"][1, :], ctx, own, False)
            stage_of(nc, lambda nc: ffn_sort.count())
            stage_of(nc, project, consts, nodes, w, src_t, dst_t, ffn_sort)

        def edge_sums(stage, name, sort, heads, width, s_table, d_table, node_values, make_beside=None):
            T, counts, ends, pairs = sort.batches, sort.counts, sort.ends, sort.pairs_out
            partial = dram(f"{name}_partial", [T * P + 1, heads * (width + 2)])
            last = stage.enter_context(nc.sbuf_tensor(f"{name}_last", [P, -(-T // P)], F32))
            with ExitStack() as own:
                lists = EdgeLists(nc, own, name, T, heads, last, node_values is None)
                stage_of(nc, read_sorted, f"{name}r", consts, lists, pairs, N)
                spread = None
                if node_values is not None:
                    spread = own.enter_context(nc.sbuf_tensor(f"{name}_spread", [P, T, heads], F32))
                    stage_of(nc, spread_over_runs, f"{name}p", consts, nodes, lists, counts, ends, node_values, d_table, spread)
                beside = make_beside(own, T // GRP) if make_beside else None
                stage_of(nc, edge_pass, f"{name}e", consts, lists, s_table, d_table, width, partial, spread, beside)
            cols = heads * (width + 2)
            b, e = (stage.enter_context(nc.sbuf_tensor(f"{name}_{n}", [P, tiles, cols], F32)) for n in ("before", "at_end"))
            stage_of(nc, gather_sums, f"{name}c", consts, nodes, lists, partial, counts, ends, heads, width, b, e)
            return b, e

        with ExitStack() as stage:
            with ExitStack() as own:
                gnn_sort = lists_of("a", batches[0], src, dst, stage, own, True)
                stage_of(nc, lambda nc: gnn_sort.count())
                stage_of(nc, lambda nc: gnn_sort.place())
            b, e = edge_sums(stage, "a", gnn_sort, H, DK, src_t, dst_t, None)
            stage_of(nc, first_residual, consts, nodes, b, e, H, DK)
        stage_of(nc, layer_norm_stats, "ln2", nodes)
        with ExitStack() as stage:
            y_t = stage.enter_context(nc.sbuf_tensor("y_t", [P, D // P, tiles * P], F32))
            feats = stage.enter_context(nc.sbuf_tensor("feats", [P, tiles, FH * FE + 2 * FH], F32))
            gate = stage.enter_context(nc.sbuf_tensor("gate", [P, tiles, FE], F32))
            stage_of(nc, gat_inputs, consts, nodes, f, y_t, feats, fsrc_t, fdst_t)
            expert_out = dram("expert_out", [FE, tiles * P, D])

            def all_experts(own, groups):
                work = Experts(nc, own, nodes, f, y_t, expert_out, groups)
                stage_of(nc, lambda nc: work.load_weights())
                return work

            with ExitStack() as inner:
                b, e = edge_sums(inner, "f", ffn_sort, FH, FE, fsrc_t, fdst_t,
                                 feats[:, :, FH * FE + FH:FH * FE + 2 * FH], all_experts)
                stage_of(nc, gates, nodes, f, feats, b, e, gate)
            stage_of(nc, mix_experts, nodes, expert_out, gate, out)


def kernel(**inputs):
    import numpy as _np
    import concourse.bacc as _bacc
    from concourse import mybir as _mybir
    from concourse.bass_utils import run_bass_kernel_spmd as _run

    nc = _bacc.Bacc("TRN2", target_bir_lowering=False, num_devices=1)
    arrays, args = {}, {}
    for name in NAMES:
        a = _np.ascontiguousarray(inputs[name])
        if a.ndim == 0:
            a = a.reshape(1)
        arrays[f"in_{name}_dram"] = a
        args[name] = nc.dram_tensor(f"in_{name}_dram", a.shape, _mybir.dt.from_np(a.dtype), kind="ExternalInput").ap()
    out = nc.dram_tensor("out_0_dram", inputs["x"].shape, _mybir.dt.float32, kind="ExternalOutput").ap()
    build(nc, args, out)
    r = _run(nc, [arrays], core_ids=[0])
    return r.results[0]["out_0_dram"]
```
